# Optimizing a Trainium2 kernel written in Bass

```python
import numpy as np
import jax
import jax.numpy as jnp

def _softmax(x, axis=-1):
    return jax.nn.softmax(x, axis=axis)

def _gelu(x):
    return jax.nn.gelu(x, approximate=True)

def _silu(x):
    return jax.nn.silu(x)

def _sigmoid(x):
    return jax.nn.sigmoid(x)

def _layernorm(x, axis=-1, eps=1e-05):
    m = jnp.mean(x, axis=axis, keepdims=True)
    v = jnp.var(x, axis=axis, keepdims=True)
    return (x - m) / jnp.sqrt(v + eps)

def _scatter_add(tgt, idx, src, axis=0):
    return tgt.at[idx].add(src)

def _segment_sum(src, seg, n):
    return jax.ops.segment_sum(src, seg, n)
kernel_name = 'mk_prb_d4_jaxref_r8_d54818'

def setup_inputs(seed: int=0):
    np.random.seed(seed)
    _w = jnp.asarray

    def _L0_attn_setup():
        import jax, jax.numpy as jnp
        import numpy as np
        import math
        B, T, D = (2, 512, 128)
        H = 16
        HEAD_DIM = D // H
        CHUNK = 64

        def chunked_attention(q, k, v, chunk_size, scale):
            Bq, Hq, Tq, hd = q.shape
            S = k.shape[2]
            nc = Tq // chunk_size
            q_chunks = q.reshape(Bq, Hq, nc, chunk_size, hd).transpose(2, 0, 1, 3, 4)
            starts = jnp.arange(nc, dtype=jnp.int32) * chunk_size
            k_pos = jnp.arange(S)

            def body(carry, xs):
                qc, start = xs
                scores = jnp.einsum('bhqd,bhkd->bhqk', qc, k) * scale
                q_pos = start + jnp.arange(chunk_size)
                causal_mask = k_pos[None, :] > q_pos[:, None]
                scores = jnp.where(causal_mask[None, None], -jnp.inf, scores)
                m = jnp.max(scores, axis=-1, keepdims=True)
                m = jnp.where(jnp.isinf(m), jnp.zeros_like(m), m)
                p = jax.nn.softmax(scores - m, axis=-1)
                oc = jnp.einsum('bhqk,bhkd->bhqd', p, v)
                return (carry, oc)
            _, outs = jax.lax.scan(body, None, (q_chunks, starts))
            return outs.transpose(1, 2, 0, 3, 4).reshape(Bq, Hq, Tq, hd)
        key = jax.random.key(seed)
        ks = jax.random.split(key, 9)
        s = 1.0 / math.sqrt(D)
        return {'x': jax.random.normal(ks[0], (B, T, D), dtype=jnp.float32), 'Wq': jax.random.normal(ks[1], (D, D), dtype=jnp.float32) * s, 'bq': jax.random.normal(ks[2], (D,), dtype=jnp.float32) * 0.01, 'Wk': jax.random.normal(ks[3], (D, D), dtype=jnp.float32) * s, 'bk': jax.random.normal(ks[4], (D,), dtype=jnp.float32) * 0.01, 'Wv': jax.random.normal(ks[5], (D, D), dtype=jnp.float32) * s, 'bv': jax.random.normal(ks[6], (D,), dtype=jnp.float32) * 0.01, 'Wo': jax.random.normal(ks[7], (D, D), dtype=jnp.float32) * s, 'bo': jax.random.normal(ks[8], (D,), dtype=jnp.float32) * 0.01}
    _L0_attn_in = _L0_attn_setup()

    def _L0_ffn_setup():
        import jax, jax.numpy as jnp
        import numpy as np
        B, L, D = (4, 64, 128)
        E, TOP_K = (16, 4)
        F = 4 * D
        key = jax.random.key(seed)
        ks = jax.random.split(key, 6)
        scale = 0.02
        return {'x': jax.random.normal(ks[0], (B, L, D), jnp.float32), 'keys': jax.random.normal(ks[1], (E, D), jnp.float32), 'w1': jax.random.normal(ks[2], (E, F, D), jnp.float32) * scale, 'b1': jnp.zeros((E, F), jnp.float32), 'w2': jax.random.normal(ks[3], (E, D, F), jnp.float32) * scale, 'b2': jnp.zeros((E, D), jnp.float32), 'rw': jax.random.normal(ks[4], (E, D), jnp.float32) * scale, 'rb': jnp.zeros((E,), jnp.float32)}
    _L0_ffn_in = _L0_ffn_setup()

    def _L1_attn_setup():
        import jax, jax.numpy as jnp
        import numpy as np
        B, T, D = (4, 256, 128)
        H, DK = (8, 64)
        EPS = 1e-06

        def _xavier(key, shape):
            fan_in, fan_out = (shape[1], shape[0])
            lim = float(np.sqrt(6.0 / (fan_in + fan_out)))
            return jax.random.uniform(key, shape, jnp.float32, -lim, lim)

        def _phi(u):
            return jax.nn.elu(u) + 1.0
        key = jax.random.key(seed)
        ks = jax.random.split(key, 7)
        x = jax.random.normal(ks[0], (B, T, D), jnp.float32)
        W_Q = _xavier(ks[1], (H * DK, D))
        W_K = _xavier(ks[2], (H * DK, D))
        W_V = _xavier(ks[3], (H * DK, D))
        W_g_w = _xavier(ks[4], (H * DK, D))
        W_g_b = jax.random.normal(ks[5], (H * DK,), jnp.float32) * 0.02
        W_O = _xavier(ks[6], (D, H * DK))
        decay_log = jnp.zeros((H,), jnp.float32)
        return {'x': x, 'W_Q': W_Q, 'W_K': W_K, 'W_V': W_V, 'W_g_w': W_g_w, 'W_g_b': W_g_b, 'W_O': W_O, 'decay_log': decay_log}
    _L1_attn_in = _L1_attn_setup()

    def _L1_ffn_setup():
        import jax, jax.numpy as jnp
        import numpy as np
        B, S, DIM, FFN, E = (4, 256, 128, 512, 8)
        key = jax.random.key(seed)
        k0, k1, k2, k3 = jax.random.split(key, 4)
        scale = 0.02
        return {'hidden_states': jax.random.normal(k0, (B, S, DIM), jnp.float32), 'router_w': jax.random.normal(k1, (DIM, E), jnp.float32) * scale, 'router_b': jnp.zeros((E,), jnp.float32), 'w1': jax.random.normal(k2, (E, DIM, 2 * FFN), jnp.float32) * scale, 'w2': jax.random.normal(k3, (E, FFN, DIM), jnp.float32) * scale}
    _L1_ffn_in = _L1_ffn_setup()

    def _L2_attn_setup():
        import jax, jax.numpy as jnp
        import numpy as np
        HEAD_NUM = 16
        NEG_BIG = 1000000.0
        key = jax.random.key(seed)
        ks = jax.random.split(key, 5)
        E = 128
        B, S = (1, 512)
        x = jax.random.normal(ks[0], (B, S, E), dtype=jnp.float32)
        W1 = jax.random.normal(ks[1], (E, 3 * E), dtype=jnp.float32) * (1.0 / np.sqrt(E))
        b1 = jax.random.normal(ks[2], (3 * E,), dtype=jnp.float32) * 0.02
        Wp = jax.random.normal(ks[3], (E, E), dtype=jnp.float32) * (1.0 / np.sqrt(E))
        bp = jax.random.normal(ks[4], (E,), dtype=jnp.float32) * 0.02
        return {'x': x, 'W1': W1, 'b1': b1, 'Wp': Wp, 'bp': bp}
    _L2_attn_in = _L2_attn_setup()

    def _L2_ffn_setup():
        import jax, jax.numpy as jnp
        import numpy as np
        E = 8
        D = 128
        DO = 128
        R = 64
        H = 32
        B, T = (8, 256)
        key = jax.random.key(seed)
        ks = jax.random.split(key, 12)
        s = lambda k, shape, fan: jax.random.normal(k, shape, jnp.float32) / np.sqrt(fan)
        return {'x': jax.random.normal(ks[0], (B, T, D), jnp.float32), 'W_base': s(ks[1], (D, DO), D), 'b_base': jnp.zeros((DO,), jnp.float32), 'Wd1': s(ks[2], (E, D, H), D), 'bd1': jnp.zeros((E, H), jnp.float32), 'Wd2': s(ks[3], (E, H, D), H), 'bd2': jnp.zeros((E, D), jnp.float32), 'Wa_down': s(ks[4], (E, D, R), D), 'ba_down': jnp.zeros((E, R), jnp.float32), 'Wa_up': s(ks[5], (E, R, DO), R), 'ba_up': jnp.zeros((E, DO), jnp.float32)}
    _L2_ffn_in = _L2_ffn_setup()

    def _L3_attn_setup():
        import jax, jax.numpy as jnp
        import numpy as np
        EMB = 128
        HEADS = 16
        HEAD_DIM = EMB // HEADS
        MAX_LEN = 125
        key = jax.random.key(seed)
        ks = jax.random.split(key, 11)
        s = 0.02
        x = jax.random.normal(ks[0], (4, 128, EMB), dtype=jnp.float32)
        Wq = jax.random.normal(ks[1], (EMB, EMB), dtype=jnp.float32) * s
        bq = jnp.zeros((EMB,), dtype=jnp.float32)
        Wk = jax.random.normal(ks[2], (EMB, EMB), dtype=jnp.float32) * s
        bk = jnp.zeros((EMB,), dtype=jnp.float32)
        Wv = jax.random.normal(ks[3], (EMB, EMB), dtype=jnp.float32) * s
        bv = jnp.zeros((EMB,), dtype=jnp.float32)
        Wp = jax.random.normal(ks[4], (EMB, EMB), dtype=jnp.float32) * s
        bp = jnp.zeros((EMB,), dtype=jnp.float32)
        bias_table = jax.random.normal(ks[5], (2 * MAX_LEN - 1, HEADS), dtype=jnp.float32) * 0.02
        temperature = jnp.ones((1,), dtype=jnp.float32)
        return {'x': x, 'Wq': Wq, 'bq': bq, 'Wk': Wk, 'bk': bk, 'Wv': Wv, 'bv': bv, 'Wp': Wp, 'bp': bp, 'bias_table': bias_table, 'temperature': temperature}
    _L3_attn_in = _L3_attn_setup()

    def _L3_ffn_setup():
        import jax, jax.numpy as jnp
        import numpy as np
        TOP_K = 2
        key = jax.random.key(seed)
        ks = jax.random.split(key, 6)
        B, S, D, E = (8, 512, 128, 8)
        s = 1.0 / np.sqrt(D)
        return {'x': jax.random.normal(ks[0], (B, S, D), dtype=jnp.float32), 'Wr': jax.random.normal(ks[1], (D, E), dtype=jnp.float32) * s, 'br': jnp.zeros((E,), dtype=jnp.float32), 'W1': jax.random.normal(ks[2], (E, D, D), dtype=jnp.float32) * s, 'b1': jnp.zeros((E, D), dtype=jnp.float32), 'W2': jax.random.normal(ks[3], (E, D, D), dtype=jnp.float32) * s, 'b2': jnp.zeros((E, D), dtype=jnp.float32)}
    _L3_ffn_in = _L3_ffn_setup()
    _d = {'L0_attn_x': _L0_attn_in['x'], 'L0_attn_Wq': _L0_attn_in['Wq'], 'L0_attn_bq': _L0_attn_in['bq'], 'L0_attn_Wk': _L0_attn_in['Wk'], 'L0_attn_bk': _L0_attn_in['bk'], 'L0_attn_Wv': _L0_attn_in['Wv'], 'L0_attn_bv': _L0_attn_in['bv'], 'L0_attn_Wo': _L0_attn_in['Wo'], 'L0_attn_bo': _L0_attn_in['bo'], 'L0_ffn_keys': _L0_ffn_in['keys'], 'L0_ffn_w1': _L0_ffn_in['w1'], 'L0_ffn_b1': _L0_ffn_in['b1'], 'L0_ffn_w2': _L0_ffn_in['w2'], 'L0_ffn_b2': _L0_ffn_in['b2'], 'L0_ffn_rw': _L0_ffn_in['rw'], 'L0_ffn_rb': _L0_ffn_in['rb'], 'L1_attn_W_Q': _L1_attn_in['W_Q'], 'L1_attn_W_K': _L1_attn_in['W_K'], 'L1_attn_W_V': _L1_attn_in['W_V'], 'L1_attn_W_g_w': _L1_attn_in['W_g_w'], 'L1_attn_W_g_b': _L1_attn_in['W_g_b'], 'L1_attn_W_O': _L1_attn_in['W_O'], 'L1_attn_decay_log': _L1_attn_in['decay_log'], 'L1_ffn_router_w': _L1_ffn_in['router_w'], 'L1_ffn_router_b': _L1_ffn_in['router_b'], 'L1_ffn_w1': _L1_ffn_in['w1'], 'L1_ffn_w2': _L1_ffn_in['w2'], 'L2_attn_W1': _L2_attn_in['W1'], 'L2_attn_b1': _L2_attn_in['b1'], 'L2_attn_Wp': _L2_attn_in['Wp'], 'L2_attn_bp': _L2_attn_in['bp'], 'L2_ffn_W_base': _L2_ffn_in['W_base'], 'L2_ffn_b_base': _L2_ffn_in['b_base'], 'L2_ffn_Wd1': _L2_ffn_in['Wd1'], 'L2_ffn_bd1': _L2_ffn_in['bd1'], 'L2_ffn_Wd2': _L2_ffn_in['Wd2'], 'L2_ffn_bd2': _L2_ffn_in['bd2'], 'L2_ffn_Wa_down': _L2_ffn_in['Wa_down'], 'L2_ffn_ba_down': _L2_ffn_in['ba_down'], 'L2_ffn_Wa_up': _L2_ffn_in['Wa_up'], 'L2_ffn_ba_up': _L2_ffn_in['ba_up'], 'L3_attn_Wq': _L3_attn_in['Wq'], 'L3_attn_bq': _L3_attn_in['bq'], 'L3_attn_Wk': _L3_attn_in['Wk'], 'L3_attn_bk': _L3_attn_in['bk'], 'L3_attn_Wv': _L3_attn_in['Wv'], 'L3_attn_bv': _L3_attn_in['bv'], 'L3_attn_Wp': _L3_attn_in['Wp'], 'L3_attn_bp': _L3_attn_in['bp'], 'L3_attn_bias_table': _L3_attn_in['bias_table'], 'L3_attn_temperature': _L3_attn_in['temperature'], 'L3_ffn_Wr': _L3_ffn_in['Wr'], 'L3_ffn_br': _L3_ffn_in['br'], 'L3_ffn_W1': _L3_ffn_in['W1'], 'L3_ffn_b1': _L3_ffn_in['b1'], 'L3_ffn_W2': _L3_ffn_in['W2'], 'L3_ffn_b2': _L3_ffn_in['b2']}
    _x0 = _d['L0_attn_x']
    _d['L0_attn_x'] = jax.random.normal(jax.random.fold_in(jax.random.key(seed), 1), (8, 512, 128), dtype=_x0.dtype)
    del _x0
    return _d

def reference(L0_attn_x, L0_attn_Wq, L0_attn_bq, L0_attn_Wk, L0_attn_bk, L0_attn_Wv, L0_attn_bv, L0_attn_Wo, L0_attn_bo, L0_ffn_keys, L0_ffn_w1, L0_ffn_b1, L0_ffn_w2, L0_ffn_b2, L0_ffn_rw, L0_ffn_rb, L1_attn_W_Q, L1_attn_W_K, L1_attn_W_V, L1_attn_W_g_w, L1_attn_W_g_b, L1_attn_W_O, L1_attn_decay_log, L1_ffn_router_w, L1_ffn_router_b, L1_ffn_w1, L1_ffn_w2, L2_attn_W1, L2_attn_b1, L2_attn_Wp, L2_attn_bp, L2_ffn_W_base, L2_ffn_b_base, L2_ffn_Wd1, L2_ffn_bd1, L2_ffn_Wd2, L2_ffn_bd2, L2_ffn_Wa_down, L2_ffn_ba_down, L2_ffn_Wa_up, L2_ffn_ba_up, L3_attn_Wq, L3_attn_bq, L3_attn_Wk, L3_attn_bk, L3_attn_Wv, L3_attn_bv, L3_attn_Wp, L3_attn_bp, L3_attn_bias_table, L3_attn_temperature, L3_ffn_Wr, L3_ffn_br, L3_ffn_W1, L3_ffn_b1, L3_ffn_W2, L3_ffn_b2):

    def _L0_attn_ref(x, Wq, bq, Wk, bk, Wv, bv, Wo, bo):
        import jax, jax.numpy as jnp
        import numpy as np
        import math
        B, T, D = (2, 512, 128)
        H = 16
        HEAD_DIM = D // H
        CHUNK = 64

        def chunked_attention(q, k, v, chunk_size, scale):
            Bq, Hq, Tq, hd = q.shape
            S = k.shape[2]
            nc = Tq // chunk_size
            q_chunks = q.reshape(Bq, Hq, nc, chunk_size, hd).transpose(2, 0, 1, 3, 4)
            starts = jnp.arange(nc, dtype=jnp.int32) * chunk_size
            k_pos = jnp.arange(S)

            def body(carry, xs):
                qc, start = xs
                scores = jnp.einsum('bhqd,bhkd->bhqk', qc, k) * scale
                q_pos = start + jnp.arange(chunk_size)
                causal_mask = k_pos[None, :] > q_pos[:, None]
                scores = jnp.where(causal_mask[None, None], -jnp.inf, scores)
                m = jnp.max(scores, axis=-1, keepdims=True)
                m = jnp.where(jnp.isinf(m), jnp.zeros_like(m), m)
                p = jax.nn.softmax(scores - m, axis=-1)
                oc = jnp.einsum('bhqk,bhkd->bhqd', p, v)
                return (carry, oc)
            _, outs = jax.lax.scan(body, None, (q_chunks, starts))
            return outs.transpose(1, 2, 0, 3, 4).reshape(Bq, Hq, Tq, hd)
        Bx, Tx, Dx = x.shape
        scale = 1.0 / math.sqrt(HEAD_DIM)

        def proj(W, b):
            y = x @ W.T + b
            return y.reshape(Bx, Tx, H, HEAD_DIM).transpose(0, 2, 1, 3)
        q = proj(Wq, bq)
        k = proj(Wk, bk)
        v = proj(Wv, bv)
        out = chunked_attention(q, k, v, CHUNK, scale)
        out = out.transpose(0, 2, 1, 3).reshape(Bx, Tx, Dx)
        return out @ Wo.T + bo

    def _L0_ffn_ref(x, keys, w1, b1, w2, b2, rw, rb):
        import jax, jax.numpy as jnp
        import numpy as np
        B, L, D = (4, 64, 128)
        E, TOP_K = (16, 4)
        F = 4 * D
        diff = x[:, :, None, :] - keys
        dist2 = jnp.sum(diff * diff, axis=-1)
        logits = -dist2 + jnp.einsum('bld,ed->ble', x, rw) + rb
        topv, topi = jax.lax.top_k(logits, TOP_K)
        w = jax.nn.softmax(topv, axis=-1)
        hidden = jax.nn.gelu(jnp.einsum('bld,efd->blef', x, w1) + b1, approximate=False)
        exp_out = jnp.einsum('blef,edf->bled', hidden, w2) + b2
        sel = jnp.take_along_axis(exp_out, topi[..., None], axis=2)
        fused = jnp.sum(w[..., None] * sel, axis=2)
        return fused

    def _L1_attn_ref(x, W_Q, W_K, W_V, W_g_w, W_g_b, W_O, decay_log):
        import jax, jax.numpy as jnp
        import numpy as np
        B, T, D = (4, 256, 128)
        H, DK = (8, 64)
        EPS = 1e-06

        def _xavier(key, shape):
            fan_in, fan_out = (shape[1], shape[0])
            lim = float(np.sqrt(6.0 / (fan_in + fan_out)))
            return jax.random.uniform(key, shape, jnp.float32, -lim, lim)

        def _phi(u):
            return jax.nn.elu(u) + 1.0
        b, t, d = x.shape
        q = _phi((x @ W_Q.T).reshape(b, t, H, DK))
        k = _phi((x @ W_K.T).reshape(b, t, H, DK))
        v = (x @ W_V.T).reshape(b, t, H, DK)
        gamma = jax.nn.sigmoid(decay_log)
        g4 = gamma[None, :, None, None]
        g3 = gamma[None, :, None]
        qT = jnp.moveaxis(q, 1, 0)
        kT = jnp.moveaxis(k, 1, 0)
        vT = jnp.moveaxis(v, 1, 0)
        S0 = jnp.zeros((b, H, DK, DK), x.dtype)
        z0 = jnp.zeros((b, H, DK), x.dtype)

        def step(carry, inp):
            S, z = carry
            qt, kt, vt = inp
            S = g4 * S + jnp.einsum('bhi,bhj->bhij', kt, vt)
            z = g3 * z + kt
            num = jnp.einsum('bhij,bhi->bhj', S, qt)
            den = jnp.sum(z * qt, axis=-1, keepdims=True) + EPS
            return ((S, z), num / den)
        _, ys = jax.lax.scan(step, (S0, z0), (qT, kT, vT))
        outputs = jnp.moveaxis(ys, 0, 1)
        gate = jax.nn.sigmoid(x @ W_g_w.T + W_g_b).reshape(b, t, H, DK)
        y = (outputs * gate).reshape(b, t, H * DK)
        return y @ W_O.T

    def _L1_ffn_ref(hidden_states, router_w, router_b, w1, w2):
        import jax, jax.numpy as jnp
        import numpy as np
        B, S, DIM, FFN, E = (4, 256, 128, 512, 8)
        b, s, d = hidden_states.shape
        x = hidden_states.reshape(-1, d)
        logits = x @ router_w + router_b
        route = jax.nn.softmax(logits, axis=1)
        max_prob = jnp.max(route, axis=1, keepdims=True)
        max_ind = jnp.argmax(route, axis=1)
        out = jnp.zeros_like(x)
        num_experts = w1.shape[0]
        for e in range(num_experts):
            h = x @ w1[e]
            a, g = jnp.split(h, 2, axis=1)
            y = jax.nn.silu(a) * g @ w2[e]
            out = jnp.where((max_ind == e)[:, None], y, out)
        out = out * max_prob
        return out.reshape(b, s, d)

    def _L2_attn_ref(x, W1, b1, Wp, bp):
        import jax, jax.numpy as jnp
        import numpy as np
        HEAD_NUM = 16
        NEG_BIG = 1000000.0
        B, S, E = x.shape
        H = HEAD_NUM
        d = E // H
        dk = jnp.asarray(d, x.dtype) ** 0.5
        h = x @ W1 + b1
        h = jnp.swapaxes(h.reshape(B, S, H, 3 * d), 1, 2)
        q, k, v = (h[..., :d], h[..., d:2 * d], h[..., 2 * d:])
        w = jnp.einsum('bhqd,bhkd->bhqk', q, k) / dk
        mask = jnp.tril(jnp.ones((S, S), dtype=x.dtype))
        w = jax.nn.softmax(w * mask - (1.0 - mask) * NEG_BIG, axis=-1)
        a = jnp.einsum('bhqk,bhkd->bhqd', w, v)
        a = jnp.swapaxes(a, 1, 2).reshape(B, S, E)
        return a @ Wp + bp

    def _L2_ffn_ref(x, W_base, b_base, Wd1, bd1, Wd2, bd2, Wa_down, ba_down, Wa_up, ba_up):
        import jax, jax.numpy as jnp
        import numpy as np
        E = 8
        D = 128
        DO = 128
        R = 64
        H = 32
        B, T = (8, 256)
        base = jnp.einsum('btd,do->bto', x, W_base) + b_base
        h = jax.nn.relu(jnp.einsum('btd,edh->ebth', x, Wd1) + bd1[:, None, None, :])
        recon = jnp.einsum('ebth,ehd->ebtd', h, Wd2) + bd2[:, None, None, :]
        losses = jnp.mean((recon - x[None]) ** 2, axis=(2, 3))
        idx = jnp.argmin(losses, axis=0)
        a = jax.nn.relu(jnp.einsum('btd,bdr->btr', x, Wa_down[idx]) + ba_down[idx][:, None, :])
        adapter_out = jnp.einsum('btr,bro->bto', a, Wa_up[idx]) + ba_up[idx][:, None, :]
        return base + adapter_out

    def _L3_attn_ref(x, Wq, bq, Wk, bk, Wv, bv, Wp, bp, bias_table, temperature):
        import jax, jax.numpy as jnp
        import numpy as np
        EMB = 128
        HEADS = 16
        HEAD_DIM = EMB // HEADS
        MAX_LEN = 125
        B, N, C = x.shape
        H, D = (HEADS, C // HEADS)

        def split_heads(t):
            return t.reshape(B, N, H, D).transpose(0, 2, 1, 3)
        q = split_heads(x @ Wq + bq)
        k = split_heads(x @ Wk + bk)
        v = split_heads(x @ Wv + bv)
        energy = jnp.einsum('bhqd,bhkd->bhqk', q, k)
        pos = jnp.arange(N)
        rel = pos[:, None] - pos[None, :] + (N - 1)
        rel = jnp.clip(rel, 0, bias_table.shape[0] - 1)
        bias = bias_table[rel].transpose(2, 0, 1)
        energy = energy + bias[None]
        scaling = jnp.sqrt(jnp.float32(C))
        temp = jnp.clip(temperature[0], 0.1, 10.0)
        att = jax.nn.softmax(energy / (scaling * temp), axis=-1)
        out = jnp.einsum('bhqk,bhkd->bhqd', att, v)
        out = out.transpose(0, 2, 1, 3).reshape(B, N, C)
        return out @ Wp + bp

    def _L3_ffn_ref(x, Wr, br, W1, b1, W2, b2):
        import jax, jax.numpy as jnp
        import numpy as np
        TOP_K = 2
        k = TOP_K
        scores0 = x[:, 0, :] @ Wr + br
        _, idx = jax.lax.top_k(scores0, k)
        W1g, b1g = (W1[idx], b1[idx])
        W2g, b2g = (W2[idx], b2[idx])
        h = jnp.einsum('bsd,bkde->bkse', x, W1g) + b1g[:, :, None, :]
        h = jax.nn.gelu(h, approximate=False)
        o = jnp.einsum('bkse,bkef->bksf', h, W2g) + b2g[:, :, None, :]
        return jnp.sum(o, axis=1) / k
    x = L0_attn_x
    xn = _layernorm(x, axis=-1)
    x = x + _L0_attn_ref(xn, L0_attn_Wq, L0_attn_bq, L0_attn_Wk, L0_attn_bk, L0_attn_Wv, L0_attn_bv, L0_attn_Wo, L0_attn_bo) + _L0_ffn_ref(xn, L0_ffn_keys, L0_ffn_w1, L0_ffn_b1, L0_ffn_w2, L0_ffn_b2, L0_ffn_rw, L0_ffn_rb)
    xn = _layernorm(x, axis=-1)
    x = x + _L1_attn_ref(xn, L1_attn_W_Q, L1_attn_W_K, L1_attn_W_V, L1_attn_W_g_w, L1_attn_W_g_b, L1_attn_W_O, L1_attn_decay_log) + _L1_ffn_ref(xn, L1_ffn_router_w, L1_ffn_router_b, L1_ffn_w1, L1_ffn_w2)
    xn = _layernorm(x, axis=-1)
    x = x + _L2_attn_ref(xn, L2_attn_W1, L2_attn_b1, L2_attn_Wp, L2_attn_bp) + _L2_ffn_ref(xn, L2_ffn_W_base, L2_ffn_b_base, L2_ffn_Wd1, L2_ffn_bd1, L2_ffn_Wd2, L2_ffn_bd2, L2_ffn_Wa_down, L2_ffn_ba_down, L2_ffn_Wa_up, L2_ffn_ba_up)
    xn = _layernorm(x, axis=-1)
    x = x + _L3_attn_ref(xn, L3_attn_Wq, L3_attn_bq, L3_attn_Wk, L3_attn_bk, L3_attn_Wv, L3_attn_bv, L3_attn_Wp, L3_attn_bp, L3_attn_bias_table, L3_attn_temperature) + _L3_ffn_ref(xn, L3_ffn_Wr, L3_ffn_br, L3_ffn_W1, L3_ffn_b1, L3_ffn_W2, L3_ffn_b2)
    return x

_drawn_inputs = setup_inputs


def setup_inputs(seed=0):
    import zlib

    import numpy as np

    out = dict(_drawn_inputs(seed))
    spreads = {'L0_ffn_b1': (0.0, 0.327),
     'L0_ffn_b2': (0.0, 0.1),
     'L0_ffn_rb': (0.0, 0.8),
     'L1_attn_decay_log': (0.0, 2.0),
     'L1_ffn_router_b': (0.0, 0.8),
     'L2_ffn_b_base': (0.0, 0.398),
     'L2_ffn_bd1': (0.0, 0.1),
     'L2_ffn_bd2': (0.0, 0.1),
     'L2_ffn_ba_down': (0.0, 0.593),
     'L2_ffn_ba_up': (0.0, 0.348),
     'L3_attn_bq': (0.0, 2.0),
     'L3_attn_bk': (0.0, 2.0),
     'L3_attn_bv': (0.0, 0.672),
     'L3_attn_bp': (0.0, 0.39),
     'L3_ffn_br': (0.0, 0.1),
     'L3_ffn_b1': (0.0, 0.852),
     'L3_ffn_b2': (0.0, 0.575)}
    factors = {'L0_attn_bq': 8.0,
     'L0_attn_bk': 200.0,
     'L0_attn_bv': 4.187,
     'L0_attn_bo': 4.11,
     'L0_ffn_rw': 8.0,
     'L1_attn_W_Q': 200.0,
     'L1_attn_W_K': 200.0,
     'L1_attn_W_g_b': 181.677,
     'L1_ffn_router_w': 8.0,
     'L1_ffn_w1': 8.0,
     'L1_ffn_w2': 8.0,
     'L2_attn_b1': 14.347,
     'L2_attn_bp': 12.47,
     'L3_attn_Wq': 8.0,
     'L3_attn_Wk': 8.0,
     'L3_attn_Wv': 7.145,
     'L3_attn_Wp': 3.578,
     'L3_attn_bias_table': 200.0,
     'L1_attn_W_g_w': 3.829}
    for name, (base, spread) in spreads.items():
        noise = np.random.default_rng([zlib.crc32(name.encode()), seed]).standard_normal(out[name].shape)
        drawn = base * np.exp(spread * noise) if base else spread * noise
        out[name] = jnp.asarray(drawn.astype(out[name].dtype))
    for name, factor in factors.items():
        out[name] = (out[name] * factor).astype(out[name].dtype)
    return out
```

```python
from contextlib import ExitStack

import numpy as np

import concourse.bass as bass
from concourse import mybir

ALU = mybir.AluOpType
ACT = mybir.ActivationFunctionType
AX = mybir.AxisListType
F32 = mybir.dt.float32
BF16 = mybir.dt.bfloat16
U32 = mybir.dt.uint32

P = 128
NBATCH, T, D = 8, 512, 128
NT = T // P
H, HD = 16, 8
HG = 4
NG = H // HG
VW = 32
NPART = 3
KROWS = NPART * NPART * HD
KAUG = KROWS + NPART
LN_EPS = 1e-05
E0, F0, TOP0 = 16, 512, 4
E1, F1 = 8, 512
H1, DK1, EPS1 = 8, 64, 1e-06
V1W = DK1 + 1
E2, R2, HID2 = 8, 64, 32
E3, TOP3 = 8, 2
TABLE3 = 249
HANKEL = 256
NHALF = 2


class Batch:

    def __init__(self, pair, half):
        self.pair, self.half = pair, half

    @property
    def index(self):
        return self.pair * NHALF + self.half

    @property
    def parity(self):
        return self.half


class Signal:

    def __init__(self, sem, per_batch, before=0):
        self.sem, self.per_batch, self.before = sem, per_batch, before

    def at(self, b, n):
        return b.pair * (NHALF * self.per_batch) + (b.half * self.per_batch + n + self.before)

    def before_batch(self, b, back=0):
        return b.pair * (NHALF * self.per_batch) + (
            b.half * self.per_batch + self.before - back * self.per_batch)


def causal_score_blocks():
    w = [T - P * k for k in range(NT)]
    first = [[(j, 0, 0)] for j in range(HG)]
    second = [[(j, 1, 0), (j, 3, w[1])] for j in range(HG)]
    third = [[(2 * i, 2, 0), (2 * i + 1, 2, w[2])] for i in range(HG // 2)]
    return [first, second, third]


def full_score_blocks():
    return [[[(j, k, 0)] for j in range(HG)] for k in range(NT)]


def causal_max_slots():
    out = [(0, [0, 1, 2, 3]), (1, [0, 1]), (1, [2, 3])]
    return out + [(q, [j]) for q in (2, 3) for j in range(HG)]


def full_max_slots():
    return [(q, [j]) for q in range(NT) for j in range(HG)]


def build(nc, a, out, layers=(0, 1, 2, 3)):
    stack = ExitStack()
    with stack:
        def sb(name, shape, dt=F32):
            return stack.enter_context(nc.sbuf_tensor(name, shape, dt))

        def sem(name):
            return stack.enter_context(nc.semaphore(name))

        bank = [stack.enter_context(nc.psum_tensor(f"bank{i}", [P, 512], F32)) for i in range(8)]

        x = sb("x", [P, NBATCH * NT, D])
        ident = sb("ident", [P, P])
        flip = sb("flip", [P, P])
        identb = sb("identb", [P, P], BF16)
        mask_q = sb("mask_q", [P, P], BF16)
        mask_k = sb("mask_k", [P, P], BF16)
        mask_f = sb("mask_f", [P, P])
        mask_qf = sb("mask_qf", [P, 2, P])
        iota16 = sb("iota16", [P, 16])
        ones = sb("ones", [P, P])
        mhalf = sb("mhalf", [P, NT])
        mean_var = sb("mean_var", [P, NT, 2])
        stats = sb("stats", [P, NT, 6])
        rstd = sb("rstd", [P, NT])
        xn = sb("xn", [P, NT, D])
        xnT = [sb(f"xnT{i}", [P, T]) for i in range(2)]
        acc = sb("acc", [P, NT, D])

        ARENA = 44544
        arena = sb("arena", [P, ARENA])
        used = [0]

        def carve(shape, dt=F32):
            per = 4 if dt in (F32, U32) else 2
            n = int(np.prod(shape[1:]))
            words = (n * per + 31) // 32 * 8
            lo = used[0]
            used[0] += words
            assert used[0] <= ARENA, used[0]
            flat = arena[0:shape[0], lo:lo + (n * per + 3) // 4]
            if dt != F32:
                flat = flat.bitcast(dt)
            if len(shape) == 2:
                return flat
            names = "abcd"[:len(shape) - 1]
            return flat.rearrange(f"p ({' '.join(names)}) -> p {' '.join(names)}",
                                  **{k: s for k, s in zip(names[1:], shape[2:])})

        x_loaded = sem("x_loaded")
        consts_cast = sem("consts_cast")
        consts_loaded = sem("consts_loaded")
        ones_set = sem("ones_set")
        layer_done = sem("layer_done")
        passed = sem("passed")
        out_stored = sem("out_stored")

        class Layer:
            pass

        def attention_plan(n, causal, mi_turns, acc_turns, mx_banks, st_banks, p_ring, scale, biased=False):
            L = Layer()
            L.n, L.causal, L.biased, L.scale = n, causal, biased, scale
            L.sub = causal_score_blocks() if causal else full_score_blocks()
            L.slots = sum(len(s) for s in L.sub)
            L.maxes = causal_max_slots() if causal else full_max_slots()
            L.MX, L.ST = mx_banks, st_banks
            L.PR = p_ring
            used[0] = 0
            L.w = {k: carve([P, D]) for k in ("q", "k", "v", "o")}
            L.bq, L.bk = carve([P, 1]), carve([P, 1])
            L.bv = carve([P, D])
            L.Qx = carve([P, H, T], BF16)
            L.Kx = carve([P, H, T], BF16)
            L.probs = carve([P, p_ring, T])
            L.Vx = carve([P, NT, H, VW])
            L.qf = carve([P, T])
            L.qs = carve([P, NPART, T], BF16)
            L.kr = carve([P, T])
            L.ks = carve([P, NPART, T], BF16)
            L.mx = carve([P, 2, NT, HG])
            L.mr = carve([P, NT, HG])
            L.nm = carve([P, 2, NT, NPART, HG], BF16)
            L.nmT = carve([NPART * HG, 2, T], BF16)
            L.oT = carve([P, T])
            L.rec = carve([P, NT, HG])
            L.att = carve([P, NT, D])
            L.attT = carve([P, T])
            L.qd = nc.dram_tensor(f"q_parts{n}", [H, HD, NPART, T], BF16, kind="Internal").ap()
            L.kd = nc.dram_tensor(f"k_parts{n}", [H, HD, NPART, T], BF16, kind="Internal").ap()
            common_signals(L, n, mi_turns, acc_turns)
            s = lambda name, k, before=0: Signal(sem(f"{name}{n}"), k, before)
            L.q1 = s("q_float", 1)
            L.qsplit = s("q_split", 3, 1)
            L.ksplit = s("k_split", 1)
            L.stored = s("parts_stored", 32, 1)
            L.kx = s("k_expanded", 16 * NPART * NPART, 1)
            L.qx = s("q_expanded", 16 * NPART * NPART, 1)
            L.nmrow = s("max_rows_in", 16 * NPART * NG, 1)
            L.mx_full = s("max_scores_full", NG * len(L.maxes))
            L.mx_free = s("max_scores_free", NG * len(L.maxes), len(mx_banks))
            L.st_full = s("scores_full", NG * L.slots, 1)
            L.st_free = s("scores_free", NG * L.slots, len(st_banks))
            L.p_free = s("probs_free", NG * L.slots, p_ring)
            L.nm_ready = s("max_parts_ready", NG)
            L.po_free = s("attended_free", NG, 1)
            L.started += [L.qsplit, L.stored, L.kx, L.qx, L.nmrow, L.st_full]
            L.init = [L.mx_free, L.st_free, L.p_free, L.po_free]
            assert (NG * L.slots) % p_ring == 0
            return L

        def common_signals(L, n, mi_turns, ac_turns):
            L.turn = {t: i for i, t in enumerate(mi_turns)}
            L.aturn = {t: i for i, t in enumerate(ac_turns)}
            mi, ac = len(mi_turns), len(ac_turns)
            s = lambda name, k, before=0: Signal(sem(f"{name}{n}"), k, before)
            L.weights = sem(f"weights{n}")
            L.setup = sem(f"setup{n}")
            L.mi_full, L.mi_done = s("misc_full", mi, 1), s("misc_free", mi, 1)
            L.ac_full, L.ac_done = s("sum_full", ac, 1), s("sum_free", ac, 1)
            L.stat = s("ln_stats", 2 * NT)
            L.started = [L.mi_full, L.ac_full]
            L.rs = s("ln_rstd", 2)
            L.xn_ready = s("xn_ready", 1, 1)
            L.started.append(L.xn_ready)

        def mi_take(pe, L, b, t):
            pe.wait_ge(L.mi_done.sem, L.mi_done.at(b, L.turn[t]))

        def mi_wait(eng, L, b, t):
            eng.wait_ge(L.mi_full.sem, L.mi_full.at(b, L.turn[t] + 1))

        def mi_ready(eng, L, b, t):
            eng.wait_ge(L.mi_done.sem, L.mi_done.at(b, L.turn[t] + 1))

        def ac_ready(eng, L, b, t):
            eng.wait_ge(L.ac_done.sem, L.ac_done.at(b, L.aturn[t] + 1))

        def ac_take(pe, L, b, t):
            pe.wait_ge(L.ac_done.sem, L.ac_done.at(b, L.aturn[t]))

        def ac_wait(eng, L, b, t):
            eng.wait_ge(L.ac_full.sem, L.ac_full.at(b, L.aturn[t] + 1))

        def link(dve, L, b, ins):
            L.count += 1
            ins.then_inc(L.chain.sem, 1)
            dve.wait_ge(L.chain.sem, L.chain.at(b, L.count))

        def mark(L, ins):
            L.count += 1
            ins.then_inc(L.chain.sem, 1)

        def catch(dve, L, b):
            dve.wait_ge(L.chain.sem, L.chain.at(b, L.count))

        def settle(eng):
            eng.sem_inc(passed, 1)

        def dve_norm(dve, L, b):
            for t in range(NT):
                dve.bn_stats(stats[:, t, :], x[:, b.index * NT + t, :]).then_inc(L.stat.sem, 1)
            dve.wait_ge(L.stat.sem, L.stat.at(b, NT))
            settle(dve)
            for t in range(NT):
                dve.bn_aggr(mean_var[:, t, :], stats[:, t, :]).then_inc(L.stat.sem, 1)
            dve.wait_ge(L.rs.sem, L.rs.at(b, 2))
            dve.wait_ge(L.stat.sem, L.stat.at(b, 2 * NT))
            dve.wait_ge(L.mi_full.sem, L.mi_full.before_batch(b))
            for t in range(NT):
                ins = dve.tensor_scalar(xn[:, t, :], x[:, b.index * NT + t, :], mean_var[:, t, 0:1],
                                        rstd[:, t:t + 1], ALU.subtract, ALU.mult)
            ins.then_inc(L.xn_ready.sem, 1)

        def pool_norm(pool, L, b):
            pool.wait_ge(L.stat.sem, L.stat.at(b, 2 * NT))
            pool.wait_ge(L.xn_ready.sem, L.xn_ready.at(b, 0))
            settle(pool)
            pool.tensor_scalar(rstd[:], mean_var[:, :, 1], LN_EPS, None, ALU.add).then_inc(L.rs.sem, 1)
            pool.wait_ge(L.rs.sem, L.rs.at(b, 1))
            pool.tensor_tensor(rstd[:], rstd[:], mhalf[:], ALU.pow).then_inc(L.rs.sem, 1)

        def pe_norm(pe, L, b):
            mi_take(pe, L, b, "xnT")
            pe.wait_ge(L.xn_ready.sem, L.xn_ready.at(b, 1))
            for t in range(NT):
                ins = pe.transpose(bank[0][:, t * P:(t + 1) * P], xn[:, t, :], ident[:])
            ins.then_inc(L.mi_full.sem, 1)

        def act_norm(act, L, b):
            mi_wait(act, L, b, "xnT")
            act.copy(xnT[b.parity][:], bank[0][:]).then_inc(L.mi_done.sem, 1)

        def pe_project(pe, L, b):
            xt = xnT[b.parity]
            mi_ready(pe, L, b, "xnT")
            for t in ("k", "q"):
                mi_take(pe, L, b, t)
                pe.matmul(bank[0][:], L.w[t][:], xt[:], start=True, stop=True).then_inc(L.mi_full.sem, 1)
            mi_take(pe, L, b, "v")
            for t in range(NT):
                ins = pe.matmul(bank[0][:, t * P:(t + 1) * P], xt[:, t * P:(t + 1) * P], L.w["v"][:],
                                start=True, stop=True)
            ins.then_inc(L.mi_full.sem, 1)

        def dve_split_k(dve, L, b):
            mi_wait(dve, L, b, "k")
            dve.wait_ge(L.stored.sem, L.stored.at(b, 0))
            link(dve, L, b, dve.tensor_scalar(L.ks[:, 0, :], bank[0][:], L.bk[:, 0:1], None, ALU.add))
            dve.scalar_tensor_tensor(out=L.kr[:], in0=bank[0][:], scalar=L.bk[:, 0:1], in1=L.ks[:, 0, :],
                                     op0=ALU.add, op1=ALU.subtract).then_inc(L.mi_done.sem, 1)
            mi_ready(dve, L, b, "k")
            link(dve, L, b, dve.tensor_copy(L.ks[:, 1, :], L.kr[:]))
            dve.tensor_tensor(L.ks[:, 2, :], L.kr[:], L.ks[:, 1, :], ALU.subtract).then_inc(L.ksplit.sem, 1)

        def act_split_q(act, L, b):
            mi_wait(act, L, b, "q")
            act.wait_ge(L.qsplit.sem, L.qsplit.at(b, 0))
            act.activation(L.qf[:], bank[0][:], ACT.Identity, bias=L.bq[:, 0:1]).then_inc(L.q1.sem, 1)
            act.wait_ge(L.stored.sem, L.stored.at(b, 0))
            act.activation(L.qs[:, 0, :], bank[0][:], ACT.Identity,
                           bias=L.bq[:, 0:1]).then_inc(L.mi_done.sem, 1)

        def pool_split_q(pool, L, b):
            s = L.qsplit
            pool.wait_ge(L.q1.sem, L.q1.at(b, 1))
            mi_ready(pool, L, b, "q")
            pool.tensor_tensor(L.qf[:], L.qf[:], L.qs[:, 0, :], ALU.subtract).then_inc(s.sem, 1)
            pool.wait_ge(s.sem, s.at(b, 1))
            settle(pool)
            pool.tensor_copy(L.qs[:, 1, :], L.qf[:]).then_inc(s.sem, 1)
            pool.wait_ge(s.sem, s.at(b, 2))
            pool.tensor_tensor(L.qs[:, 2, :], L.qf[:], L.qs[:, 1, :], ALU.subtract).then_inc(s.sem, 1)

        def dve_v(dve, L, b):
            mi_wait(dve, L, b, "v")
            dve.tensor_tensor(
                L.Vx[:, :, :, 0:HD], bank[0][:].rearrange("p (t h d) -> p t h d", t=NT, d=HD),
                L.bv[:].rearrange("p (o h d) -> p o h d", o=1, d=HD).to_broadcast([P, NT, H, HD]),
                ALU.add).then_inc(L.mi_done.sem, 1)

        def sp_expand(sp, L, b):
            sp.wait_ge(L.kx.sem, L.kx.at(b, 0))
            sp.wait_ge(L.qx.sem, L.qx.at(b, 0))
            settle(sp)
            sp.wait_ge(L.ksplit.sem, L.ksplit.at(b, 1))
            sp.dma_start(L.kd.rearrange("h d i t -> (h d) i t"), L.ks[:]).then_inc(L.stored.sem, 16)
            sp.wait_ge(L.qsplit.sem, L.qsplit.at(b, 3))
            sp.dma_start(L.qd.rearrange("h d i t -> (h d) i t"), L.qs[:]).then_inc(L.stored.sem, 16)
            sp.wait_ge(L.stored.sem, L.stored.at(b, 32))
            settle(sp)
            sp.wait_ge(L.st_full.sem, L.st_full.at(b, 0))
            for j in range(NPART):
                for i in range(NPART):
                    r = (j * NPART + i) * HD
                    src = L.kd[:, :, j, :].rearrange("h d t -> d h t")
                    (sp.dma_start(L.Kx[r:r + HD, :, :], src)
                       .then_inc(L.kx.sem, 16))
            for j in range(NPART):
                for i in range(NPART):
                    r = (j * NPART + i) * HD
                    src = L.qd[:, :, i, :].rearrange("h d t -> d h t")
                    sp.dma_start(L.Qx[r:r + HD, :, :], src).then_inc(L.qx.sem, 16)

        def sp_max_rows(sp, L, b, g):
            mi_ready(sp, L, b, f"nm{g}")
            for i in range(NPART):
                sp.dma_start(L.Qx[KROWS + i:KROWS + i + 1, g * HG:(g + 1) * HG, :],
                             L.nmT[i * HG:(i + 1) * HG, g % 2, :]).then_inc(L.nmrow.sem, 16)

        def pe_max(pe, L, b, g):
            if g == 0:
                pe.wait_ge(L.kx.sem, L.kx.at(b, L.kx.per_batch))
                pe.wait_ge(L.qx.sem, L.qx.at(b, L.qx.per_batch))
            n = g * len(L.maxes)
            for i, (q, heads) in enumerate(L.maxes):
                w = (q + 1) * P if L.causal else T
                mx = L.MX[(n + i) % len(L.MX)]
                pe.wait_ge(L.mx_free.sem, L.mx_free.at(b, n + i + 1 - len(L.MX)))
                for k, j in enumerate(heads):
                    h = g * HG + j
                    far = L.biased and q < 2
                    ins = pe.matmul(mx[:, k * w:(k + 1) * w], L.Qx[0:KROWS, h, q * P:(q + 1) * P],
                                    L.Kx[0:KROWS, h, 0:w], start=True, stop=not (L.causal or far))
                    if L.causal:
                        ins = pe.matmul(mx[:, k * w + q * P:k * w + (q + 1) * P], identb[:], mask_q[:],
                                        start=False, stop=True)
                    if far and q == 0:
                        pe.matmul(mx[:, 2 * P:3 * P], L.bias[:, h, P:2 * P], ident[:],
                                  start=False, stop=False)
                        ins = pe.matmul(mx[:, 3 * P:4 * P], L.bias[:, h, 0:P], ident[:],
                                        start=False, stop=True)
                    if far and q == 1:
                        ins = pe.matmul(mx[:, 3 * P:4 * P], L.bias[:, h, P:2 * P], ident[:],
                                        start=False, stop=True)
                ins.then_inc(L.mx_full.sem, 1)

        def dve_max(dve, L, b, g):
            n = g * len(L.maxes)
            for i, (q, heads) in enumerate(L.maxes):
                w = (q + 1) * P if L.causal else T
                mx = L.MX[(n + i) % len(L.MX)]
                dve.wait_ge(L.mx_full.sem, L.mx_full.at(b, n + i + 1))
                dve.reduce_max(L.mx[:, g % 2, q, heads[0]:heads[-1] + 1],
                               mx[:, 0:w * len(heads)].rearrange("p (j k) -> p j k", k=w),
                               AX.X).then_inc(L.mx_free.sem, 1)
            dve.wait_ge(L.mx_free.sem, L.mx_free.at(b, n + len(L.maxes)))
            if g >= 2:
                mi_wait(dve, L, b, f"nm{g - 2}")
            m, nm = L.mx[:, g % 2], L.nm[:, g % 2]
            link(dve, L, b, dve.tensor_scalar(nm[:, :, 0, :], m, -1.0, None, ALU.mult))
            link(dve, L, b, dve.scalar_tensor_tensor(out=L.mr[:], in0=m, scalar=-1.0, in1=nm[:, :, 0, :],
                                                     op0=ALU.mult, op1=ALU.subtract))
            link(dve, L, b, dve.tensor_copy(nm[:, :, 1, :], L.mr[:]))
            dve.tensor_tensor(nm[:, :, 2, :], L.mr[:], nm[:, :, 1, :],
                              ALU.subtract).then_inc(L.nm_ready.sem, 1)
            dve.wait_ge(L.nm_ready.sem, L.nm_ready.at(b, g + 1))

        def pe_max_rows(pe, L, b, g):
            mi_take(pe, L, b, f"nm{g}")
            pe.wait_ge(L.nm_ready.sem, L.nm_ready.at(b, g + 1))
            view = bank[0][0:NPART * HG, 0:T // 2].bitcast(BF16)
            for t in range(NT):
                ins = pe.transpose(view[:, t * P:(t + 1) * P],
                                   L.nm[:, g % 2, t, :, :].rearrange("p i j -> p (i j)"), identb[:])
            ins.then_inc(L.mi_full.sem, 1)

        def act_max_rows(act, L, b, g):
            mi_wait(act, L, b, f"nm{g}")
            act.wait_ge(L.nmrow.sem, L.nmrow.at(b, 16 * NPART * max(g - 1, 0)))
            view = bank[0][0:NPART * HG, 0:T // 2].bitcast(BF16)
            act.copy(L.nmT[:, g % 2, :], view).then_inc(L.mi_done.sem, 1)

        def pe_scores(pe, L, b, g, k):
            n = g * L.slots + sum(len(s) for s in L.sub[:k])
            for i, blocks in enumerate(L.sub[k]):
                st = L.ST[(n + i) % len(L.ST)]
                pe.wait_ge(L.st_free.sem, L.st_free.at(b, n + i + 1 - len(L.ST)))
                for j, kb, c in blocks:
                    h = g * HG + j
                    w = T - kb * P if L.causal else T
                    far = L.biased and kb >= 2
                    ins = pe.matmul(st[:, c:c + w], L.Kx[0:KAUG, h, kb * P:(kb + 1) * P],
                                    L.Qx[0:KAUG, h, T - w:T], start=True, stop=not (L.causal or far))
                    if L.causal:
                        ins = pe.matmul(st[:, c:c + P], identb[:], mask_k[:], start=False, stop=True)
                    if far and kb == 2:
                        ins = pe.matmul(st[:, 0:P], ident[:], L.bias[:, h, P:2 * P],
                                        start=False, stop=True)
                    if far and kb == 3:
                        ins = pe.matmul(st[:, 0:2 * P], ident[:], L.bias[:, h, 0:2 * P],
                                        start=False, stop=True)
                ins.then_inc(L.st_full.sem, 1)

        def act_exp(act, L, b, g, k):
            n = g * L.slots + sum(len(s) for s in L.sub[:k])
            for i, blocks in enumerate(L.sub[k]):
                st = L.ST[(n + i) % len(L.ST)]
                w = T if len(blocks) == 1 else sum(T - kb * P for _, kb, _ in blocks)
                act.wait_ge(L.st_full.sem, L.st_full.at(b, n + i + 1))
                act.wait_ge(L.p_free.sem, L.p_free.at(b, n + i + 1 - L.PR))
                act.activation(L.probs[:, (n + i) % L.PR, 0:w], st[:, 0:w], ACT.Exp,
                               scale=L.scale).then_inc(L.st_free.sem, 1)

        def pe_attend(pe, L, b, g, k):
            n = g * L.slots + sum(len(s) for s in L.sub[:k])
            m = len(L.sub[k])
            if k == 0:
                pe.wait_ge(L.po_free.sem, L.po_free.at(b, g))
                mi_ready(pe, L, b, "v")
            pe.wait_ge(L.st_free.sem, L.st_free.at(b, n + m))
            pieces = sorted((kb, j, i, c) for i, blocks in enumerate(L.sub[k]) for j, kb, c in blocks)
            for kb, j, i, c in pieces:
                w = T - kb * P if L.causal else T
                h = g * HG + j
                ins = pe.matmul(bank[2][j * VW:(j + 1) * VW, T - w:T], L.Vx[:, kb, h, :],
                                L.probs[:, (n + i) % L.PR, c:c + w], start=(kb == 0),
                                stop=(k == len(L.sub) - 1), skip_group_check=True)
            ins.then_inc(L.p_free.sem, m)

        def dve_attended(dve, L, b, g):
            dve.wait_ge(L.p_free.sem, L.p_free.at(b, (g + 1) * L.slots))
            dve.tensor_copy(L.oT[:], bank[2][:]).then_inc(L.po_free.sem, 1)

        def pe_attended(pe, L, b, g):
            mi_take(pe, L, b, f"pt{g}")
            pe.wait_ge(L.po_free.sem, L.po_free.at(b, g + 1))
            for t in range(NT):
                ins = pe.transpose(bank[0][:, t * P:(t + 1) * P], L.oT[:, t * P:(t + 1) * P], ident[:])
            ins.then_inc(L.mi_full.sem, 1)

        def dve_divide(dve, L, b, g):
            mi_wait(dve, L, b, f"pt{g}")
            view = bank[0][:].rearrange("p (t j c) -> p t j c", t=NT, c=VW)
            link(dve, L, b, dve.reciprocal(L.rec[:], view[:, :, :, HD]))
            dve.tensor_tensor(
                L.att[:, :, g * HG * HD:(g + 1) * HG * HD].rearrange("p t (j d) -> p t j d", d=HD),
                view[:, :, :, 0:HD], L.rec[:].unsqueeze(3).to_broadcast([P, NT, HG, HD]),
                ALU.mult).then_inc(L.mi_done.sem, 1)

        def pe_turn_attention(pe, L, b):
            mi_take(pe, L, b, "aT")
            mi_ready(pe, L, b, "pt3")
            for t in range(NT):
                ins = pe.transpose(bank[0][:, t * P:(t + 1) * P], L.att[:, t, :], ident[:])
            ins.then_inc(L.mi_full.sem, 1)

        def act_turn_attention(act, L, b):
            mi_wait(act, L, b, "aT")
            act.wait_ge(L.ac_full.sem, L.ac_full.at(b, 0))
            act.copy(L.attT[:], bank[0][:]).then_inc(L.mi_done.sem, 1)

        def pe_out(pe, L, b):
            mi_ready(pe, L, b, "aT")
            for t in range(NT):
                ins = pe.matmul(bank[1][:, t * P:(t + 1) * P], L.attT[:, t * P:(t + 1) * P], L.w["o"][:],
                                start=False, stop=True, skip_group_check=True)
            return ins

        def pe_attention(pe, L, b):
            for g in range(NG + 1):
                if g < NG:
                    pe_max(pe, L, b, g)
                if g >= 1:
                    pe.wait_ge(L.nmrow.sem, L.nmrow.at(b, 16 * NPART * g))
                    for k in range(len(L.sub) + 1):
                        if k < len(L.sub):
                            pe_scores(pe, L, b, g - 1, k)
                        if k >= 1:
                            pe_attend(pe, L, b, g - 1, k - 1)
                if g < NG:
                    pe_max_rows(pe, L, b, g)
                if g >= 1:
                    pe_attended(pe, L, b, g - 1)

        def dve_attention(dve, L, b):
            for g in range(NG + 1):
                if g < NG:
                    dve_max(dve, L, b, g)
                if g >= 1:
                    dve_attended(dve, L, b, g - 1)
                    dve_divide(dve, L, b, g - 1)

        def sp_attention(sp, L, b):
            sp_expand(sp, L, b)
            for g in range(NG):
                sp_max_rows(sp, L, b, g)

        ATT_TURNS = ["nm0", "nm1", "pt0", "nm2", "pt1", "nm3", "pt2", "pt3"]

        def pool_attention_setup(pool, L):
            pool.memset(L.Kx[64:96, :, :], 1.0).then_inc(L.setup, 1)
            pool.wait_ge(L.setup, 1)
            pool.memset(L.Vx[:, :, :, HD:VW], 0.0).then_inc(L.setup, 1)
            pool.wait_ge(L.setup, 2)
            pool.memset(L.Vx[:, :, :, HD:HD + 1], 1.0).then_inc(L.setup, 1)

        def each_batch(eng, body):
            with eng.Fori(0, NBATCH // NHALF) as pair:
                for half in range(NHALF):
                    body(Batch(pair, half))

        def load(sp, L, dst, src):
            sp.dma_start(dst, src).then_inc(L.weights, 16)
            L.loads += 1

        def pe_bias(pe, bias):
            return pe.matmul(bank[1][:], ones[0:1, :],
                             bias[0:1, :].rearrange("p (o n) -> p o n", o=1).to_broadcast([1, NT, D]),
                             start=True, stop=False, skip_group_check=True)

        def pe_logits(pe, L, b, w, e):
            mi_take(pe, L, b, "logit")
            for t in range(NT):
                ins = pe.matmul(bank[0][:, t * e:(t + 1) * e], xnT[b.parity][:, t * P:(t + 1) * P], w,
                                start=True, stop=True)
            ins.then_inc(L.mi_full.sem, 1)

        def pe_down(pe, L, b, e, hidden_there, count):
            ac_take(pe, L, b, f"y{e}")
            pe.wait_ge(hidden_there.sem, hidden_there.at(b, count))
            for t in range(NT):
                for f in range(4):
                    ins = pe.matmul(bank[1][:, t * P:(t + 1) * P], L.hT[:, e % 2, f, t * P:(t + 1) * P],
                                    L.w2[:, e, f, :], start=(f == 0), stop=(f == 3))
            ins.then_inc(L.ac_full.sem, 1)

        def hidden_buffer_free(eng, L, b, e):
            if e >= 2:
                ac_wait(eng, L, b, f"y{e - 2}")
            else:
                eng.wait_ge(L.ac_full.sem, L.ac_full.at(b, 0))

        def dve_combine(dve, L, b, e, n_experts):
            ac_wait(dve, L, b, f"y{e}")
            last = e == n_experts - 1
            if e:
                ac_ready(dve, L, b, f"y{e - 1}")
            for t in range(NT):
                dst = x[:, b.index * NT + t, :] if last else acc[:, t, :]
                ins = dve.scalar_tensor_tensor(
                    out=dst, in0=bank[1][:, t * P:(t + 1) * P], scalar=L.wd[:, t, e:e + 1],
                    in1=acc[:, t, :], op0=ALU.mult, op1=ALU.add)
                if t < NT - 1:
                    mark(L, ins)
            ins.then_inc(L.ac_done.sem, 1)

        def dve_residual(dve, L, b):
            ac_wait(dve, L, b, "out")
            dve.tensor_tensor(acc[:], bank[1][:].rearrange("p (t n) -> p t n", t=NT),
                              x[:, bass.ds(b.index * NT, NT), :], ALU.add).then_inc(L.ac_done.sem, 1)
            ac_ready(dve, L, b, "out")

        def groups(eng):
            return range(NG + 1)

        def layer0():
            L = attention_plan(0, True, ["xnT", "k", "q", "v", "logit"] + ATT_TURNS + ["wT", "aT"],
                               ["out"] + [f"y{e}" for e in range(E0)],
                               [bank[3]], [bank[4], bank[5]], 10, float(HD) ** -0.5)
            s = lambda name, k, before=0: Signal(sem(f"{name}0"), k, before)
            L.w1 = carve([P, E0, F0])
            L.w2 = carve([P, E0, 4, D])
            L.b1 = carve([P, E0 * 4])
            L.b2 = carve([E0, D])
            L.keysT, L.rwT, L.rb = carve([P, E0]), carve([P, E0]), carve([P, E0])
            L.logit_w, L.logit_shift, L.ksq = carve([P, E0]), carve([P, E0]), carve([P, E0])
            L.bo = carve([1, D])
            L.lg = carve([P, NT, E0])
            L.top = carve([P, NT, 8])
            L.idx = carve([P, NT, 8], U32)
            L.idxf = carve([P, NT, TOP0])
            L.ev = carve([P, NT, TOP0])
            L.es = carve([P, NT])
            L.eq = carve([P, NT * TOP0, E0])
            L.wd = carve([P, NT, E0])
            L.wT = carve([E0, T])
            L.hT = carve([P, 2, 4, T])
            L.chain = s("dve_chain", 80)
            L.gate_in = s("gate_diffs", 1)
            L.gate_exp = s("gate_exps", 1)
            L.wd_ready = s("gates_ready", 1)
            L.h_full = s("hidden_full", E0 * 4)
            L.h_free = s("hidden_free", E0 * 4, 2)
            L.init += [L.h_free]
            L.experts = [sem(f"experts0_{i}") for i in range(4)]
            L.keys_squared, L.keys_summed = sem("keys_squared"), sem("keys_summed")
            HB = [bank[6], bank[7]]

            def sp_prog(sp):
                L.loads = 0
                for dst, name in ((L.w["k"], "L0_attn_Wk"), (L.w["q"], "L0_attn_Wq"), (L.w["v"], "L0_attn_Wv"),
                                  (L.w["o"], "L0_attn_Wo"), (L.bq, "L0_attn_bq"), (L.bk, "L0_attn_bk"),
                                  (L.bo, "L0_attn_bo"), (L.b1, "L0_ffn_b1"), (L.b2, "L0_ffn_b2"),
                                  (L.keysT, "L0_ffn_keys"), (L.rwT, "L0_ffn_rw")):
                    load(sp, L, dst, a[name])
                load(sp, L, L.bv, a["L0_attn_bv"].partition_broadcast(P))
                load(sp, L, L.rb, a["L0_ffn_rb"].partition_broadcast(P))
                for i in range(4):
                    e = slice(4 * i, 4 * i + 4)
                    sp.dma_start(L.w1[:, e, :], a["L0_ffn_w1"][:, e, :]).then_inc(L.experts[i], 16)
                    sp.dma_start(L.w2[:, e, :, :], a["L0_ffn_w2"][:, e, :, :]).then_inc(L.experts[i], 16)
                each_batch(sp, lambda b: sp_attention(sp, L, b))

            def pool_prog(pool):
                pool_attention_setup(pool, L)

                def body(b):
                    pool_norm(pool, L, b)
                    pool_split_q(pool, L, b)
                each_batch(pool, body)

            def act_prog(act):
                act.wait_ge(L.weights, 16 * 13)

                def body(b):
                    act_norm(act, L, b)
                    act_split_q(act, L, b)
                    act.wait_ge(L.gate_in.sem, L.gate_in.at(b, 1))
                    act.activation(L.ev[:], L.ev[:], ACT.Exp).then_inc(L.gate_exp.sem, 1)
                    for g in range(NG + 1):
                        if g >= 1:
                            for k in range(len(L.sub)):
                                act_exp(act, L, b, g - 1, k)
                        if g < NG:
                            act_max_rows(act, L, b, g)
                    mi_wait(act, L, b, "wT")
                    act.copy(L.wT[:], bank[0][0:E0, :]).then_inc(L.mi_done.sem, 1)
                    act_turn_attention(act, L, b)
                    for e in range(E0):
                        hidden_buffer_free(act, L, b, e)
                        for f in range(4):
                            n = 4 * e + f
                            act.wait_ge(L.h_full.sem, L.h_full.at(b, n + 1))
                            act.activation(L.hT[:, e % 2, f, :], HB[n % 2][:], ACT.Gelu,
                                           bias=L.b1[:, n:n + 1]).then_inc(L.h_free.sem, 1)
                each_batch(act, body)

            def pe_prog(pe):
                pe.wait_ge(L.weights, 16 * 13)
                pe.wait_ge(L.setup, 3)
                pe.wait_ge(L.keys_squared, 2)
                pe.matmul(bank[1][:, 0:E0], ones[:], L.ksq[:], start=True, stop=True).then_inc(L.keys_summed, 1)
                pe.wait_ge(L.keys_squared, 3)

                def body(b):
                    pe_norm(pe, L, b)
                    pe_project(pe, L, b)
                    pe_logits(pe, L, b, L.logit_w[:], E0)
                    pe_attention(pe, L, b)
                    mi_take(pe, L, b, "wT")
                    pe.wait_ge(L.wd_ready.sem, L.wd_ready.at(b, 1))
                    for t in range(NT):
                        ins = pe.transpose(bank[0][0:E0, t * P:(t + 1) * P], L.wd[:, t, :], ident[:])
                    ins.then_inc(L.mi_full.sem, 1)
                    pe_turn_attention(pe, L, b)
                    ac_take(pe, L, b, "out")
                    pe_bias(pe, L.bo)
                    for t in range(NT):
                        pe.matmul(bank[1][:, t * P:(t + 1) * P], L.wT[:, t * P:(t + 1) * P], L.b2[:],
                                  start=False, stop=False, skip_group_check=True)
                    pe_out(pe, L, b).then_inc(L.ac_full.sem, 1)
                    for e in range(E0 + 1):
                        if e < E0:
                            if e % 4 == 0:
                                pe.wait_ge(L.experts[e // 4], 32)
                            for f in range(4):
                                n = 4 * e + f
                                pe.wait_ge(L.h_free.sem, L.h_free.at(b, n - 1))
                                pe.matmul(HB[n % 2][:], L.w1[:, e, f * P:(f + 1) * P], xnT[b.parity][:],
                                          start=True, stop=True).then_inc(L.h_full.sem, 1)
                        if e >= 1:
                            pe_down(pe, L, b, e - 1, L.h_free, 4 * e)
                each_batch(pe, body)

            def dve_prog(dve):
                dve.wait_ge(L.weights, 16 * 13)
                dve.tensor_tensor(L.ksq[:], L.keysT, L.keysT, ALU.mult).then_inc(L.keys_squared, 1)
                dve.scalar_tensor_tensor(out=L.logit_w[:], in0=L.keysT, scalar=2.0, in1=L.rwT, op0=ALU.mult,
                                         op1=ALU.add).then_inc(L.keys_squared, 1)
                dve.wait_ge(L.keys_summed, 1)
                dve.tensor_tensor(L.logit_shift[:], L.rb, bank[1][:, 0:E0], ALU.subtract).then_inc(L.keys_squared, 1)
                dve.wait_ge(L.keys_squared, 3)

                def body(b):
                    L.count = 0
                    dve_norm(dve, L, b)
                    dve_split_k(dve, L, b)
                    dve_v(dve, L, b)
                    mi_wait(dve, L, b, "logit")
                    dve.tensor_tensor(L.lg[:], bank[0][:, 0:NT * E0].rearrange("p (t e) -> p t e", t=NT),
                                      L.logit_shift[:].unsqueeze(1).to_broadcast([P, NT, E0]),
                                      ALU.add).then_inc(L.mi_done.sem, 1)
                    mi_ready(dve, L, b, "logit")
                    settle(dve)
                    for t in range(NT):
                        mark(L, dve.max(L.top[:, t, :], L.lg[:, t, :]))
                    catch(dve, L, b)
                    dve.tensor_tensor(L.ev[:], L.top[:, :, 0:TOP0],
                                      L.top[:, :, 0:1].to_broadcast([P, NT, TOP0]),
                                      ALU.subtract).then_inc(L.gate_in.sem, 1)
                    for t in range(NT):
                        mark(L, dve.max_index(L.idx[:, t, :], L.top[:, t, :], L.lg[:, t, :]))
                    catch(dve, L, b)
                    link(dve, L, b, dve.tensor_copy(L.idxf[:], L.idx[:, :, 0:TOP0]))
                    wide = [P, NT * TOP0, E0]
                    link(dve, L, b, dve.tensor_tensor(
                        L.eq[:], iota16[:].unsqueeze(1).to_broadcast(wide),
                        L.idxf[:].rearrange("p t k -> p (t k)").unsqueeze(2).to_broadcast(wide), ALU.is_equal))
                    dve.wait_ge(L.gate_exp.sem, L.gate_exp.at(b, 1))
                    link(dve, L, b, dve.reduce_sum(L.es[:], L.ev[:], AX.X))
                    link(dve, L, b, dve.reciprocal(L.es[:], L.es[:]))
                    link(dve, L, b, dve.tensor_tensor(
                        L.ev[:], L.ev[:], L.es[:].unsqueeze(2).to_broadcast([P, NT, TOP0]), ALU.mult))
                    link(dve, L, b, dve.tensor_tensor(
                        L.eq[:], L.eq[:],
                        L.ev[:].rearrange("p t k -> p (t k)").unsqueeze(2).to_broadcast(wide), ALU.mult))
                    dve.reduce_sum(L.wd[:], L.eq[:].rearrange("p (t k) e -> p t e k", t=NT),
                                   AX.X).then_inc(L.wd_ready.sem, 1)
                    dve_attention(dve, L, b)
                    dve.wait_ge(L.wd_ready.sem, L.wd_ready.at(b, 1))
                    dve_residual(dve, L, b)
                    for e in range(E0):
                        dve_combine(dve, L, b, e, E0)
                    assert L.count == L.chain.per_batch, L.count
                each_batch(dve, body)

            return L, sp_prog, pool_prog, act_prog, pe_prog, dve_prog

        def layer1():
            class L:
                pass
            used[0] = 0
            FT = H1 * DK1 // P
            SLOTS = 3
            common_signals(L, 1, ["xnT", "logit"] + [f"yT{c}" for c in range(FT)],
                           [f"h{h}" for h in range(H1)] + ["out"] + [f"y{e}" for e in range(E1)])
            s = lambda name, k, before=0: Signal(sem(f"{name}1"), k, before)
            L.init = []
            L.w = {k: carve([P, H1 * DK1]) for k in "kqvg"}
            L.wo = carve([P, FT, D])
            L.bg = carve([1, H1 * DK1])
            L.rw = carve([P, E1])
            L.rb = carve([P, E1])
            L.w1 = carve([P, E1, 2 * F1])
            L.w2 = carve([P, E1, 4, D])
            L.dist = carve([P, T])
            L.decay = carve([P, 3, H1])
            L.lng = carve([P, H1])
            L.dt = carve([P, H1, T])
            L.kq = {k: carve([P, FT, T]) for k in "kq"}
            L.relu = carve([P, 2, T])
            L.neg = carve([P, 2, T])
            L.V = carve([P, NT, H1, V1W])
            L.eg = carve([P, NT, H1 * DK1])
            L.am = carve([P, 2 * SLOTS, T])
            L.den = carve([P, NT])
            L.div = carve([P, NT, DK1])
            L.y = carve([P, NT, H1 * DK1])
            L.yT = carve([P, FT, T])
            L.lg = carve([P, NT, E1])
            L.top = carve([P, NT, 8])
            L.idx = carve([P, NT, 8], U32)
            L.idxf = carve([P, NT])
            L.ev = carve([P, NT, E1])
            L.es = carve([P, NT])
            L.wd = carve([P, NT, E1])
            L.silu = carve([P, 2, T])
            L.hT = carve([P, 2, 4, T])
            L.chain = s("dve_chain", 69)
            L.gate_in = s("gate_diffs", 1)
            L.gate_exp = s("gate_exps", 1)
            L.exp_ready = s("phi_exp", 2 * FT)
            L.phi = s("phi_ready", 2 * FT, 1)
            L.a_full = s("a_full", 3 * FT + 4 * E1)
            L.a_free = s("a_free", 3 * FT + 4 * E1, 2)
            L.g_full = s("g_full", NT + 4 * E1)
            L.g_free = s("g_free", NT + 4 * E1, 2)
            L.s_full = s("decayed_full", SLOTS * H1, 1)
            L.s_free = s("decayed_free", SLOTS * H1, 2)
            L.init = [L.a_free, L.g_free, L.s_free]
            L.started += [L.phi, L.s_full]
            L.experts = sem("experts1")
            L.decay_act, L.decay_dve = sem("decay_act"), sem("decay_dve")
            A, G, S = [bank[4], bank[5]], [bank[6], bank[7]], [bank[2], bank[3]]
            NW = 16 * 10

            def sp_prog(sp):
                L.loads = 0
                load(sp, L, L.decay[:, 0, :], a["L1_attn_decay_log"].partition_broadcast(P))
                load(sp, L, L.dist, a["const_dist"])
                for k, name in zip("kqvg", ("W_K", "W_Q", "W_V", "W_g_w")):
                    load(sp, L, L.w[k], a["L1_attn_" + name])
                load(sp, L, L.bg, a["L1_attn_W_g_b"])
                load(sp, L, L.wo, a["L1_attn_W_O"])
                load(sp, L, L.rw, a["L1_ffn_router_w"])
                load(sp, L, L.rb, a["L1_ffn_router_b"].partition_broadcast(P))
                sp.dma_start(L.w1, a["L1_ffn_w1"]).then_inc(L.experts, 16)
                sp.dma_start(L.w2, a["L1_ffn_w2"]).then_inc(L.experts, 16)

            def pool_prog(pool):
                pool.memset(L.V[:, :, :, DK1:V1W], 1.0).then_inc(L.setup, 1)

                def body(b):
                    pool_norm(pool, L, b)
                    for n in range(2 * FT):
                        dst = L.kq["kq"[n // FT]][:, n % FT, :]
                        pool.wait_ge(L.exp_ready.sem, L.exp_ready.at(b, n + 1))
                        if n == 0:
                            pool.wait_ge(L.s_full.sem, L.s_full.at(b, 0))
                        pool.tensor_tensor(dst, L.relu[:, n % 2, :], L.neg[:, n % 2, :],
                                           ALU.add).then_inc(L.phi.sem, 1)
                each_batch(pool, body)

            def act_prog(act):
                act.wait_ge(L.weights, NW)
                act.activation(L.decay[:, 1, :], L.decay[:, 0, :], ACT.Abs).then_inc(L.decay_act, 1)
                act.wait_ge(L.decay_act, 1)
                act.activation(L.decay[:, 1, :], L.decay[:, 1, :], ACT.Exp, scale=-1.0).then_inc(L.decay_act, 1)
                act.wait_ge(L.decay_dve, 1)
                act.activation(L.decay[:, 2, :], L.decay[:, 1, :], ACT.Ln).then_inc(L.decay_act, 1)
                act.wait_ge(L.decay_dve, 3)
                for h in range(H1):
                    act.activation(L.dt[:, h, :], L.dist[:], ACT.Exp,
                                   scale=L.lng[:, h:h + 1]).then_inc(L.decay_act, 1)

                def body(b):
                    act_norm(act, L, b)
                    for n in range(2 * FT):
                        act.wait_ge(L.a_full.sem, L.a_full.at(b, n + 1))
                        act.wait_ge(L.phi.sem, L.phi.at(b, max(n - 1, 0)))
                        act.activation(L.relu[:, n % 2, :], A[n % 2][:], ACT.Relu)
                        act.activation(L.neg[:, n % 2, :], A[n % 2][:], ACT.Relu,
                                       scale=-1.0).then_inc(L.a_free.sem, 1)
                        act.wait_ge(L.a_free.sem, L.a_free.at(b, n + 1))
                        act.activation(L.neg[:, n % 2, :], L.neg[:, n % 2, :], ACT.Exp,
                                       scale=-1.0).then_inc(L.exp_ready.sem, 1)
                    for t in range(NT):
                        n = 2 * FT + t
                        act.wait_ge(L.a_full.sem, L.a_full.at(b, n + 1))
                        act.activation(L.eg[:, t, :], A[n % 2][:], ACT.Exp, scale=-1.0).then_inc(L.a_free.sem, 1)
                    act.wait_ge(L.gate_in.sem, L.gate_in.at(b, 1))
                    act.activation(L.ev[:], L.ev[:], ACT.Exp).then_inc(L.gate_exp.sem, 1)
                    for c in range(FT):
                        mi_wait(act, L, b, f"yT{c}")
                        act.copy(L.yT[:, c, :], bank[0][:]).then_inc(L.mi_done.sem, 1)
                    for e in range(E1):
                        for f in range(4):
                            n = 4 * e + f
                            act.wait_ge(L.a_full.sem, L.a_full.at(b, 3 * FT + n + 1))
                            act.wait_ge(L.g_free.sem, L.g_free.at(b, NT + n - 1))
                            act.activation(L.silu[:, n % 2, :], A[n % 2][:], ACT.Silu).then_inc(L.a_free.sem, 1)
                each_batch(act, body)

            def pe_prog(pe):
                pe.wait_ge(L.weights, NW)
                pe.wait_ge(L.setup, 1)

                def scores(b, h):
                    lo, m = DK1 * (h % 2), h // 2
                    rows = slice(lo, lo + DK1)
                    for i, blocks in enumerate([[(0, 0)], [(1, 0), (3, T - P)], [(2, 0)]]):
                        n = SLOTS * h + i
                        pe.wait_ge(L.s_free.sem, L.s_free.at(b, n - 1))
                        for kb, c in blocks:
                            ins = pe.matmul(S[n % 2][:, c:c + T - kb * P], L.kq["k"][rows, m, kb * P:(kb + 1) * P],
                                            L.kq["q"][rows, m, kb * P:T], start=True, stop=True)
                        ins.then_inc(L.s_full.sem, 1)

                def attend(b, h):
                    where = {0: (0, 0), 1: (1, 0), 2: (2, 0), 3: (1, T - P)}
                    ac_take(pe, L, b, f"h{h}")
                    pe.wait_ge(L.s_free.sem, L.s_free.at(b, SLOTS * (h + 1)))
                    for t in range(NT):
                        for kb in range(t + 1):
                            slot, c = where[kb]
                            c += (t - kb) * P
                            ins = pe.matmul(bank[1][:, t * V1W:(t + 1) * V1W],
                                            L.am[:, SLOTS * (h % 2) + slot, c:c + P], L.V[:, kb, h, :],
                                            start=(kb == 0), stop=(kb == t))
                    ins.then_inc(L.ac_full.sem, 1)

                def body(b):
                    xt = xnT[b.parity]
                    pe_norm(pe, L, b)
                    mi_ready(pe, L, b, "xnT")
                    pe_logits(pe, L, b, L.rw[:], E1)
                    for n in range(2 * FT):
                        pe.wait_ge(L.a_free.sem, L.a_free.at(b, n - 1))
                        pe.matmul(A[n % 2][:], L.w["kq"[n // FT]][:, (n % FT) * P:(n % FT + 1) * P], xt[:],
                                  start=True, stop=True).then_inc(L.a_full.sem, 1)
                    for t in range(NT):
                        pe.wait_ge(L.g_free.sem, L.g_free.at(b, t - 1))
                        pe.matmul(G[t % 2][:], xt[:, t * P:(t + 1) * P], L.w["v"][:],
                                  start=True, stop=True).then_inc(L.g_full.sem, 1)
                        n = 2 * FT + t
                        pe.wait_ge(L.a_free.sem, L.a_free.at(b, n - 1))
                        pe.matmul(A[n % 2][:], ones[0:1, :], L.bg[:], start=True, stop=False)
                        pe.matmul(A[n % 2][:], xt[:, t * P:(t + 1) * P], L.w["g"][:],
                                  start=False, stop=True).then_inc(L.a_full.sem, 1)
                    pe.wait_ge(L.phi.sem, L.phi.at(b, 2 * FT))
                    pe.wait_ge(L.g_free.sem, L.g_free.at(b, NT))
                    for h in range(H1 + 1):
                        if h < H1:
                            scores(b, h)
                        if h >= 1:
                            attend(b, h - 1)
                    for c in range(FT):
                        mi_take(pe, L, b, f"yT{c}")
                        ac_ready(pe, L, b, f"h{H1 - 1}")
                        for t in range(NT):
                            ins = pe.transpose(bank[0][:, t * P:(t + 1) * P], L.y[:, t, c * P:(c + 1) * P],
                                               ident[:])
                        ins.then_inc(L.mi_full.sem, 1)
                    ac_take(pe, L, b, "out")
                    mi_ready(pe, L, b, f"yT{FT - 1}")
                    for t in range(NT):
                        for c in range(FT):
                            ins = pe.matmul(bank[1][:, t * P:(t + 1) * P], L.yT[:, c, t * P:(t + 1) * P],
                                            L.wo[:, c, :], start=(c == 0), stop=(c == FT - 1))
                    ins.then_inc(L.ac_full.sem, 1)
                    pe.wait_ge(L.experts, 32)
                    for e in range(E1 + 1):
                        if e < E1:
                            for f in range(4):
                                n = 4 * e + f
                                pe.wait_ge(L.a_free.sem, L.a_free.at(b, 3 * FT + n - 1))
                                pe.matmul(A[n % 2][:], L.w1[:, e, f * P:(f + 1) * P], xt[:],
                                          start=True, stop=True).then_inc(L.a_full.sem, 1)
                                pe.wait_ge(L.g_free.sem, L.g_free.at(b, NT + n - 1))
                                pe.matmul(G[n % 2][:], L.w1[:, e, F1 + f * P:F1 + (f + 1) * P], xt[:],
                                          start=True, stop=True).then_inc(L.g_full.sem, 1)
                        if e >= 1:
                            pe_down(pe, L, b, e - 1, L.g_free, NT + 4 * e)
                each_batch(pe, body)

            def dve_prog(dve):
                dve.wait_ge(L.weights, NW)
                dve.wait_ge(L.decay_act, 2)
                dve.tensor_scalar(L.decay[:, 1, :], L.decay[:, 1, :], 1.0, None, ALU.add).then_inc(L.decay_dve, 1)
                dve.tensor_scalar(L.lng[:], L.decay[:, 0, :], 0.0, None, ALU.min).then_inc(L.decay_dve, 1)
                dve.wait_ge(L.decay_dve, 2)
                dve.wait_ge(L.decay_act, 3)
                dve.tensor_tensor(L.lng[:], L.lng[:], L.decay[:, 2, :], ALU.subtract).then_inc(L.decay_dve, 1)
                dve.wait_ge(L.decay_act, 3 + H1)
                dve.tensor_tensor(L.dt[:, :, 0:P], L.dt[:, :, 0:P],
                                  mask_f[:].unsqueeze(1).to_broadcast([P, H1, P]), ALU.mult).then_inc(L.decay_dve, 1)
                dve.wait_ge(L.decay_dve, 4)

                def decay(b, h):
                    if h >= 2:
                        ac_wait(dve, L, b, f"h{h - 2}")
                    else:
                        dve.wait_ge(L.ac_full.sem, L.ac_full.at(b, 0))
                    for i in range(SLOTS):
                        n = SLOTS * h + i
                        am = L.am[:, SLOTS * (h % 2) + i, :]
                        dve.wait_ge(L.s_full.sem, L.s_full.at(b, n + 1))
                        parts = [(0, T)] if i == 0 else [(0, T - P), (T - P, P)] if i == 1 else [(0, T - 2 * P)]
                        for k, (c, w) in enumerate(parts):
                            ins = dve.tensor_tensor(am[:, c:c + w], S[n % 2][:, c:c + w], L.dt[:, h, 0:w], ALU.mult)
                            if k < len(parts) - 1:
                                mark(L, ins)
                        ins.then_inc(L.s_free.sem, 1)

                def divide(b, h):
                    ac_wait(dve, L, b, f"h{h}")
                    num = bank[1][:, 0:NT * V1W].rearrange("p (t c) -> p t c", t=NT)
                    cols = slice(h * DK1, (h + 1) * DK1)
                    link(dve, L, b, dve.tensor_scalar(L.den[:], num[:, :, DK1], EPS1, None, ALU.add))
                    link(dve, L, b, dve.scalar_tensor_tensor(
                        out=L.div[:], in0=L.eg[:, :, cols], scalar=1.0,
                        in1=L.den[:].unsqueeze(2).to_broadcast([P, NT, DK1]), op0=ALU.add, op1=ALU.mult))
                    link(dve, L, b, dve.reciprocal(L.div[:], L.div[:]))
                    dve.tensor_tensor(L.y[:, :, cols], num[:, :, 0:DK1], L.div[:],
                                      ALU.mult).then_inc(L.ac_done.sem, 1)

                def body(b):
                    L.count = 0
                    dve_norm(dve, L, b)
                    mi_wait(dve, L, b, "logit")
                    dve.tensor_tensor(L.lg[:], bank[0][:, 0:NT * E1].rearrange("p (t e) -> p t e", t=NT),
                                      L.rb[:].unsqueeze(1).to_broadcast([P, NT, E1]),
                                      ALU.add).then_inc(L.mi_done.sem, 1)
                    mi_ready(dve, L, b, "logit")
                    settle(dve)
                    for t in range(NT):
                        mark(L, dve.max(L.top[:, t, :], L.lg[:, t, :]))
                    catch(dve, L, b)
                    dve.tensor_tensor(L.ev[:], L.lg[:], L.top[:, :, 0:1].to_broadcast([P, NT, E1]),
                                      ALU.subtract).then_inc(L.gate_in.sem, 1)
                    for t in range(NT):
                        mark(L, dve.max_index(L.idx[:, t, :], L.top[:, t, :], L.lg[:, t, :]))
                    for t in range(NT):
                        dve.wait_ge(L.g_full.sem, L.g_full.at(b, t + 1))
                        dve.tensor_copy(L.V[:, t, :, 0:DK1],
                                        G[t % 2][:].rearrange("p (h d) -> p h d", h=H1)).then_inc(L.g_free.sem, 1)
                    catch(dve, L, b)
                    link(dve, L, b, dve.tensor_copy(L.idxf[:], L.idx[:, :, 0]))
                    wide = [P, NT, E1]
                    link(dve, L, b, dve.tensor_tensor(
                        L.wd[:], iota16[:, 0:E1].unsqueeze(1).to_broadcast(wide),
                        L.idxf[:].unsqueeze(2).to_broadcast(wide), ALU.is_equal))
                    dve.wait_ge(L.gate_exp.sem, L.gate_exp.at(b, 1))
                    link(dve, L, b, dve.reduce_sum(L.es[:], L.ev[:], AX.X))
                    link(dve, L, b, dve.reciprocal(L.es[:], L.es[:]))
                    link(dve, L, b, dve.tensor_tensor(
                        L.wd[:], L.wd[:], L.es[:].unsqueeze(2).to_broadcast(wide), ALU.mult))
                    for h in range(H1 + 1):
                        if h < H1:
                            decay(b, h)
                        if h >= 1:
                            divide(b, h - 1)
                    dve_residual(dve, L, b)
                    for e in range(E1 + 1):
                        if e < E1:
                            hidden_buffer_free(dve, L, b, e)
                            for f in range(4):
                                n = 4 * e + f
                                dve.wait_ge(L.g_full.sem, L.g_full.at(b, NT + n + 1))
                                dve.wait_ge(L.a_free.sem, L.a_free.at(b, 3 * FT + n + 1))
                                dve.tensor_tensor(L.hT[:, e % 2, f, :], L.silu[:, n % 2, :], G[n % 2][:],
                                                  ALU.mult).then_inc(L.g_free.sem, 1)
                        if e >= 1:
                            dve_combine(dve, L, b, e - 1, E1)
                    assert L.count == L.chain.per_batch, L.count
                each_batch(dve, body)

            return L, sp_prog, pool_prog, act_prog, pe_prog, dve_prog

        def layer2():
            L = attention_plan(2, True, ["xnT", "k", "q", "v", "h0", "h1"] + [f"r{e}" for e in range(E2)] +
                               ["loss"] + ATT_TURNS + ["a", "aT"], ["out"],
                               [bank[3], bank[4]], [bank[5], bank[6], bank[7]], 10, float(HD) ** -0.5)
            s = lambda name, k, before=0: Signal(sem(f"{name}2"), k, before)
            L.bp, L.bbase = carve([1, D]), carve([1, D])
            L.base = carve([P, D])
            L.wd1 = carve([P, 2, P])
            L.bd1 = carve([P, 2])
            L.wd2 = carve([P, 2, D])
            L.bd2 = carve([P, E2])
            L.hd = carve([P, 2, T])
            L.diff = carve([P, 2, T])
            L.loss = carve([P, E2])
            L.nloss = carve([P, E2])
            L.top = carve([P, 8])
            L.idx = carve([P, 8], U32)
            L.wdown = carve([P, R2])
            L.bdown = carve([R2, 1])
            L.wup = carve([R2 + 1, D])
            L.a = carve([R2 + 1, T])
            L.chain = s("dve_chain", 19)
            L.squared = s("squared", E2, 1)
            L.chosen = s("adapter_chosen", 1)
            L.picked = s("adapter_in", 64, 1)
            L.started += [L.squared, L.picked]
            NW = 16 * 13

            def sp_prog(sp):
                L.loads = 0
                for dst, name in ((L.w["k"], "L2_attn_Wk"), (L.w["q"], "L2_attn_Wq"), (L.w["v"], "L2_attn_Wv"),
                                  (L.w["o"], "L2_attn_Wp"), (L.bq, "L2_attn_bq"), (L.bk, "L2_attn_bk"),
                                  (L.bp, "L2_attn_bp"), (L.bbase, "L2_ffn_b_base"), (L.base, "L2_ffn_W_base"),
                                  (L.wd1, "L2_ffn_Wd1"), (L.bd1, "L2_ffn_bd1"), (L.wd2, "L2_ffn_Wd2"),
                                  (L.bd2, "L2_ffn_bd2")):
                    load(sp, L, dst, a[name])
                load(sp, L, L.bv, a["L2_attn_bv"].partition_broadcast(P))

                def body(b):
                    sp_expand(sp, L, b)
                    sp.wait_ge(L.ac_full.sem, L.ac_full.at(b, 0))
                    sp.wait_ge(L.chosen.sem, L.chosen.at(b, 1))
                    settle(sp)
                    e = sp.value_load(L.idx[0:1, 0:1], min_val=0, max_val=E2 - 1)
                    for dst, src in ((L.wdown, a["L2_ffn_Wa_down"][bass.ds(e, 1), :, :]),
                                     (L.wup[0:R2, :], a["L2_ffn_Wa_up"][bass.ds(e, 1), :, :]),
                                     (L.wup[R2:R2 + 1, :], a["L2_ffn_ba_up"][bass.ds(e, 1), :, :]),
                                     (L.bdown, a["L2_ffn_ba_down"][bass.ds(e, 1), :, :])):
                        sp.dma_start(dst, src.rearrange("e p c -> (e p) c")).then_inc(L.picked.sem, 16)
                    for g in range(NG):
                        sp_max_rows(sp, L, b, g)
                each_batch(sp, body)

            def pool_prog(pool):
                pool_attention_setup(pool, L)
                pool.wait_ge(L.setup, 3)
                pool.memset(L.a[R2:R2 + 1, :], 1.0).then_inc(L.setup, 1)
                pool.wait_ge(L.setup, 4)

                def body(b):
                    pool_norm(pool, L, b)
                    pool_split_q(pool, L, b)
                each_batch(pool, body)

            def act_prog(act):
                act.wait_ge(L.weights, 16 * 14)

                def body(b):
                    act_norm(act, L, b)
                    act_split_q(act, L, b)
                    for i in range(2):
                        mi_wait(act, L, b, f"h{i}")
                        act.activation(L.hd[:, i, :], bank[0][:], ACT.Relu,
                                       bias=L.bd1[:, i:i + 1]).then_inc(L.mi_done.sem, 1)
                    for e in range(E2):
                        mi_ready(act, L, b, f"r{e}")
                        if e == 0:
                            mi_wait(act, L, b, "h1")
                        act.activation(L.diff[:, e % 2, :], L.diff[:, e % 2, :], ACT.Square,
                                       accum_out=L.loss[:, e:e + 1]).then_inc(L.squared.sem, 1)
                    for g in range(NG + 1):
                        if g >= 1:
                            for k in range(len(L.sub)):
                                act_exp(act, L, b, g - 1, k)
                        if g < NG:
                            act_max_rows(act, L, b, g)
                    mi_wait(act, L, b, "a")
                    act.activation(L.a[0:R2, :], bank[0][0:R2, :], ACT.Relu,
                                   bias=L.bdown[:, 0:1]).then_inc(L.mi_done.sem, 1)
                    act_turn_attention(act, L, b)
                each_batch(act, body)

            def pe_prog(pe):
                pe.wait_ge(L.weights, 16 * 14)
                pe.wait_ge(L.setup, 4)

                def body(b):
                    xt = xnT[b.parity]
                    pe_norm(pe, L, b)
                    pe_project(pe, L, b)
                    for i in range(2):
                        mi_take(pe, L, b, f"h{i}")
                        pe.matmul(bank[0][:], L.wd1[:, i, :], xt[:], start=True,
                                  stop=True).then_inc(L.mi_full.sem, 1)
                    for e in range(E2):
                        mi_take(pe, L, b, f"r{e}")
                        rows = slice(HID2 * (e % 4), HID2 * (e % 4 + 1))
                        pe.matmul(bank[0][:], L.wd2[rows, e // 4, :], L.hd[rows, e // 4, :], start=True,
                                  stop=True).then_inc(L.mi_full.sem, 1)
                    mi_take(pe, L, b, "loss")
                    pe.wait_ge(L.squared.sem, L.squared.at(b, E2))
                    pe.matmul(bank[0][:, 0:E2], ones[:], L.loss[:], start=True,
                              stop=True).then_inc(L.mi_full.sem, 1)
                    pe_attention(pe, L, b)
                    mi_take(pe, L, b, "a")
                    pe.wait_ge(L.picked.sem, L.picked.at(b, 64))
                    pe.matmul(bank[0][0:R2, :], L.wdown[:], xt[:], start=True,
                              stop=True).then_inc(L.mi_full.sem, 1)
                    pe_turn_attention(pe, L, b)
                    ac_take(pe, L, b, "out")
                    pe_bias(pe, L.bp)
                    mi_ready(pe, L, b, "a")
                    for t in range(NT):
                        cols = slice(t * P, (t + 1) * P)
                        pe.matmul(bank[1][:, cols], ones[0:1, :], L.bbase[:], start=False, stop=False,
                                  skip_group_check=True)
                        pe.matmul(bank[1][:, cols], xt[:, cols], L.base[:], start=False, stop=False,
                                  skip_group_check=True)
                        pe.matmul(bank[1][:, cols], L.a[:, cols], L.wup[:], start=False, stop=False,
                                  skip_group_check=True)
                    pe_out(pe, L, b).then_inc(L.ac_full.sem, 1)
                each_batch(pe, body)

            def dve_prog(dve):
                dve.wait_ge(L.weights, 16 * 14)

                def body(b):
                    L.count = 0
                    dve_norm(dve, L, b)
                    dve_split_k(dve, L, b)
                    dve_v(dve, L, b)
                    for e in range(E2):
                        mi_wait(dve, L, b, f"r{e}")
                        dve.wait_ge(L.squared.sem, L.squared.at(b, max(e - 1, 0)))
                        dve.scalar_tensor_tensor(out=L.diff[:, e % 2, :], in0=bank[0][:],
                                                 scalar=L.bd2[:, e:e + 1], in1=xnT[b.parity][:], op0=ALU.add,
                                                 op1=ALU.subtract).then_inc(L.mi_done.sem, 1)
                    mi_wait(dve, L, b, "loss")
                    dve.tensor_scalar(L.nloss[:], bank[0][:, 0:E2], -1.0, None, ALU.mult).then_inc(L.mi_done.sem, 1)
                    mi_ready(dve, L, b, "loss")
                    settle(dve)
                    link(dve, L, b, dve.max(L.top[:], L.nloss[:]))
                    dve.wait_ge(L.picked.sem, L.picked.at(b, 0))
                    settle(dve)
                    dve.max_index(L.idx[:], L.top[:], L.nloss[:]).then_inc(L.chosen.sem, 1)
                    dve_attention(dve, L, b)
                    ac_wait(dve, L, b, "out")
                    rows = x[:, bass.ds(b.index * NT, NT), :]
                    dve.tensor_tensor(rows, bank[1][:].rearrange("p (t n) -> p t n", t=NT), rows,
                                      ALU.add).then_inc(L.ac_done.sem, 1)
                    assert L.count == L.chain.per_batch, L.count
                each_batch(dve, body)

            return L, sp_prog, pool_prog, act_prog, pe_prog, dve_prog

        def layer3():
            L = attention_plan(3, False, ["xnT", "k", "q", "v", "score"] + ATT_TURNS + ["h0", "h1", "aT"],
                               ["mix", "out"], [bank[3], bank[4]], [bank[5], bank[6], bank[7]], 16, None, True)
            s = lambda name, k, before=0: Signal(sem(f"{name}3"), k, before)
            L.scale = carve([P, 1])
            L.bias = carve([P, H, HANKEL])
            L.hankel = carve([P, H, HANKEL])
            L.table = carve([H, 384])
            L.last = carve([H, 1])
            L.bp = carve([1, D])
            L.wr, L.br = carve([P, E3]), carve([P, E3])
            L.sc, L.top, L.idx = carve([P, E3]), carve([P, 8]), carve([P, 8], U32)
            L.w1, L.w2 = carve([P, TOP3, D]), carve([P, TOP3, D])
            L.b1 = [carve([P, 1]) for _ in range(TOP3)]
            L.b2 = [carve([1, D]) for _ in range(TOP3)]
            L.hT = carve([P, TOP3, T])
            L.tabled = nc.dram_tensor("bias_by_distance", [H, 384], F32, kind="Internal").ap()
            L.chain = s("dve_chain", 19)
            L.chosen = s("experts_chosen", 1)
            L.picked = s("experts_in", 16 * 4 * TOP3, 1)
            L.started += [L.picked]
            L.table_dve, L.table_dma = sem("table_dve"), sem("table_dma")
            L.bias_full, L.bias_free = sem("bias_full"), sem("bias_free")
            NW = 16 * 12

            def sp_prog(sp):
                L.loads = 0
                load(sp, L, L.table[:, 0:TABLE3], a["L3_attn_bias_table"])
                load(sp, L, L.scale, a["L3_attn_temperature"].partition_broadcast(P))
                for dst, name in ((L.w["k"], "L3_attn_Wk"), (L.w["q"], "L3_attn_Wq"), (L.w["v"], "L3_attn_Wv"),
                                  (L.w["o"], "L3_attn_Wp"), (L.bq, "L3_attn_bq"), (L.bk, "L3_attn_bk"),
                                  (L.bp, "L3_attn_bp"), (L.wr, "L3_ffn_Wr")):
                    load(sp, L, dst, a[name])
                load(sp, L, L.bv, a["L3_attn_bv"].partition_broadcast(P))
                load(sp, L, L.br, a["L3_ffn_br"].partition_broadcast(P))
                sp.wait_ge(L.table_dve, 3)
                sp.dma_start(L.tabled, L.table[:]).then_inc(L.table_dma, 16)
                sp.wait_ge(L.table_dma, 16)
                sp.dma_start(L.hankel[:], bass.AP(L.tabled.tensor, 0, [[1, P], [384, H], [1, HANKEL]])
                             ).then_inc(L.table_dma, 16)

                def body(b):
                    sp_expand(sp, L, b)
                    sp.wait_ge(L.ac_full.sem, L.ac_full.at(b, 0))
                    sp.wait_ge(L.chosen.sem, L.chosen.at(b, 1))
                    settle(sp)
                    for k in range(TOP3):
                        e = sp.value_load(L.idx[0:1, k:k + 1], min_val=0, max_val=E3 - 1)
                        for dst, src in ((L.w1[:, k, :], a["L3_ffn_W1"][bass.ds(e, 1), :, :]),
                                         (L.w2[:, k, :], a["L3_ffn_W2"][bass.ds(e, 1), :, :]),
                                         (L.b1[k], a["L3_ffn_b1"][bass.ds(e, 1), :, :]),
                                         (L.b2[k], a["L3_ffn_b2"][bass.ds(e, 1), :, :])):
                            sp.dma_start(dst, src.rearrange("e p c -> (e p) c")).then_inc(L.picked.sem, 16)
                    for g in range(NG):
                        sp_max_rows(sp, L, b, g)
                each_batch(sp, body)

            def pool_prog(pool):
                pool_attention_setup(pool, L)

                def body(b):
                    pool_norm(pool, L, b)
                    pool_split_q(pool, L, b)
                each_batch(pool, body)

            def act_prog(act):
                act.wait_ge(L.weights, NW)

                def body(b):
                    act_norm(act, L, b)
                    act_split_q(act, L, b)
                    for g in range(NG + 1):
                        if g >= 1:
                            for k in range(len(L.sub)):
                                act_exp(act, L, b, g - 1, k)
                        if g < NG:
                            act_max_rows(act, L, b, g)
                    for k in range(TOP3):
                        mi_wait(act, L, b, f"h{k}")
                        act.activation(L.hT[:, k, :], bank[0][:], ACT.Gelu,
                                       bias=L.b1[k][:, 0:1]).then_inc(L.mi_done.sem, 1)
                    act_turn_attention(act, L, b)
                each_batch(act, body)

            def pe_prog(pe):
                pe.wait_ge(L.weights, NW)
                pe.wait_ge(L.setup, 3)
                pe.wait_ge(L.table_dma, 32)
                for n in range(H // 2):
                    if n >= 1:
                        pe.wait_ge(L.bias_free, n)
                    pe.matmul(bank[1][:], flip[:], L.hankel[:, 2 * n:2 * n + 2, :].rearrange("p h i -> p (h i)"),
                              start=True, stop=True).then_inc(L.bias_full, 1)
                pe.wait_ge(L.bias_free, H // 2)

                def body(b):
                    xt = xnT[b.parity]
                    pe_norm(pe, L, b)
                    pe_project(pe, L, b)
                    mi_take(pe, L, b, "score")
                    pe.matmul(bank[0][:, 0:E3], xt[:, 0:1].to_broadcast([P, P]), L.wr[:], start=True,
                              stop=True).then_inc(L.mi_full.sem, 1)
                    pe_attention(pe, L, b)
                    pe.wait_ge(L.picked.sem, L.picked.at(b, 16 * 4 * TOP3))
                    for k in range(TOP3):
                        mi_take(pe, L, b, f"h{k}")
                        pe.matmul(bank[0][:], L.w1[:, k, :], xt[:], start=True,
                                  stop=True).then_inc(L.mi_full.sem, 1)
                    pe_turn_attention(pe, L, b)
                    ac_take(pe, L, b, "mix")
                    mi_ready(pe, L, b, f"h{TOP3 - 1}")
                    pe_bias(pe, L.b2[0])
                    for t in range(NT):
                        cols = slice(t * P, (t + 1) * P)
                        pe.matmul(bank[1][:, cols], ones[0:1, :], L.b2[1][:], start=False, stop=False,
                                  skip_group_check=True)
                        for k in range(TOP3):
                            ins = pe.matmul(bank[1][:, cols], L.hT[:, k, cols], L.w2[:, k, :], start=False,
                                            stop=(k == TOP3 - 1), skip_group_check=True)
                    ins.then_inc(L.ac_full.sem, 1)
                    ac_take(pe, L, b, "out")
                    pe_bias(pe, L.bp)
                    pe_out(pe, L, b).then_inc(L.ac_full.sem, 1)
                each_batch(pe, body)

            def dve_prog(dve):
                dve.wait_ge(L.weights, NW)
                dve.tensor_copy(L.last[:], L.table[:, TABLE3 - 1:TABLE3]).then_inc(L.table_dve, 1)
                dve.memset(L.table[:, TABLE3:384], 0.0).then_inc(L.table_dve, 1)
                dve.wait_ge(L.table_dve, 2)
                dve.tensor_scalar(L.table[:, 0:TABLE3], L.table[:, 0:TABLE3], L.last[:, 0:1], None,
                                  ALU.subtract).then_inc(L.table_dve, 1)
                dve.tensor_scalar(L.scale[:], L.scale[:], 0.1, 10.0, ALU.max, ALU.min).then_inc(L.table_dve, 1)
                dve.wait_ge(L.table_dve, 4)
                dve.tensor_scalar(L.scale[:], L.scale[:], float(np.sqrt(np.float32(D))), None,
                                  ALU.mult).then_inc(L.table_dve, 1)
                dve.wait_ge(L.table_dve, 5)
                dve.reciprocal(L.scale[:], L.scale[:]).then_inc(L.table_dve, 1)
                dve.wait_ge(L.table_dve, 6)
                for n in range(H // 2):
                    dve.wait_ge(L.bias_full, n + 1)
                    dve.tensor_copy(L.bias[:, 2 * n:2 * n + 2, :].rearrange("p h i -> p (h i)"),
                                    bank[1][:]).then_inc(L.bias_free, 1)

                def body(b):
                    L.count = 0
                    dve_norm(dve, L, b)
                    dve_split_k(dve, L, b)
                    dve_v(dve, L, b)
                    mi_wait(dve, L, b, "score")
                    dve.tensor_tensor(L.sc[:], bank[0][:, 0:E3], L.br[:], ALU.add).then_inc(L.mi_done.sem, 1)
                    mi_ready(dve, L, b, "score")
                    settle(dve)
                    link(dve, L, b, dve.max(L.top[:], L.sc[:]))
                    dve.wait_ge(L.picked.sem, L.picked.at(b, 0))
                    settle(dve)
                    dve.max_index(L.idx[:], L.top[:], L.sc[:]).then_inc(L.chosen.sem, 1)
                    dve_attention(dve, L, b)
                    rows = x[:, bass.ds(b.index * NT, NT), :]
                    ac_wait(dve, L, b, "mix")
                    dve.scalar_tensor_tensor(
                        out=acc[:], in0=bank[1][:].rearrange("p (t n) -> p t n", t=NT), scalar=1.0 / TOP3,
                        in1=rows, op0=ALU.mult, op1=ALU.add).then_inc(L.ac_done.sem, 1)
                    ac_ready(dve, L, b, "mix")
                    ac_wait(dve, L, b, "out")
                    dve.tensor_tensor(rows, bank[1][:].rearrange("p (t n) -> p t n", t=NT), acc[:],
                                      ALU.add).then_inc(L.ac_done.sem, 1)
                    assert L.count == L.chain.per_batch, L.count
                each_batch(dve, body)

            return L, sp_prog, pool_prog, act_prog, pe_prog, dve_prog

        made = {0: layer0, 1: layer1, 2: layer2, 3: layer3}
        programs = [made[i]() for i in layers]

        def finish_layer(eng, n):
            eng.drain().then_inc(layer_done, 1)
            eng.wait_ge(layer_done, 5 * (n + 1))

        block = stack.enter_context(nc.Block())

        @block.sync
        def _(sp):
            for dst, name in ((ident, "const_ident"), (flip, "const_flip"), (mask_f, "const_keep"),
                              (iota16, "const_iota"), (mask_qf, "const_mask")):
                sp.dma_start(dst[:], a[name]).then_inc(consts_loaded, 16)
            sp.dma_start(x[:], a["L0_attn_x"].rearrange("b (t p) d -> p (b t) d", p=P)).then_inc(x_loaded, 16)
            for n, (_, sp_prog, *_rest) in enumerate(programs):
                sp_prog(sp)
                finish_layer(sp, n)
            sp.dma_start(out.rearrange("b (t p) d -> p (b t) d", p=P), x[:]).then_inc(out_stored, 16)
            sp.wait_ge(out_stored, 16)

        @block.gpsimd
        def _(pool):
            for L, *_rest in programs:
                for signal in L.init + L.started + [L.mi_done, L.ac_done]:
                    pool.sem_inc(signal.sem, signal.before)
            pool.memset(ones[:], 1.0).then_inc(ones_set, 1)
            pool.memset(mhalf[:], -0.5).then_inc(ones_set, 1)
            pool.wait_ge(ones_set, 2)
            for n, (_, _, pool_prog, *_rest) in enumerate(programs):
                pool_prog(pool)
                finish_layer(pool, n)

        @block.scalar
        def _(act):
            for n, (_, _, _, act_prog, *_rest) in enumerate(programs):
                act_prog(act)
                finish_layer(act, n)

        @block.tensor
        def _(pe):
            pe.wait_ge(consts_loaded, 16 * 5)
            pe.wait_ge(consts_cast, 3)
            pe.wait_ge(ones_set, 1)
            for n, (_, _, _, _, pe_prog, _dve) in enumerate(programs):
                pe_prog(pe)
                finish_layer(pe, n)

        @block.vector
        def _(dve):
            dve.wait_ge(consts_loaded, 16 * 5)
            dve.tensor_copy(identb[:], ident[:]).then_inc(consts_cast, 1)
            dve.tensor_copy(mask_q[:], mask_qf[:, 0, :]).then_inc(consts_cast, 1)
            dve.tensor_copy(mask_k[:], mask_qf[:, 1, :]).then_inc(consts_cast, 1)
            dve.wait_ge(x_loaded, 16)
            for n, (*_rest, dve_prog) in enumerate(programs):
                dve_prog(dve)
                finish_layer(dve, n)


def _layouts(v):
    c = np.ascontiguousarray
    out = {"L0_attn_x": v["L0_attn_x"]}
    for k in ("q", "k", "v", "o"):
        out[f"L0_attn_W{k}"] = c(v[f"L0_attn_W{k}"].T)
    for k in ("q", "k"):
        out[f"L0_attn_b{k}"] = v[f"L0_attn_b{k}"].reshape(D, 1)
        out[f"L3_attn_b{k}"] = v[f"L3_attn_b{k}"].reshape(D, 1)
    out["L0_attn_bo"] = v["L0_attn_bo"].reshape(1, D)
    for name in ("L0_attn_bv", "L0_ffn_rb", "L1_attn_decay_log", "L1_ffn_router_b", "L3_attn_bv", "L3_ffn_br",
                 "L3_attn_temperature"):
        out[name] = v[name]
    out["L0_ffn_keys"] = c(v["L0_ffn_keys"].T)
    out["L0_ffn_rw"] = c(v["L0_ffn_rw"].T)
    out["L0_ffn_w1"] = c(v["L0_ffn_w1"].transpose(2, 0, 1))
    out["L0_ffn_w2"] = c(v["L0_ffn_w2"].transpose(2, 0, 1).reshape(4, P, E0, D).transpose(1, 2, 0, 3))
    out["L0_ffn_b1"] = c(v["L0_ffn_b1"].reshape(E0, 4, P).transpose(2, 0, 1).reshape(P, E0 * 4))
    out["L0_ffn_b2"] = v["L0_ffn_b2"]
    for name in ("W_Q", "W_K", "W_V", "W_g_w"):
        out[f"L1_attn_{name}"] = c(v[f"L1_attn_{name}"].T)
    out["L1_attn_W_g_b"] = v["L1_attn_W_g_b"].reshape(1, H1 * DK1)
    out["L1_attn_W_O"] = c(v["L1_attn_W_O"].T.reshape(4, P, D).transpose(1, 0, 2))
    out["L1_ffn_router_w"] = v["L1_ffn_router_w"]
    out["L1_ffn_w1"] = c(v["L1_ffn_w1"].transpose(1, 0, 2))
    out["L1_ffn_w2"] = c(v["L1_ffn_w2"].reshape(E1, 4, P, D).transpose(2, 0, 1, 3))
    w = v["L2_attn_W1"].reshape(D, H, 3, HD)
    bb = v["L2_attn_b1"].reshape(H, 3, HD)
    for i, k in enumerate("qkv"):
        out[f"L2_attn_W{k}"] = c(w[:, :, i, :].reshape(D, D))
        out[f"L2_attn_b{k}"] = c(bb[:, i, :].reshape(D, 1))
    out["L2_attn_bv"] = out["L2_attn_bv"].reshape(D)
    out["L2_attn_Wp"] = v["L2_attn_Wp"]
    out["L2_attn_bp"] = v["L2_attn_bp"].reshape(1, D)
    out["L2_ffn_W_base"] = v["L2_ffn_W_base"]
    out["L2_ffn_b_base"] = v["L2_ffn_b_base"].reshape(1, D)
    out["L2_ffn_Wd1"] = c(v["L2_ffn_Wd1"].transpose(1, 0, 2).reshape(D, 2, P))
    out["L2_ffn_bd1"] = c(v["L2_ffn_bd1"].reshape(2, P).T)
    out["L2_ffn_Wd2"] = c(v["L2_ffn_Wd2"].reshape(2, P, D).transpose(1, 0, 2))
    out["L2_ffn_bd2"] = c(v["L2_ffn_bd2"].T)
    out["L2_ffn_Wa_down"], out["L2_ffn_Wa_up"] = v["L2_ffn_Wa_down"], v["L2_ffn_Wa_up"]
    out["L2_ffn_ba_down"] = v["L2_ffn_ba_down"].reshape(E2, R2, 1)
    out["L2_ffn_ba_up"] = v["L2_ffn_ba_up"].reshape(E2, 1, D)
    for name in ("L3_attn_Wq", "L3_attn_Wk", "L3_attn_Wv", "L3_attn_Wp", "L3_ffn_Wr", "L3_ffn_W1", "L3_ffn_W2"):
        out[name] = v[name]
    out["L3_attn_bp"] = v["L3_attn_bp"].reshape(1, D)
    out["L3_attn_bias_table"] = c(v["L3_attn_bias_table"].T)
    out["L3_ffn_b1"] = v["L3_ffn_b1"].reshape(E3, D, 1)
    out["L3_ffn_b2"] = v["L3_ffn_b2"].reshape(E3, 1, D)
    p, f = np.arange(P)[:, None], np.arange(P)[None, :]
    out["const_ident"] = np.eye(P, dtype=np.float32)
    out["const_flip"] = c(np.eye(P, dtype=np.float32)[::-1])
    out["const_keep"] = (f >= p).astype(np.float32)
    out["const_iota"] = np.tile(np.arange(16, dtype=np.float32), (P, 1))
    out["const_mask"] = c(np.stack([(f > p), (p > f)], 1).astype(np.float32) * np.float32(-3e38))
    out["const_dist"] = np.maximum(np.arange(T)[None, :] - p, 0).astype(np.float32)
    return {k: c(z) for k, z in out.items()}


def kernel(**inputs):
    import concourse.bacc as bacc
    from concourse.bass_utils import run_bass_kernel_spmd

    arrays = _layouts({k: np.asarray(z) for k, z in inputs.items()})
    nc = bacc.Bacc("TRN2", target_bir_lowering=False, num_devices=1)
    a = {k: nc.dram_tensor(f"in_{k}", list(z.shape), F32, kind="ExternalInput").ap() for k, z in arrays.items()}
    out = nc.dram_tensor("out", [NBATCH, T, D], F32, kind="ExternalOutput").ap()
    build(nc, a, out)
    r = run_bass_kernel_spmd(nc, [{f"in_{k}": z for k, z in arrays.items()}], core_ids=[0])
    return r.results[0]["out"]
```

```python
from contextlib import ExitStack

import numpy as np

import concourse.bass as bass
from concourse import mybir

ALU = mybir.AluOpType
ACT = mybir.ActivationFunctionType
AX = mybir.AxisListType
F32 = mybir.dt.float32
BF16 = mybir.dt.bfloat16
U32 = mybir.dt.uint32

P = 128
NBATCH, T, D = 8, 512, 128
NT = T // P
H, HD = 16, 8
HG = 4
NG = H // HG
VW = 32
NPART = 3
KROWS = NPART * NPART * HD
KAUG = KROWS + NPART
LN_EPS = 1e-05
E0, F0, TOP0 = 16, 512, 4
E1, F1 = 8, 512
H1, DK1, EPS1 = 8, 64, 1e-06
V1W = DK1 + 1
E2, R2, HID2 = 8, 64, 32
E3, TOP3 = 8, 2
TABLE3 = 249
HANKEL = 256
NHALF = 2
HEADS_UNIT = 3
FIRST_UNIT = 4
LAG = 4


class Batch:

    def __init__(self, pair, half):
        self.pair, self.half = pair, half

    @property
    def index(self):
        return self.pair * NHALF + self.half

    @property
    def parity(self):
        return self.half % 2

    def following(self):
        return Batch(self.pair, self.half + 1)


class Signal:

    def __init__(self, sem, per_batch, before=0):
        self.sem, self.per_batch, self.before = sem, per_batch, before

    def at(self, b, n):
        return b.pair * (NHALF * self.per_batch) + (b.half * self.per_batch + n + self.before)


class Turns:

    def __init__(self, bank, names, full, done):
        self.bank, self.names, self.full, self.done = bank, names, full, done

    def number(self, name):
        return self.names.index(name)


def causal_score_blocks():
    w = [T - P * k for k in range(NT)]
    first = [[(j, 0, 0)] for j in range(HG)]
    second = [[(j, 1, 0), (j, 3, w[1])] for j in range(HG)]
    third = [[(2 * i, 2, 0), (2 * i + 1, 2, w[2])] for i in range(HG // 2)]
    return [first, second, third]


def full_score_blocks():
    return [[[(j, k, 0)] for j in range(HG)] for k in range(NT)]


def causal_max_slots():
    out = [(0, [0, 1, 2, 3]), (1, [0, 1]), (1, [2, 3])]
    return out + [(q, [j]) for q in (2, 3) for j in range(HG)]


def full_max_slots():
    return [(q, [j]) for q in range(NT) for j in range(HG)]


def build(nc, a, out, layers=(0, 1, 2, 3)):
    stack = ExitStack()
    with stack:
        def sb(name, shape, dt=F32):
            return stack.enter_context(nc.sbuf_tensor(name, shape, dt))

        def sem(name):
            return stack.enter_context(nc.semaphore(name))

        bank = [stack.enter_context(nc.psum_tensor(f"bank{i}", [P, 512], F32)) for i in range(8)]

        x = sb("x", [P, NBATCH * NT, D])
        ident = sb("ident", [P, P])
        flip = sb("flip", [P, P])
        identb = sb("identb", [P, P], BF16)
        mask_q = sb("mask_q", [P, P], BF16)
        mask_k = sb("mask_k", [P, P], BF16)
        mask_f = sb("mask_f", [P, P])
        mask_qf = sb("mask_qf", [P, 2, P])
        iota16 = sb("iota16", [P, 16])
        ones = sb("ones", [P, P])
        mhalf = sb("mhalf", [P, NT])
        mean_var = sb("mean_var", [P, NT, 2])
        stats = sb("stats", [P, NT, 6])
        rstd = sb("rstd", [P, NT])
        xn = sb("xn", [P, NT, D])
        xnT = [sb(f"xnT{i}", [P, T]) for i in range(2)]
        acc = sb("acc", [P, NT, D])

        ARENA = 44544
        arena = sb("arena", [P, ARENA])
        used = [0]

        def carve(shape, dt=F32):
            per = 4 if dt in (F32, U32) else 2
            n = int(np.prod(shape[1:]))
            words = (n * per + 31) // 32 * 8
            lo = used[0]
            used[0] += words
            assert used[0] <= ARENA, used[0]
            flat = arena[0:shape[0], lo:lo + (n * per + 3) // 4]
            if dt != F32:
                flat = flat.bitcast(dt)
            if len(shape) == 2:
                return flat
            names = "abcd"[:len(shape) - 1]
            return flat.rearrange(f"p ({' '.join(names)}) -> p {' '.join(names)}",
                                  **{k: s for k, s in zip(names[1:], shape[2:])})

        x_loaded = sem("x_loaded")
        consts_cast = sem("consts_cast")
        consts_loaded = sem("consts_loaded")
        ones_set = sem("ones_set")
        layer_done = sem("layer_done")
        passed = sem("passed")
        out_stored = sem("out_stored")

        class Layer:
            pass

        def attention_plan(n, causal, early, late, mx_banks, st_banks, p_ring, scale, biased=False, copies=1):
            L = Layer()
            L.n, L.causal, L.biased, L.scale = n, causal, biased, scale
            L.sub = causal_score_blocks() if causal else full_score_blocks()
            L.slots = sum(len(s) for s in L.sub)
            L.blocks = [blocks for step in L.sub for blocks in step]
            L.own_pe, L.own_act, L.own_dve = {}, {}, {}
            L.maxes = causal_max_slots() if causal else full_max_slots()
            L.mturns = len(L.maxes) + 1
            L.MX, L.ST = mx_banks, st_banks
            L.PR = p_ring
            L.copies = copies
            L.lead = len(mx_banks) * 2
            used[0] = 0
            L.w = {k: carve([P, D]) for k in ("q", "k", "v", "o")}
            L.bq, L.bk = carve([P, 1]), carve([P, 1])
            L.bv = carve([P, D])
            L.Qx = [carve([P, H, T], BF16) for _ in range(copies)]
            L.Kx = [carve([P, H, T], BF16) for _ in range(copies)]
            L.probs = carve([P, p_ring, T])
            L.Vx = [carve([P, NT, H, VW]) for _ in range(copies)]
            L.qf = carve([P, T])
            L.qs = carve([P, NPART, T], BF16)
            L.kr = carve([P, T])
            L.ks = carve([P, NPART, T], BF16)
            L.mx = carve([P, 2, NT, HG])
            L.mr = carve([P, NT, HG])
            L.nm = carve([P, 2, NT, NPART, HG], BF16)
            L.nmT = carve([NPART * HG, 2, T], BF16)
            L.oT = carve([P, T])
            L.rec = carve([P, NT, HG])
            L.att = carve([P, NT, D])
            L.attT = carve([P, T])
            L.qd = nc.dram_tensor(f"q_parts{n}", [H, HD, NPART, T], BF16, kind="Internal").ap()
            L.kd = nc.dram_tensor(f"k_parts{n}", [H, HD, NPART, T], BF16, kind="Internal").ap()
            common_signals(L, n, early, late)
            s = lambda name, k, before=0: Signal(sem(f"{name}{n}"), k, before)
            L.q1 = s("q_float", 1)
            L.qsplit = s("q_split", 3, 1)
            L.ksplit = s("k_split", 1)
            L.stored = s("parts_stored", 32, 1)
            L.kx = s("k_expanded", 16 * NPART * NPART, 1)
            L.qx = s("q_expanded", 16 * NPART * NPART, 1)
            L.nmrow = s("max_rows_in", 16 * NPART * NG, 1)
            L.mx_full = s("max_scores_full", NG * L.mturns)
            L.mx_free = s("max_scores_free", NG * L.mturns, len(mx_banks))
            L.st_full = s("scores_full", NG * L.slots, 1)
            L.st_free = s("scores_free", NG * L.slots, len(st_banks))
            L.p_free = s("probs_free", NG * L.slots, p_ring)
            L.nm_ready = s("max_parts_ready", NG)
            L.po_free = s("attended_free", NG, 1)
            L.started += [L.qsplit, L.stored, L.kx, L.qx, L.nmrow, L.st_full]
            L.init = [L.mx_free, L.st_free, L.p_free, L.po_free]
            assert (NG * L.slots) % p_ring == 0
            return L

        def common_signals(L, n, early, late):
            s = lambda name, k, before=0: Signal(sem(f"{name}{n}"), k, before)
            L.weights = sem(f"weights{n}")
            L.setup = sem(f"setup{n}")
            L.early = Turns(bank[0], early, s("early_full", len(early), 1), s("early_done", len(early), 1))
            L.late = Turns(bank[1], late, s("late_full", len(late), 1), s("late_done", len(late), 1))
            L.stat = s("ln_stats", 2 * NT)
            L.rs = s("ln_rstd", 2)
            L.xn_ready = s("xn_ready", 1, 1)
            L.started = [L.xn_ready] + [x for t in (L.early, L.late) for x in (t.full, t.done)]

        def turns(L, name):
            return L.early if name in L.early.names else L.late

        def take(pe, L, b, name):
            t = turns(L, name)
            pe.wait_ge(t.done.sem, t.done.at(b, t.number(name)))
            return t.bank

        def fill(L, name, ins):
            ins.then_inc(turns(L, name).full.sem, 1)

        def there(eng, L, b, name):
            t = turns(L, name)
            eng.wait_ge(t.full.sem, t.full.at(b, t.number(name) + 1))
            return t.bank

        def emptied(L, name, ins):
            ins.then_inc(turns(L, name).done.sem, 1)

        def ready(eng, L, b, name):
            t = turns(L, name)
            eng.wait_ge(t.done.sem, t.done.at(b, t.number(name) + 1))

        def chain_value(L):
            if L.trip is None:
                return L.count
            return L.chain.at(L.trip, L.count)

        def mark(L, ins):
            L.count += 1
            ins.then_inc(L.chain.sem, 1)

        def catch(dve, L):
            dve.wait_ge(L.chain.sem, chain_value(L))

        def link(dve, L, ins):
            mark(L, ins)
            catch(dve, L)

        def settle(eng):
            eng.sem_inc(passed, 1)

        def dve_norm(dve, L, b):
            for t in range(NT):
                dve.bn_stats(stats[:, t, :], x[:, b.index * NT + t, :]).then_inc(L.stat.sem, 1)
            dve.wait_ge(L.stat.sem, L.stat.at(b, NT))
            settle(dve)
            for t in range(NT):
                dve.bn_aggr(mean_var[:, t, :], stats[:, t, :]).then_inc(L.stat.sem, 1)
            dve.wait_ge(L.rs.sem, L.rs.at(b, 2))
            dve.wait_ge(L.stat.sem, L.stat.at(b, 2 * NT))
            dve.wait_ge(L.early.full.sem, L.early.full.at(b, 0))
            for t in range(NT):
                ins = dve.tensor_scalar(xn[:, t, :], x[:, b.index * NT + t, :], mean_var[:, t, 0:1],
                                        rstd[:, t:t + 1], ALU.subtract, ALU.mult)
            ins.then_inc(L.xn_ready.sem, 1)

        def pool_norm(pool, L, b):
            pool.wait_ge(L.stat.sem, L.stat.at(b, 2 * NT))
            pool.wait_ge(L.xn_ready.sem, L.xn_ready.at(b, 0))
            settle(pool)
            pool.tensor_scalar(rstd[:], mean_var[:, :, 1], LN_EPS, None, ALU.add).then_inc(L.rs.sem, 1)
            pool.wait_ge(L.rs.sem, L.rs.at(b, 1))
            pool.tensor_tensor(rstd[:], rstd[:], mhalf[:], ALU.pow).then_inc(L.rs.sem, 1)

        def pe_norm(pe, L, b):
            bk = take(pe, L, b, "xnT")
            pe.wait_ge(L.xn_ready.sem, L.xn_ready.at(b, 1))
            for t in range(NT):
                ins = pe.transpose(bk[:, t * P:(t + 1) * P], xn[:, t, :], ident[:])
            fill(L, "xnT", ins)

        def act_norm(act, L, b):
            bk = there(act, L, b, "xnT")
            emptied(L, "xnT", act.copy(xnT[b.parity][:], bk[:]))

        def pe_project(pe, L, b, t):
            xt = xnT[b.parity]
            if t == "k":
                ready(pe, L, b, "xnT")
            bk = take(pe, L, b, t)
            if t == "v":
                for n in range(NT):
                    ins = pe.matmul(bk[:, n * P:(n + 1) * P], xt[:, n * P:(n + 1) * P], L.w["v"][:],
                                    start=True, stop=True)
            else:
                ins = pe.matmul(bk[:], L.w[t][:], xt[:], start=True, stop=True)
            fill(L, t, ins)

        def dve_split_k(dve, L, b):
            bk = there(dve, L, b, "k")
            dve.wait_ge(L.stored.sem, L.stored.at(b, 0))
            link(dve, L, dve.tensor_scalar(L.ks[:, 0, :], bk[:], L.bk[:, 0:1], None, ALU.add))
            emptied(L, "k", dve.scalar_tensor_tensor(out=L.kr[:], in0=bk[:], scalar=L.bk[:, 0:1],
                                                     in1=L.ks[:, 0, :], op0=ALU.add, op1=ALU.subtract))
            ready(dve, L, b, "k")
            link(dve, L, dve.tensor_copy(L.ks[:, 1, :], L.kr[:]))
            dve.tensor_tensor(L.ks[:, 2, :], L.kr[:], L.ks[:, 1, :], ALU.subtract).then_inc(L.ksplit.sem, 1)

        def act_split_q(act, L, b):
            bk = there(act, L, b, "q")
            act.wait_ge(L.qsplit.sem, L.qsplit.at(b, 0))
            act.activation(L.qf[:], bk[:], ACT.Identity, bias=L.bq[:, 0:1]).then_inc(L.q1.sem, 1)
            act.wait_ge(L.stored.sem, L.stored.at(b, 0))
            emptied(L, "q", act.activation(L.qs[:, 0, :], bk[:], ACT.Identity, bias=L.bq[:, 0:1]))

        def pool_split_q(pool, L, b):
            s = L.qsplit
            pool.wait_ge(L.q1.sem, L.q1.at(b, 1))
            ready(pool, L, b, "q")
            pool.tensor_tensor(L.qf[:], L.qf[:], L.qs[:, 0, :], ALU.subtract).then_inc(s.sem, 1)
            pool.wait_ge(s.sem, s.at(b, 1))
            settle(pool)
            pool.tensor_copy(L.qs[:, 1, :], L.qf[:]).then_inc(s.sem, 1)
            pool.wait_ge(s.sem, s.at(b, 2))
            pool.tensor_tensor(L.qs[:, 2, :], L.qf[:], L.qs[:, 1, :], ALU.subtract).then_inc(s.sem, 1)

        def dve_v(dve, L, b):
            bk = there(dve, L, b, "v")
            emptied(L, "v", dve.tensor_tensor(
                copy_of(L.Vx, b)[:, :, :, 0:HD], bk[:].rearrange("p (t h d) -> p t h d", t=NT, d=HD),
                L.bv[:].rearrange("p (o h d) -> p o h d", o=1, d=HD).to_broadcast([P, NT, H, HD]), ALU.add))

        def copy_of(buffers, b):
            return buffers[b.parity % len(buffers)]

        def sp_expand(sp, L, b, first=False):
            sp.wait_ge(L.kx.sem, L.kx.at(b, 0))
            sp.wait_ge(L.qx.sem, L.qx.at(b, 0))
            settle(sp)
            sp.wait_ge(L.ksplit.sem, L.ksplit.at(b, 1))
            sp.dma_start(L.kd.rearrange("h d i t -> (h d) i t"), L.ks[:]).then_inc(L.stored.sem, 16)
            sp.wait_ge(L.qsplit.sem, L.qsplit.at(b, 3))
            sp.dma_start(L.qd.rearrange("h d i t -> (h d) i t"), L.qs[:]).then_inc(L.stored.sem, 16)
            sp.wait_ge(L.stored.sem, L.stored.at(b, 32))
            settle(sp)
            if not first:
                sp.wait_ge(L.st_full.sem, L.st_full.at(b, -(L.copies - 1) * L.st_full.per_batch))
            for j in range(NPART):
                for i in range(NPART):
                    r = (j * NPART + i) * HD
                    src = L.kd[:, :, j, :].rearrange("h d t -> d h t")
                    sp.dma_start(copy_of(L.Kx, b)[r:r + HD, :, :], src).then_inc(L.kx.sem, 16)
            for j in range(NPART):
                for i in range(NPART):
                    r = (j * NPART + i) * HD
                    src = L.qd[:, :, i, :].rearrange("h d t -> d h t")
                    sp.dma_start(copy_of(L.Qx, b)[r:r + HD, :, :], src).then_inc(L.qx.sem, 16)

        def sp_max_rows(sp, L, b, g):
            sp.wait_ge(L.mx_free.sem, L.mx_free.at(b, (g + 1) * L.mturns))
            for i in range(NPART):
                sp.dma_start(copy_of(L.Qx, b)[KROWS + i:KROWS + i + 1, g * HG:(g + 1) * HG, :],
                             L.nmT[i * HG:(i + 1) * HG, g % 2, :]).then_inc(L.nmrow.sem, 16)

        def pe_max(pe, L, b, g, i):
            if g == 0 and i == 0:
                pe.wait_ge(L.kx.sem, L.kx.at(b, L.kx.per_batch))
                pe.wait_ge(L.qx.sem, L.qx.at(b, L.qx.per_batch))
            Qx, Kx = copy_of(L.Qx, b), copy_of(L.Kx, b)
            n = g * L.mturns + i
            q, heads = L.maxes[i]
            w = (q + 1) * P if L.causal else T
            mx = L.MX[n % len(L.MX)]
            pe.wait_ge(L.mx_free.sem, L.mx_free.at(b, n + 1 - len(L.MX)))
            for k, j in enumerate(heads):
                h = g * HG + j
                far = L.biased and q < 2
                ins = pe.matmul(mx[:, k * w:(k + 1) * w], Qx[0:KROWS, h, q * P:(q + 1) * P],
                                Kx[0:KROWS, h, 0:w], start=True, stop=not (L.causal or far))
                if L.causal:
                    ins = pe.matmul(mx[:, k * w + q * P:k * w + (q + 1) * P], identb[:], mask_q[:],
                                    start=False, stop=True)
                if far and q == 0:
                    pe.matmul(mx[:, 2 * P:3 * P], L.bias[:, h, P:2 * P], ident[:],
                              start=False, stop=False)
                    ins = pe.matmul(mx[:, 3 * P:4 * P], L.bias[:, h, 0:P], ident[:],
                                    start=False, stop=True)
                if far and q == 1:
                    ins = pe.matmul(mx[:, 3 * P:4 * P], L.bias[:, h, P:2 * P], ident[:],
                                    start=False, stop=True)
            ins.then_inc(L.mx_full.sem, 1)

        def dve_max(dve, L, b, g, i):
            n = g * L.mturns + i
            q, heads = L.maxes[i]
            w = (q + 1) * P if L.causal else T
            mx = L.MX[n % len(L.MX)]
            dve.wait_ge(L.mx_full.sem, L.mx_full.at(b, n + 1))
            dve.reduce_max(L.mx[:, g % 2, q, heads[0]:heads[-1] + 1],
                           mx[:, 0:w * len(heads)].rearrange("p (j k) -> p j k", k=w),
                           AX.X).then_inc(L.mx_free.sem, 1)
            if i < len(L.maxes) - 1:
                return
            dve.wait_ge(L.mx_free.sem, L.mx_free.at(b, n + 1))
            m, nm = L.mx[:, g % 2], L.nm[:, g % 2]
            link(dve, L, dve.tensor_scalar(nm[:, :, 0, :], m, -1.0, None, ALU.mult))
            link(dve, L, dve.scalar_tensor_tensor(out=L.mr[:], in0=m, scalar=-1.0, in1=nm[:, :, 0, :],
                                                  op0=ALU.mult, op1=ALU.subtract))
            link(dve, L, dve.tensor_copy(nm[:, :, 1, :], L.mr[:]))
            dve.tensor_tensor(nm[:, :, 2, :], L.mr[:], nm[:, :, 1, :],
                              ALU.subtract).then_inc(L.nm_ready.sem, 1)

        def max_rows_view(L, g):
            n = g * L.mturns + L.mturns - 1
            return n, L.MX[n % len(L.MX)][0:NPART * HG, 0:T // 2].bitcast(BF16)

        def pe_max_rows(pe, L, b, g):
            n, view = max_rows_view(L, g)
            pe.wait_ge(L.mx_free.sem, L.mx_free.at(b, n + 1 - len(L.MX)))
            pe.wait_ge(L.nm_ready.sem, L.nm_ready.at(b, g + 1))
            for t in range(NT):
                ins = pe.transpose(view[:, t * P:(t + 1) * P],
                                   L.nm[:, g % 2, t, :, :].rearrange("p i j -> p (i j)"), identb[:])
            ins.then_inc(L.mx_full.sem, 1)

        def dve_max_rows(dve, L, b, g):
            n, view = max_rows_view(L, g)
            dve.wait_ge(L.mx_full.sem, L.mx_full.at(b, n + 1))
            dve.wait_ge(L.nmrow.sem, L.nmrow.at(b, 16 * NPART * max(g - 1, 0)))
            dve.tensor_copy(L.nmT[:, g % 2, :], view).then_inc(L.mx_free.sem, 1)

        def pe_scores(pe, L, b, g, i):
            Qx, Kx = copy_of(L.Qx, b), copy_of(L.Kx, b)
            if i == 0:
                pe.wait_ge(L.nmrow.sem, L.nmrow.at(b, 16 * NPART * (g + 1)))
            n = g * L.slots + i
            st = L.ST[n % len(L.ST)]
            pe.wait_ge(L.st_free.sem, L.st_free.at(b, n + 1 - len(L.ST)))
            for j, kb, c in L.blocks[i]:
                h = g * HG + j
                w = T - kb * P if L.causal else T
                far = L.biased and kb >= 2
                ins = pe.matmul(st[:, c:c + w], Kx[0:KAUG, h, kb * P:(kb + 1) * P],
                                Qx[0:KAUG, h, T - w:T], start=True, stop=not (L.causal or far))
                if L.causal:
                    ins = pe.matmul(st[:, c:c + P], identb[:], mask_k[:], start=False, stop=True)
                if far and kb == 2:
                    ins = pe.matmul(st[:, 0:P], ident[:], L.bias[:, h, P:2 * P],
                                    start=False, stop=True)
                if far and kb == 3:
                    ins = pe.matmul(st[:, 0:2 * P], ident[:], L.bias[:, h, 0:2 * P],
                                    start=False, stop=True)
            ins.then_inc(L.st_full.sem, 1)

        def act_exp(act, L, b, g, i):
            n = g * L.slots + i
            st = L.ST[n % len(L.ST)]
            w = sum(T - kb * P if L.causal else T for _, kb, _ in L.blocks[i])
            act.wait_ge(L.st_full.sem, L.st_full.at(b, n + 1))
            act.wait_ge(L.p_free.sem, L.p_free.at(b, n + 1 - L.PR))
            act.activation(L.probs[:, n % L.PR, 0:w], st[:, 0:w], ACT.Exp,
                           scale=L.scale).then_inc(L.st_free.sem, 1)

        def pe_attend(pe, L, b, g, k):
            n = g * L.slots + sum(len(s) for s in L.sub[:k])
            m = len(L.sub[k])
            if k == 0:
                pe.wait_ge(L.po_free.sem, L.po_free.at(b, g))
                if g == 0:
                    ready(pe, L, b, "v")
            pe.wait_ge(L.st_free.sem, L.st_free.at(b, n + m))
            pieces = sorted((kb, j, i, c) for i, blocks in enumerate(L.sub[k]) for j, kb, c in blocks)
            for kb, j, i, c in pieces:
                w = T - kb * P if L.causal else T
                ins = pe.matmul(bank[2][j * VW:(j + 1) * VW, T - w:T], copy_of(L.Vx, b)[:, kb, g * HG + j, :],
                                L.probs[:, (n + i) % L.PR, c:c + w], start=(kb == 0),
                                stop=(k == len(L.sub) - 1), skip_group_check=True)
            ins.then_inc(L.p_free.sem, m)

        def dve_attended(dve, L, b, g):
            dve.wait_ge(L.p_free.sem, L.p_free.at(b, (g + 1) * L.slots))
            dve.tensor_copy(L.oT[:], bank[2][:]).then_inc(L.po_free.sem, 1)

        def pe_attended(pe, L, b, g):
            bk = take(pe, L, b, f"pt{g}")
            pe.wait_ge(L.po_free.sem, L.po_free.at(b, g + 1))
            for t in range(NT):
                ins = pe.transpose(bk[:, t * P:(t + 1) * P], L.oT[:, t * P:(t + 1) * P], ident[:])
            fill(L, f"pt{g}", ins)

        def dve_divide(dve, L, b, g):
            bk = there(dve, L, b, f"pt{g}")
            view = bk[:].rearrange("p (t j c) -> p t j c", t=NT, c=VW)
            link(dve, L, dve.reciprocal(L.rec[:], view[:, :, :, HD]))
            emptied(L, f"pt{g}", dve.tensor_tensor(
                L.att[:, :, g * HG * HD:(g + 1) * HG * HD].rearrange("p t (j d) -> p t j d", d=HD),
                view[:, :, :, 0:HD], L.rec[:].unsqueeze(3).to_broadcast([P, NT, HG, HD]), ALU.mult))

        def pe_turn_attention(pe, L, b):
            bk = take(pe, L, b, "aT")
            ready(pe, L, b, "pt3")
            for t in range(NT):
                ins = pe.transpose(bk[:, t * P:(t + 1) * P], L.att[:, t, :], ident[:])
            fill(L, "aT", ins)

        def act_turn_attention(act, L, b):
            bk = there(act, L, b, "aT")
            emptied(L, "aT", act.copy(L.attT[:], bk[:]))

        def pe_out(pe, L, b):
            ready(pe, L, b, "aT")
            for t in range(NT):
                ins = pe.matmul(bank[1][:, t * P:(t + 1) * P], L.attT[:, t * P:(t + 1) * P], L.w["o"][:],
                                start=False, stop=True, skip_group_check=True)
            return ins

        def group_steps(L, s, wrap=False):
            m, S = [], []
            if s < NG or wrap:
                m = [("max", s % NG, i, s == NG) for i in range(len(L.maxes))]
            if s >= 1:
                S = [("score", s - 1, i, False) for i in range(L.slots)]
            lead = min(L.lead, len(m))
            steps, m = m[:lead], m[lead:]
            if s >= 2:
                steps.append(("turn", s - 2, 0, False))
            ends = {}
            n = 0
            for k, sub in enumerate(L.sub if S else []):
                n += len(sub)
                ends.setdefault(min(n - 1 + LAG, L.slots - 1), []).append(("attend", s - 1, k, False))
            for i in range(max(len(S), len(m))):
                if i < len(S):
                    steps.append(S[i])
                if i < len(m):
                    steps.append(m[i])
                steps += ends.get(i, [])
            if S:
                steps.append(("attended", s - 1, 0, False))
            if s < NG or wrap:
                steps.append(("max_rows", s % NG, 0, s == NG))
            return steps

        def pe_step(pe, L, b, what, g, i):
            if what == "max":
                pe_max(pe, L, b, g, i)
            elif what == "max_rows":
                pe_max_rows(pe, L, b, g)
            elif what == "score":
                pe_scores(pe, L, b, g, i)
            elif what == "attend":
                pe_attend(pe, L, b, g, i)
            elif what == "turn":
                pe_attended(pe, L, b, g)
            elif what == "norm":
                pe_norm(pe, L, b)
            elif what in ("k", "q", "v"):
                pe_project(pe, L, b, what)
            elif what in L.own_pe:
                L.own_pe[what](pe, L, b, i)

        def act_step(act, L, b, what, g, i):
            if what == "score":
                act_exp(act, L, b, g, i)
            elif what == "norm":
                act_norm(act, L, b)
            elif what == "q":
                act_split_q(act, L, b)
            elif what in L.own_act:
                L.own_act[what](act, L, b, i)

        def dve_step(dve, L, b, what, g, i):
            if what == "max":
                dve_max(dve, L, b, g, i)
            elif what == "max_rows":
                dve_max_rows(dve, L, b, g)
            elif what == "attended":
                dve_attended(dve, L, b, g)
            elif what == "turn":
                dve_divide(dve, L, b, g)
            elif what == "center":
                dve_norm(dve, L, b)
            elif what == "k":
                dve_split_k(dve, L, b)
            elif what == "v":
                dve_v(dve, L, b)
            elif what in L.own_dve:
                L.own_dve[what](dve, L, b, i)

        def take_steps(step, eng, L, b, steps):
            for what, g, i, later in steps:
                step(eng, L, b.following() if later else b, what, g, i)

        def pool_attention_setup(pool, L):
            for c in range(L.copies):
                pool.memset(L.Kx[c][64:96, :, :], 1.0).then_inc(L.setup, 1)
                pool.wait_ge(L.setup, 3 * c + 1)
                pool.memset(L.Vx[c][:, :, :, HD:VW], 0.0).then_inc(L.setup, 1)
                pool.wait_ge(L.setup, 3 * c + 2)
                pool.memset(L.Vx[c][:, :, :, HD:HD + 1], 1.0).then_inc(L.setup, 1)
                pool.wait_ge(L.setup, 3 * c + 3)

        def each_batch(eng, body):
            with eng.Fori(0, NBATCH // NHALF) as pair:
                for half in range(NHALF):
                    body(Batch(pair, half))

        def pipelined(eng, L, first, trip):
            L.trip, L.count = None, 0
            first(Batch(0, 0))
            L.chain.before = L.count
            pairs = NBATCH // NHALF

            def run(b, more):
                L.trip, L.count = b, 0
                trip(b, more)
            with eng.Fori(0, pairs - 1) as pair:
                for half in range(NHALF):
                    run(Batch(pair, half), True)
            for half in range(NHALF):
                run(Batch(pairs - 1, half), half < NHALF - 1)

        def beside(steps, extra, first, gap):
            out = list(steps)
            for i in reversed(range(len(extra))):
                out.insert(min(first + i * gap, len(steps)), extra[i])
            return out

        def sp_expand_ahead(sp, L, pick):
            def first(b):
                sp_expand(sp, L, b, True)
                sp_max_rows(sp, L, b, 0)
                pick(b)

            def trip(b, more):
                sp_max_rows(sp, L, b, 1)
                sp_max_rows(sp, L, b, 2)
                if more:
                    sp_expand(sp, L, b.following())
                sp_max_rows(sp, L, b, 3)
                if more:
                    sp_max_rows(sp, L, b.following(), 0)
                    pick(b.following())
            pipelined(sp, L, first, trip)

        def load(sp, L, dst, src):
            sp.dma_start(dst, src).then_inc(L.weights, 16)
            L.loads += 1

        def pe_bias(pe, bias):
            return pe.matmul(bank[1][:], ones[0:1, :],
                             bias[0:1, :].rearrange("p (o n) -> p o n", o=1).to_broadcast([1, NT, D]),
                             start=True, stop=False, skip_group_check=True)

        def pe_logits(pe, L, b, w, e):
            take(pe, L, b, "logit")
            for t in range(NT):
                ins = pe.matmul(bank[0][:, t * e:(t + 1) * e], xnT[b.parity][:, t * P:(t + 1) * P], w,
                                start=True, stop=True)
            ins.then_inc(L.early.full.sem, 1)

        def pe_down(pe, L, b, e, t, hidden_there, count):
            if t == 0:
                take(pe, L, b, f"y{e}")
                pe.wait_ge(hidden_there.sem, hidden_there.at(b, count))
            for f in range(4):
                ins = pe.matmul(bank[1][:, t * P:(t + 1) * P], L.hT[:, e % 2, f, t * P:(t + 1) * P],
                                L.w2[:, e, f, :], start=(f == 0), stop=(f == 3))
            if t == NT - 1:
                fill(L, f"y{e}", ins)

        def hidden_buffer_free(eng, L, b, e):
            if e >= 2:
                there(eng, L, b, f"y{e - 2}")
            else:
                eng.wait_ge(L.late.full.sem, L.late.full.at(b, 0))

        def dve_combine(dve, L, b, e, n_experts):
            there(dve, L, b, f"y{e}")
            last = e == n_experts - 1
            if e:
                ready(dve, L, b, f"y{e - 1}")
            for t in range(NT):
                dst = x[:, b.index * NT + t, :] if last else acc[:, t, :]
                ins = dve.scalar_tensor_tensor(
                    out=dst, in0=bank[1][:, t * P:(t + 1) * P], scalar=copy_of(L.wd, b)[:, t, e:e + 1],
                    in1=acc[:, t, :], op0=ALU.mult, op1=ALU.add)
                if t < NT - 1:
                    mark(L, ins)
            ins.then_inc(L.late.done.sem, 1)

        def dve_residual(dve, L, b):
            there(dve, L, b, "out")
            dve.tensor_tensor(acc[:], bank[1][:].rearrange("p (t n) -> p t n", t=NT),
                              x[:, bass.ds(b.index * NT, NT), :], ALU.add).then_inc(L.late.done.sem, 1)
            ready(dve, L, b, "out")

        def layer0():
            L = attention_plan(0, True, ["xnT", "k", "q", "v", "logit"] + [f"pt{g}" for g in range(NG)],
                               ["wT", "aT", "out"] + [f"y{e}" for e in range(E0)],
                               [bank[3]], [bank[4], bank[5]], 10, float(HD) ** -0.5)
            s = lambda name, k, before=0: Signal(sem(f"{name}0"), k, before)
            L.w1 = carve([P, E0, F0])
            L.w2 = carve([P, E0, 4, D])
            L.b1 = carve([P, E0 * 4])
            L.b2 = carve([E0, D])
            L.keysT, L.rwT, L.rb = carve([P, E0]), carve([P, E0]), carve([P, E0])
            L.logit_w, L.logit_shift, L.ksq = carve([P, E0]), carve([P, E0]), carve([P, E0])
            L.bo = carve([1, D])
            L.lg = carve([P, NT, E0])
            L.top = carve([P, NT, 8])
            L.idx = carve([P, NT, 8], U32)
            L.idxf = carve([P, NT, TOP0])
            L.ev = carve([P, NT, TOP0])
            L.es = carve([P, NT])
            L.eq = carve([P, NT * TOP0, E0])
            L.wd = [carve([P, NT, E0]) for _ in range(NHALF)]
            L.wT = carve([E0, T])
            L.hT = carve([P, 2, 4, T])
            L.chain = s("dve_chain", 80)
            L.gate_in = s("gate_diffs", 1)
            L.gate_exp = s("gate_exps", 1)
            L.wd_ready = s("gates_ready", 1)
            L.h_full = s("hidden_full", E0 * 4)
            L.h_free = s("hidden_free", E0 * 4, 2)
            L.init += [L.h_free]
            L.experts = [sem(f"experts0_{i}") for i in range(4)]
            L.keys_squared, L.keys_summed = sem("keys_squared"), sem("keys_summed")
            HB = [bank[6], bank[7]]

            lead_in = [[("center", 0, 0, True)], [(t, 0, 0, True) for t in ("norm", "k", "q", "v", "logit")]]
            groups = [(what, g, i, True) for s in range(NG + 1) for what, g, i, _ in group_steps(L, s)]
            groups.append(("turn", NG - 1, 0, True))
            units = [lead_in[0], lead_in[1]] + [[] for _ in range(E0 - 1)]
            for n, step in enumerate(groups):
                units[FIRST_UNIT + n * (E0 + 1 - FIRST_UNIT) // len(groups)].append(step)

            parts = []
            for unit in units:
                maxes = [step for step in unit if step[0] in ("max", "max_rows")]
                others = [step for step in unit if step not in maxes]
                parts.append([maxes[f * len(maxes) // 4:(f + 1) * len(maxes) // 4] for f in range(4)] +
                             [others[t * len(others) // NT:(t + 1) * len(others) // NT] for t in range(NT)])
            parts[E0][NT] = [step for part in parts[E0][:NT + 1] for step in part]
            parts[E0][:NT] = [[] for _ in range(NT)]

            def whole(step, eng, b):
                take_steps(step, eng, L, b, [(what, g, i, False) for unit in units for what, g, i, _ in unit])

            def sp_prog(sp):
                L.loads = 0
                for dst, name in ((L.w["k"], "L0_attn_Wk"), (L.w["q"], "L0_attn_Wq"), (L.w["v"], "L0_attn_Wv"),
                                  (L.w["o"], "L0_attn_Wo"), (L.bq, "L0_attn_bq"), (L.bk, "L0_attn_bk"),
                                  (L.bo, "L0_attn_bo"), (L.b1, "L0_ffn_b1"), (L.b2, "L0_ffn_b2"),
                                  (L.keysT, "L0_ffn_keys"), (L.rwT, "L0_ffn_rw")):
                    load(sp, L, dst, a[name])
                load(sp, L, L.bv, a["L0_attn_bv"].partition_broadcast(P))
                load(sp, L, L.rb, a["L0_ffn_rb"].partition_broadcast(P))
                for i in range(4):
                    e = slice(4 * i, 4 * i + 4)
                    sp.dma_start(L.w1[:, e, :], a["L0_ffn_w1"][:, e, :]).then_inc(L.experts[i], 16)
                    sp.dma_start(L.w2[:, e, :, :], a["L0_ffn_w2"][:, e, :, :]).then_inc(L.experts[i], 16)
                
                def body(b):
                    sp_expand(sp, L, b)
                    for g in range(NG):
                        sp_max_rows(sp, L, b, g)
                each_batch(sp, body)

            def pool_prog(pool):
                pool_attention_setup(pool, L)

                def body(b):
                    pool_norm(pool, L, b)
                    pool_split_q(pool, L, b)
                each_batch(pool, body)

            def act_prog(act):
                act.wait_ge(L.weights, 16 * 13)

                def gate(act, L, b, _):
                    act.wait_ge(L.gate_in.sem, L.gate_in.at(b, 1))
                    act.activation(L.ev[:], L.ev[:], ACT.Exp).then_inc(L.gate_exp.sem, 1)
                L.own_act["logit"] = gate

                def trip(b, more):
                    bk = there(act, L, b, "wT")
                    emptied(L, "wT", act.copy(L.wT[:], bk[0:E0, :]))
                    act_turn_attention(act, L, b)
                    for e in range(E0 + 1):
                        if e < E0:
                            hidden_buffer_free(act, L, b, e)
                            for f in range(4):
                                n = 4 * e + f
                                act.wait_ge(L.h_full.sem, L.h_full.at(b, n + 1))
                                act.activation(L.hT[:, e % 2, f, :], HB[n % 2][:], ACT.Gelu,
                                               bias=L.b1[:, n:n + 1]).then_inc(L.h_free.sem, 1)
                        if more:
                            take_steps(act_step, act, L, b, units[e])
                pipelined(act, L, lambda b: whole(act_step, act, b), trip)

            def pe_prog(pe):
                pe.wait_ge(L.weights, 16 * 13)
                pe.wait_ge(L.setup, 3)
                pe.wait_ge(L.keys_squared, 2)
                pe.matmul(bank[1][:, 0:E0], ones[:], L.ksq[:], start=True, stop=True).then_inc(L.keys_summed, 1)
                pe.wait_ge(L.keys_squared, 3)

                L.own_pe["logit"] = lambda pe, L, b, _: pe_logits(pe, L, b, L.logit_w[:], E0)

                def trip(b, more):
                    bk = take(pe, L, b, "wT")
                    pe.wait_ge(L.wd_ready.sem, L.wd_ready.at(b, 1))
                    for t in range(NT):
                        ins = pe.transpose(bk[0:E0, t * P:(t + 1) * P], copy_of(L.wd, b)[:, t, :], ident[:])
                    fill(L, "wT", ins)
                    pe_turn_attention(pe, L, b)
                    take(pe, L, b, "out")
                    pe_bias(pe, L.bo)
                    for t in range(NT):
                        pe.matmul(bank[1][:, t * P:(t + 1) * P], L.wT[:, t * P:(t + 1) * P], L.b2[:],
                                  start=False, stop=False, skip_group_check=True)
                    fill(L, "out", pe_out(pe, L, b))
                    for e in range(E0 + 1):
                        if e < E0:
                            pe.wait_ge(L.experts[e // 4], 32)
                            for f in range(4):
                                n = 4 * e + f
                                pe.wait_ge(L.h_free.sem, L.h_free.at(b, n - 1))
                                pe.matmul(HB[n % 2][:], L.w1[:, e, f * P:(f + 1) * P], xnT[b.parity][:],
                                          start=True, stop=True).then_inc(L.h_full.sem, 1)
                                if more:
                                    take_steps(pe_step, pe, L, b, parts[e][f])
                        for t in range(NT):
                            if more:
                                take_steps(pe_step, pe, L, b, parts[e][NT + t])
                            if e >= 1:
                                pe_down(pe, L, b, e - 1, t, L.h_free, 4 * e)
                pipelined(pe, L, lambda b: whole(pe_step, pe, b), trip)

            def dve_prog(dve):
                dve.wait_ge(L.weights, 16 * 13)
                dve.tensor_tensor(L.ksq[:], L.keysT, L.keysT, ALU.mult).then_inc(L.keys_squared, 1)
                dve.scalar_tensor_tensor(out=L.logit_w[:], in0=L.keysT, scalar=2.0, in1=L.rwT, op0=ALU.mult,
                                         op1=ALU.add).then_inc(L.keys_squared, 1)
                dve.wait_ge(L.keys_summed, 1)
                dve.tensor_tensor(L.logit_shift[:], L.rb, bank[1][:, 0:E0], ALU.subtract).then_inc(L.keys_squared, 1)
                dve.wait_ge(L.keys_squared, 3)

                def gate(dve, L, b, _):
                    wd = copy_of(L.wd, b)
                    there(dve, L, b, "logit")
                    dve.tensor_tensor(L.lg[:], bank[0][:, 0:NT * E0].rearrange("p (t e) -> p t e", t=NT),
                                      L.logit_shift[:].unsqueeze(1).to_broadcast([P, NT, E0]),
                                      ALU.add).then_inc(L.early.done.sem, 1)
                    ready(dve, L, b, "logit")
                    settle(dve)
                    for t in range(NT):
                        mark(L, dve.max(L.top[:, t, :], L.lg[:, t, :]))
                    catch(dve, L)
                    dve.tensor_tensor(L.ev[:], L.top[:, :, 0:TOP0],
                                      L.top[:, :, 0:1].to_broadcast([P, NT, TOP0]),
                                      ALU.subtract).then_inc(L.gate_in.sem, 1)
                    for t in range(NT):
                        mark(L, dve.max_index(L.idx[:, t, :], L.top[:, t, :], L.lg[:, t, :]))
                    catch(dve, L)
                    link(dve, L, dve.tensor_copy(L.idxf[:], L.idx[:, :, 0:TOP0]))
                    wide = [P, NT * TOP0, E0]
                    link(dve, L, dve.tensor_tensor(
                        L.eq[:], iota16[:].unsqueeze(1).to_broadcast(wide),
                        L.idxf[:].rearrange("p t k -> p (t k)").unsqueeze(2).to_broadcast(wide), ALU.is_equal))
                    dve.wait_ge(L.gate_exp.sem, L.gate_exp.at(b, 1))
                    link(dve, L, dve.reduce_sum(L.es[:], L.ev[:], AX.X))
                    link(dve, L, dve.reciprocal(L.es[:], L.es[:]))
                    link(dve, L, dve.tensor_tensor(
                        L.ev[:], L.ev[:], L.es[:].unsqueeze(2).to_broadcast([P, NT, TOP0]), ALU.mult))
                    link(dve, L, dve.tensor_tensor(
                        L.eq[:], L.eq[:],
                        L.ev[:].rearrange("p t k -> p (t k)").unsqueeze(2).to_broadcast(wide), ALU.mult))
                    dve.reduce_sum(wd[:], L.eq[:].rearrange("p (t k) e -> p t e k", t=NT),
                                   AX.X).then_inc(L.wd_ready.sem, 1)
                L.own_dve["logit"] = gate

                def trip(b, more):
                    dve.wait_ge(L.wd_ready.sem, L.wd_ready.at(b, 1))
                    dve_residual(dve, L, b)
                    for e in range(E0 + 1):
                        for part in parts[e] if more else []:
                            take_steps(dve_step, dve, L, b, part)
                        if e >= 1:
                            dve_combine(dve, L, b, e - 1, E0)
                    assert not more or L.count == L.chain.per_batch, L.count
                pipelined(dve, L, lambda b: whole(dve_step, dve, b), trip)

            return L, sp_prog, pool_prog, act_prog, pe_prog, dve_prog

        def layer1():
            class L:
                pass
            used[0] = 0
            FT = H1 * DK1 // P
            PROJ = 2 * FT + NT
            SLOTS = 3
            common_signals(L, 1, ["xnT", "logit"] + [f"v{t}" for t in range(NT)] +
                           [f"h{h}" for h in range(H1)] + [f"yT{c}" for c in range(FT)],
                           ["out"] + [f"y{e}" for e in range(E1)])
            s = lambda name, k, before=0: Signal(sem(f"{name}1"), k, before)
            L.init = []
            L.w = {k: carve([P, H1 * DK1]) for k in "kqvg"}
            L.wo = carve([P, FT, D])
            L.bg = carve([1, H1 * DK1])
            L.rw = carve([P, E1])
            L.rb = carve([P, E1])
            L.w1 = carve([P, E1, 2 * F1])
            L.w2 = carve([P, E1, 4, D])
            L.dist = carve([P, T])
            L.decay = carve([P, 3, H1])
            L.lng = carve([P, H1])
            L.dt = carve([P, H1, T])
            L.kq = {k: carve([P, FT, T]) for k in "kq"}
            L.relu = carve([P, 2, T])
            L.neg = carve([P, 2, T])
            L.V = carve([P, NT, H1, V1W])
            L.eg = carve([P, NT, H1 * DK1])
            L.am = carve([P, 2 * SLOTS, T])
            L.den = carve([P, NT])
            L.div = carve([P, NT, DK1])
            L.y = carve([P, NT, H1 * DK1])
            L.yT = carve([P, FT, T])
            L.lg = carve([P, NT, E1])
            L.top = carve([P, NT, 8])
            L.idx = carve([P, NT, 8], U32)
            L.idxf = carve([P, NT])
            L.ev = carve([P, NT, E1])
            L.es = carve([P, NT])
            L.wd = [carve([P, NT, E1]) for _ in range(NHALF)]
            L.silu = carve([P, 2, T])
            L.hT = carve([P, 2, 4, T])
            L.chain = s("dve_chain", 69)
            L.gate_in = s("gate_diffs", 1)
            L.gate_exp = s("gate_exps", 1)
            L.exp_ready = s("phi_exp", 2 * FT)
            L.phi = s("phi_ready", 2 * FT, 1)
            L.r_full = s("projected_full", PROJ)
            L.r_free = s("projected_free", PROJ, 2)
            L.a_full = s("a_full", 4 * E1)
            L.a_free = s("a_free", 4 * E1, 2)
            L.g_full = s("g_full", 4 * E1)
            L.g_free = s("g_free", 4 * E1, 2)
            L.s_full = s("decayed_full", SLOTS * H1, 1)
            L.s_free = s("decayed_free", SLOTS * H1, 2)
            L.init = [L.a_free, L.g_free, L.s_free, L.r_free]
            L.started += [L.phi, L.s_full]
            L.experts = sem("experts1")
            L.decay_act, L.decay_dve = sem("decay_act"), sem("decay_dve")
            A, G, S = [bank[4], bank[5]], [bank[6], bank[7]], [bank[2], bank[3]]
            NW = 16 * 10

            lead_in = [("center", 0, 0, True), ("norm", 0, 0, True), ("logit", 0, 0, True)] + [("phi", 0, n, True) for n in range(2 * FT)]
            for t in range(NT):
                lead_in += [("gate", 0, t, True), ("value", 0, t, True)]
            heads = []
            for h in range(H1 + 1):
                for i in range(SLOTS if h < H1 else 0):
                    heads.append(("decayed", h, i, True))
                    if i == 0 and h >= 2:
                        heads.append(("divide", 0, h - 2, True))
                if h == H1:
                    heads.append(("divide", 0, H1 - 2, True))
                if h >= 1:
                    heads.append(("weighted", 0, h - 1, True))
            heads.append(("divide", 0, H1 - 1, True))
            heads += [("turn_y", 0, c, True) for c in range(FT)]
            parts = [[[] for _ in range(2 * NT)] for _ in range(E1 + 1)]
            first = [(e, NT + t) for e in range(HEADS_UNIT) for t in range(NT)]
            rest = [(e, t) for e in range(HEADS_UNIT, E1 + 1) for t in range(2 * NT) if e < E1 or t >= NT]
            for steps, places in ((lead_in, first), (heads, rest)):
                for n, step in enumerate(steps):
                    e, t = places[n * len(places) // len(steps)]
                    parts[e][t].append(step)
            at_once = [(what, g, i, False) for what, g, i, _ in lead_in + heads]

            def sp_prog(sp):
                L.loads = 0
                load(sp, L, L.decay[:, 0, :], a["L1_attn_decay_log"].partition_broadcast(P))
                load(sp, L, L.dist, a["const_dist"])
                for k, name in zip("kqvg", ("W_K", "W_Q", "W_V", "W_g_w")):
                    load(sp, L, L.w[k], a["L1_attn_" + name])
                load(sp, L, L.bg, a["L1_attn_W_g_b"])
                load(sp, L, L.wo, a["L1_attn_W_O"])
                load(sp, L, L.rw, a["L1_ffn_router_w"])
                load(sp, L, L.rb, a["L1_ffn_router_b"].partition_broadcast(P))
                sp.dma_start(L.w1, a["L1_ffn_w1"]).then_inc(L.experts, 16)
                sp.dma_start(L.w2, a["L1_ffn_w2"]).then_inc(L.experts, 16)

            def pool_prog(pool):
                pool.memset(L.V[:, :, :, DK1:V1W], 1.0).then_inc(L.setup, 1)

                def body(b):
                    pool_norm(pool, L, b)
                    for n in range(2 * FT):
                        dst = L.kq["kq"[n // FT]][:, n % FT, :]
                        pool.wait_ge(L.exp_ready.sem, L.exp_ready.at(b, n + 1))
                        if n == 0:
                            pool.wait_ge(L.s_full.sem, L.s_full.at(b, 0))
                        pool.tensor_tensor(dst, L.relu[:, n % 2, :], L.neg[:, n % 2, :],
                                           ALU.add).then_inc(L.phi.sem, 1)
                each_batch(pool, body)

            def act_prog(act):
                act.wait_ge(L.weights, NW)
                act.activation(L.decay[:, 1, :], L.decay[:, 0, :], ACT.Abs).then_inc(L.decay_act, 1)
                act.wait_ge(L.decay_act, 1)
                act.activation(L.decay[:, 1, :], L.decay[:, 1, :], ACT.Exp, scale=-1.0).then_inc(L.decay_act, 1)
                act.wait_ge(L.decay_dve, 1)
                act.activation(L.decay[:, 2, :], L.decay[:, 1, :], ACT.Ln).then_inc(L.decay_act, 1)
                act.wait_ge(L.decay_dve, 3)
                for h in range(H1):
                    act.activation(L.dt[:, h, :], L.dist[:], ACT.Exp,
                                   scale=L.lng[:, h:h + 1]).then_inc(L.decay_act, 1)

                def phi(act, L, b, n):
                    bk = S[n % 2]
                    act.wait_ge(L.r_full.sem, L.r_full.at(b, n + 1))
                    act.wait_ge(L.phi.sem, L.phi.at(b, max(n - 1, 0)))
                    act.activation(L.relu[:, n % 2, :], bk[:], ACT.Relu)
                    act.activation(L.neg[:, n % 2, :], bk[:], ACT.Relu, scale=-1.0).then_inc(L.r_free.sem, 1)
                    act.wait_ge(L.r_free.sem, L.r_free.at(b, n + 1))
                    act.activation(L.neg[:, n % 2, :], L.neg[:, n % 2, :], ACT.Exp,
                                   scale=-1.0).then_inc(L.exp_ready.sem, 1)

                def gate(act, L, b, t):
                    n = 2 * FT + t
                    act.wait_ge(L.r_full.sem, L.r_full.at(b, n + 1))
                    act.activation(L.eg[:, t, :], S[n % 2][:], ACT.Exp, scale=-1.0).then_inc(L.r_free.sem, 1)
                    if t == 0:
                        act.wait_ge(L.gate_in.sem, L.gate_in.at(b, 1))
                        act.activation(L.ev[:], L.ev[:], ACT.Exp).then_inc(L.gate_exp.sem, 1)

                def turn_y(act, L, b, c):
                    bk = there(act, L, b, f"yT{c}")
                    emptied(L, f"yT{c}", act.copy(L.yT[:, c, :], bk[:]))
                L.own_act = {"phi": phi, "gate": gate, "turn_y": turn_y}

                def trip(b, more):
                    for e in range(E1 + 1):
                        for f in range(4 if e < E1 else 0):
                            n = 4 * e + f
                            act.wait_ge(L.a_full.sem, L.a_full.at(b, n + 1))
                            act.wait_ge(L.g_free.sem, L.g_free.at(b, n - 1))
                            act.activation(L.silu[:, n % 2, :], A[n % 2][:], ACT.Silu).then_inc(L.a_free.sem, 1)
                            if more:
                                take_steps(act_step, act, L, b, parts[e][f])
                        for t in range(NT if more else 0):
                            take_steps(act_step, act, L, b, parts[e][NT + t])
                pipelined(act, L, lambda b: take_steps(act_step, act, L, b, at_once), trip)

            def pe_prog(pe):
                pe.wait_ge(L.weights, NW)
                pe.wait_ge(L.setup, 1)

                def logit(pe, L, b, _):
                    ready(pe, L, b, "xnT")
                    pe_logits(pe, L, b, L.rw[:], E1)

                def phi(pe, L, b, n):
                    if n == 0:
                        pe.wait_ge(L.s_free.sem, L.s_free.at(b, 0))
                    pe.wait_ge(L.r_free.sem, L.r_free.at(b, n - 1))
                    pe.matmul(S[n % 2][:], L.w["kq"[n // FT]][:, (n % FT) * P:(n % FT + 1) * P],
                              xnT[b.parity][:], start=True, stop=True).then_inc(L.r_full.sem, 1)

                def gate(pe, L, b, t):
                    n = 2 * FT + t
                    pe.wait_ge(L.r_free.sem, L.r_free.at(b, n - 1))
                    pe.matmul(S[n % 2][:], ones[0:1, :], L.bg[:], start=True, stop=False)
                    pe.matmul(S[n % 2][:], xnT[b.parity][:, t * P:(t + 1) * P], L.w["g"][:],
                              start=False, stop=True).then_inc(L.r_full.sem, 1)

                def value(pe, L, b, t):
                    bk = take(pe, L, b, f"v{t}")
                    fill(L, f"v{t}", pe.matmul(bk[:], xnT[b.parity][:, t * P:(t + 1) * P], L.w["v"][:],
                                               start=True, stop=True))

                def scores(b, h, i):
                    if h == 0 and i == 0:
                        pe.wait_ge(L.r_free.sem, L.r_free.at(b, PROJ))
                        pe.wait_ge(L.phi.sem, L.phi.at(b, 2 * FT))
                    lo, m = DK1 * (h % 2), h // 2
                    rows = slice(lo, lo + DK1)
                    n = SLOTS * h + i
                    pe.wait_ge(L.s_free.sem, L.s_free.at(b, n - 1))
                    for kb, c in ([(0, 0)], [(1, 0), (3, T - P)], [(2, 0)])[i]:
                        ins = pe.matmul(S[n % 2][:, c:c + T - kb * P], L.kq["k"][rows, m, kb * P:(kb + 1) * P],
                                        L.kq["q"][rows, m, kb * P:T], start=True, stop=True)
                    ins.then_inc(L.s_full.sem, 1)

                def weighted(pe, L, b, h):
                    where = {0: (0, 0), 1: (1, 0), 2: (2, 0), 3: (1, T - P)}
                    bk = take(pe, L, b, f"h{h}")
                    pe.wait_ge(L.s_free.sem, L.s_free.at(b, SLOTS * (h + 1)))
                    for t in range(NT):
                        for kb in range(t + 1):
                            slot, c = where[kb]
                            c += (t - kb) * P
                            ins = pe.matmul(bk[:, t * V1W:(t + 1) * V1W],
                                            L.am[:, SLOTS * (h % 2) + slot, c:c + P], L.V[:, kb, h, :],
                                            start=(kb == 0), stop=(kb == t))
                    fill(L, f"h{h}", ins)

                def turn_y(pe, L, b, c):
                    bk = take(pe, L, b, f"yT{c}")
                    for t in range(NT):
                        ins = pe.transpose(bk[:, t * P:(t + 1) * P], L.y[:, t, c * P:(c + 1) * P], ident[:])
                    fill(L, f"yT{c}", ins)
                L.own_pe = {"logit": logit, "phi": phi, "gate": gate, "value": value, "weighted": weighted,
                            "turn_y": turn_y}

                def steps(pe, L, b, what, g, i):
                    if what == "decayed":
                        scores(b, g, i)
                    else:
                        pe_step(pe, L, b, what, g, i)

                def trip(b, more):
                    xt = xnT[b.parity]
                    bk = take(pe, L, b, "out")
                    ready(pe, L, b, f"yT{FT - 1}")
                    for t in range(NT):
                        for c in range(FT):
                            ins = pe.matmul(bk[:, t * P:(t + 1) * P], L.yT[:, c, t * P:(t + 1) * P],
                                            L.wo[:, c, :], start=(c == 0), stop=(c == FT - 1))
                    fill(L, "out", ins)
                    pe.wait_ge(L.experts, 32)
                    for e in range(E1 + 1):
                        for f in range(4 if e < E1 else 0):
                            n = 4 * e + f
                            pe.wait_ge(L.a_free.sem, L.a_free.at(b, n - 1))
                            pe.matmul(A[n % 2][:], L.w1[:, e, f * P:(f + 1) * P], xt[:],
                                      start=True, stop=True).then_inc(L.a_full.sem, 1)
                            pe.wait_ge(L.g_free.sem, L.g_free.at(b, n - 1))
                            pe.matmul(G[n % 2][:], L.w1[:, e, F1 + f * P:F1 + (f + 1) * P], xt[:],
                                      start=True, stop=True).then_inc(L.g_full.sem, 1)
                            if more:
                                take_steps(steps, pe, L, b, parts[e][f])
                        for t in range(NT):
                            if more:
                                take_steps(steps, pe, L, b, parts[e][NT + t])
                            if e >= 1:
                                pe_down(pe, L, b, e - 1, t, L.g_free, 4 * e)
                pipelined(pe, L, lambda b: take_steps(steps, pe, L, b, at_once), trip)

            def dve_prog(dve):
                dve.wait_ge(L.weights, NW)
                dve.wait_ge(L.decay_act, 2)
                dve.tensor_scalar(L.decay[:, 1, :], L.decay[:, 1, :], 1.0, None, ALU.add).then_inc(L.decay_dve, 1)
                dve.tensor_scalar(L.lng[:], L.decay[:, 0, :], 0.0, None, ALU.min).then_inc(L.decay_dve, 1)
                dve.wait_ge(L.decay_dve, 2)
                dve.wait_ge(L.decay_act, 3)
                dve.tensor_tensor(L.lng[:], L.lng[:], L.decay[:, 2, :], ALU.subtract).then_inc(L.decay_dve, 1)
                dve.wait_ge(L.decay_act, 3 + H1)
                dve.tensor_tensor(L.dt[:, :, 0:P], L.dt[:, :, 0:P],
                                  mask_f[:].unsqueeze(1).to_broadcast([P, H1, P]), ALU.mult).then_inc(L.decay_dve, 1)
                dve.wait_ge(L.decay_dve, 4)

                def decay(b, h, i):
                    n = SLOTS * h + i
                    if i == 0 and h >= 2:
                        there(dve, L, b, f"h{h - 2}")
                    elif i == 0:
                        dve.wait_ge(L.early.full.sem, L.early.full.at(b, 0))
                    am = L.am[:, SLOTS * (h % 2) + i, :]
                    dve.wait_ge(L.s_full.sem, L.s_full.at(b, n + 1))
                    pieces = [(0, T)] if i == 0 else [(0, T - P), (T - P, P)] if i == 1 else [(0, T - 2 * P)]
                    for k, (c, w) in enumerate(pieces):
                        ins = dve.tensor_tensor(am[:, c:c + w], S[n % 2][:, c:c + w], L.dt[:, h, 0:w], ALU.mult)
                        if k < len(pieces) - 1:
                            mark(L, ins)
                    ins.then_inc(L.s_free.sem, 1)

                def divide(dve, L, b, h):
                    bk = there(dve, L, b, f"h{h}")
                    num = bk[:, 0:NT * V1W].rearrange("p (t c) -> p t c", t=NT)
                    cols = slice(h * DK1, (h + 1) * DK1)
                    link(dve, L, dve.tensor_scalar(L.den[:], num[:, :, DK1], EPS1, None, ALU.add))
                    link(dve, L, dve.scalar_tensor_tensor(
                        out=L.div[:], in0=L.eg[:, :, cols], scalar=1.0,
                        in1=L.den[:].unsqueeze(2).to_broadcast([P, NT, DK1]), op0=ALU.add, op1=ALU.mult))
                    link(dve, L, dve.reciprocal(L.div[:], L.div[:]))
                    emptied(L, f"h{h}", dve.tensor_tensor(L.y[:, :, cols], num[:, :, 0:DK1], L.div[:], ALU.mult))

                def value(dve, L, b, t):
                    bk = there(dve, L, b, f"v{t}")
                    emptied(L, f"v{t}", dve.tensor_copy(L.V[:, t, :, 0:DK1],
                                                        bk[:].rearrange("p (h d) -> p h d", h=H1)))
                    if t == NT - 1:
                        weigh(b)

                def logit(dve, L, b, _):
                    bk = there(dve, L, b, "logit")
                    emptied(L, "logit", dve.tensor_tensor(
                        L.lg[:], bk[:, 0:NT * E1].rearrange("p (t e) -> p t e", t=NT),
                        L.rb[:].unsqueeze(1).to_broadcast([P, NT, E1]), ALU.add))
                    ready(dve, L, b, "logit")
                    settle(dve)
                    for t in range(NT):
                        mark(L, dve.max(L.top[:, t, :], L.lg[:, t, :]))
                    catch(dve, L)
                    dve.tensor_tensor(L.ev[:], L.lg[:], L.top[:, :, 0:1].to_broadcast([P, NT, E1]),
                                      ALU.subtract).then_inc(L.gate_in.sem, 1)
                    for t in range(NT):
                        mark(L, dve.max_index(L.idx[:, t, :], L.top[:, t, :], L.lg[:, t, :]))

                def weigh(b):
                    wd = copy_of(L.wd, b)
                    catch(dve, L)
                    link(dve, L, dve.tensor_copy(L.idxf[:], L.idx[:, :, 0]))
                    wide = [P, NT, E1]
                    link(dve, L, dve.tensor_tensor(
                        wd[:], iota16[:, 0:E1].unsqueeze(1).to_broadcast(wide),
                        L.idxf[:].unsqueeze(2).to_broadcast(wide), ALU.is_equal))
                    dve.wait_ge(L.gate_exp.sem, L.gate_exp.at(b, 1))
                    link(dve, L, dve.reduce_sum(L.es[:], L.ev[:], AX.X))
                    link(dve, L, dve.reciprocal(L.es[:], L.es[:]))
                    link(dve, L, dve.tensor_tensor(
                        wd[:], wd[:], L.es[:].unsqueeze(2).to_broadcast(wide), ALU.mult))
                L.own_dve = {"logit": logit, "value": value, "divide": divide}

                def steps(dve, L, b, what, g, i):
                    if what == "decayed":
                        decay(b, g, i)
                    else:
                        dve_step(dve, L, b, what, g, i)

                def trip(b, more):
                    dve_residual(dve, L, b)
                    for e in range(E1 + 1):
                        for f in range(4 if e < E1 else 0):
                            n = 4 * e + f
                            if f == 0:
                                hidden_buffer_free(dve, L, b, e)
                            dve.wait_ge(L.g_full.sem, L.g_full.at(b, n + 1))
                            dve.wait_ge(L.a_free.sem, L.a_free.at(b, n + 1))
                            dve.tensor_tensor(L.hT[:, e % 2, f, :], L.silu[:, n % 2, :], G[n % 2][:],
                                              ALU.mult).then_inc(L.g_free.sem, 1)
                            if more:
                                take_steps(steps, dve, L, b, parts[e][f])
                        for t in range(NT if more else 0):
                            take_steps(steps, dve, L, b, parts[e][NT + t])
                        if e >= 1:
                            dve_combine(dve, L, b, e - 1, E1)
                    assert not more or L.count == L.chain.per_batch, L.count
                pipelined(dve, L, lambda b: take_steps(steps, dve, L, b, at_once), trip)

            return L, sp_prog, pool_prog, act_prog, pe_prog, dve_prog

        def layer2():
            L = attention_plan(2, True, ["xnT", "k", "q", "v", "h0", "h1"] + [f"r{e}" for e in range(E2)] +
                               ["loss"], ["pt0", "pt1", "pt2", "a", "pt3", "aT", "out"],
                               [bank[3], bank[4]], [bank[5], bank[6], bank[7]], 10, float(HD) ** -0.5,
                               copies=NHALF)
            s = lambda name, k, before=0: Signal(sem(f"{name}2"), k, before)
            L.bp, L.bbase = carve([1, D]), carve([1, D])
            L.base = carve([P, D])
            L.wd1 = carve([P, 2, P])
            L.bd1 = carve([P, 2])
            L.wd2 = carve([P, 2, D])
            L.bd2 = carve([P, E2])
            L.hd = carve([P, 2, T])
            L.diff = carve([P, 2, T])
            L.loss = carve([P, E2])
            L.nloss = carve([P, E2])
            L.top = carve([P, 8])
            L.idx = carve([P, 8], U32)
            L.wdown = carve([P, R2])
            L.bdown = carve([R2, 1])
            L.wup = carve([R2 + 1, D])
            L.a = carve([R2 + 1, T])
            L.chain = s("dve_chain", 19)
            L.squared = s("squared", E2, 1)
            L.chosen = s("adapter_chosen", 1)
            L.picked = s("adapter_in", 64, 1)
            L.started += [L.squared, L.picked]
            NW = 16 * 13

            project = [(t, 0, 0, True) for t in ("center", "norm", "k", "q", "v")]
            trial = [("hidden", 0, i, True) for i in range(2)] + [("rebuild", 0, e, True) for e in range(E2)]
            trial.append(("loss", 0, 0, True))
            first_steps = [(what, 0, i, False) for what, _, i, _ in project + trial] + group_steps(L, 0)
            more_steps = (group_steps(L, 1) + beside(group_steps(L, 2), project, 0, 4) +
                          beside(group_steps(L, 3), trial[:5], 2, 5) +
                          beside(group_steps(L, 4, True), trial[5:], 2, 4))
            last_steps = [step for g in range(1, NG + 1) for step in group_steps(L, g)]

            def sp_prog(sp):
                L.loads = 0
                for dst, name in ((L.w["k"], "L2_attn_Wk"), (L.w["q"], "L2_attn_Wq"), (L.w["v"], "L2_attn_Wv"),
                                  (L.w["o"], "L2_attn_Wp"), (L.bq, "L2_attn_bq"), (L.bk, "L2_attn_bk"),
                                  (L.bp, "L2_attn_bp"), (L.bbase, "L2_ffn_b_base"), (L.base, "L2_ffn_W_base"),
                                  (L.wd1, "L2_ffn_Wd1"), (L.bd1, "L2_ffn_bd1"), (L.wd2, "L2_ffn_Wd2"),
                                  (L.bd2, "L2_ffn_bd2")):
                    load(sp, L, dst, a[name])
                load(sp, L, L.bv, a["L2_attn_bv"].partition_broadcast(P))

                def pick(b):
                    sp.wait_ge(L.late.full.sem, L.late.full.at(b, 0))
                    sp.wait_ge(L.chosen.sem, L.chosen.at(b, 1))
                    settle(sp)
                    e = sp.value_load(L.idx[0:1, 0:1], min_val=0, max_val=E2 - 1)
                    for dst, src in ((L.wdown, a["L2_ffn_Wa_down"][bass.ds(e, 1), :, :]),
                                     (L.wup[0:R2, :], a["L2_ffn_Wa_up"][bass.ds(e, 1), :, :]),
                                     (L.wup[R2:R2 + 1, :], a["L2_ffn_ba_up"][bass.ds(e, 1), :, :]),
                                     (L.bdown, a["L2_ffn_ba_down"][bass.ds(e, 1), :, :])):
                        sp.dma_start(dst, src.rearrange("e p c -> (e p) c")).then_inc(L.picked.sem, 16)
                sp_expand_ahead(sp, L, pick)

            def pool_prog(pool):
                pool_attention_setup(pool, L)
                pool.wait_ge(L.setup, 3 * L.copies)
                pool.memset(L.a[R2:R2 + 1, :], 1.0).then_inc(L.setup, 1)
                pool.wait_ge(L.setup, 3 * L.copies + 1)

                def body(b):
                    pool_norm(pool, L, b)
                    pool_split_q(pool, L, b)
                each_batch(pool, body)

            def act_prog(act):
                act.wait_ge(L.weights, 16 * 14)

                def hidden(act, L, b, i):
                    bk = there(act, L, b, f"h{i}")
                    emptied(L, f"h{i}", act.activation(L.hd[:, i, :], bk[:], ACT.Relu, bias=L.bd1[:, i:i + 1]))

                def rebuild(act, L, b, e):
                    ready(act, L, b, f"r{e}")
                    act.activation(L.diff[:, e % 2, :], L.diff[:, e % 2, :], ACT.Square,
                                   accum_out=L.loss[:, e:e + 1]).then_inc(L.squared.sem, 1)
                L.own_act = {"hidden": hidden, "rebuild": rebuild}

                def trip(b, more):
                    take_steps(act_step, act, L, b, more_steps if more else last_steps)
                    bk = there(act, L, b, "a")
                    emptied(L, "a", act.activation(L.a[0:R2, :], bk[0:R2, :], ACT.Relu, bias=L.bdown[:, 0:1]))
                    act_turn_attention(act, L, b)
                pipelined(act, L, lambda b: take_steps(act_step, act, L, b, first_steps), trip)

            def pe_prog(pe):
                pe.wait_ge(L.weights, 16 * 14)
                pe.wait_ge(L.setup, 3 * L.copies + 1)

                def hidden(pe, L, b, i):
                    bk = take(pe, L, b, f"h{i}")
                    fill(L, f"h{i}", pe.matmul(bk[:], L.wd1[:, i, :], xnT[b.parity][:], start=True, stop=True))

                def rebuild(pe, L, b, e):
                    bk = take(pe, L, b, f"r{e}")
                    rows = slice(HID2 * (e % 4), HID2 * (e % 4 + 1))
                    fill(L, f"r{e}", pe.matmul(bk[:], L.wd2[rows, e // 4, :], L.hd[rows, e // 4, :],
                                               start=True, stop=True))

                def loss(pe, L, b, _):
                    bk = take(pe, L, b, "loss")
                    pe.wait_ge(L.squared.sem, L.squared.at(b, E2))
                    fill(L, "loss", pe.matmul(bk[:, 0:E2], ones[:], L.loss[:], start=True, stop=True))
                L.own_pe = {"hidden": hidden, "rebuild": rebuild, "loss": loss}

                def trip(b, more):
                    xt = xnT[b.parity]
                    take_steps(pe_step, pe, L, b, more_steps if more else last_steps)
                    bk = take(pe, L, b, "a")
                    pe.wait_ge(L.picked.sem, L.picked.at(b, 64))
                    fill(L, "a", pe.matmul(bk[0:R2, :], L.wdown[:], xt[:], start=True, stop=True))
                    pe_attended(pe, L, b, NG - 1)
                    pe_turn_attention(pe, L, b)
                    take(pe, L, b, "out")
                    pe_bias(pe, L.bp)
                    ready(pe, L, b, "a")
                    for t in range(NT):
                        cols = slice(t * P, (t + 1) * P)
                        pe.matmul(bank[1][:, cols], ones[0:1, :], L.bbase[:], start=False, stop=False,
                                  skip_group_check=True)
                        pe.matmul(bank[1][:, cols], xt[:, cols], L.base[:], start=False, stop=False,
                                  skip_group_check=True)
                        pe.matmul(bank[1][:, cols], L.a[:, cols], L.wup[:], start=False, stop=False,
                                  skip_group_check=True)
                    fill(L, "out", pe_out(pe, L, b))
                pipelined(pe, L, lambda b: take_steps(pe_step, pe, L, b, first_steps), trip)

            def dve_prog(dve):
                dve.wait_ge(L.weights, 16 * 14)

                def rebuild(dve, L, b, e):
                    bk = there(dve, L, b, f"r{e}")
                    dve.wait_ge(L.squared.sem, L.squared.at(b, max(e - 1, 0)))
                    emptied(L, f"r{e}", dve.scalar_tensor_tensor(
                        out=L.diff[:, e % 2, :], in0=bk[:], scalar=L.bd2[:, e:e + 1], in1=xnT[b.parity][:],
                        op0=ALU.add, op1=ALU.subtract))

                def loss(dve, L, b, _):
                    bk = there(dve, L, b, "loss")
                    emptied(L, "loss", dve.tensor_scalar(L.nloss[:], bk[:, 0:E2], -1.0, None, ALU.mult))
                    ready(dve, L, b, "loss")
                    settle(dve)
                    link(dve, L, dve.max(L.top[:], L.nloss[:]))
                    dve.wait_ge(L.picked.sem, L.picked.at(b, 0))
                    settle(dve)
                    dve.max_index(L.idx[:], L.top[:], L.nloss[:]).then_inc(L.chosen.sem, 1)
                L.own_dve = {"rebuild": rebuild, "loss": loss}

                def trip(b, more):
                    take_steps(dve_step, dve, L, b, more_steps if more else last_steps)
                    dve_divide(dve, L, b, NG - 1)
                    bk = there(dve, L, b, "out")
                    rows = x[:, bass.ds(b.index * NT, NT), :]
                    emptied(L, "out", dve.tensor_tensor(rows, bk[:].rearrange("p (t n) -> p t n", t=NT), rows,
                                                        ALU.add))
                    assert not more or L.count == L.chain.per_batch, L.count
                pipelined(dve, L, lambda b: take_steps(dve_step, dve, L, b, first_steps), trip)

            return L, sp_prog, pool_prog, act_prog, pe_prog, dve_prog

        def layer3():
            L = attention_plan(3, False, ["xnT", "k", "q", "v", "score"],
                               ["pt0", "pt1", "pt2", "h0", "h1", "pt3", "mix", "aT", "out"],
                               [bank[3], bank[4]], [bank[5], bank[6], bank[7]], 16, None, True, copies=NHALF)
            s = lambda name, k, before=0: Signal(sem(f"{name}3"), k, before)
            L.scale = carve([P, 1])
            L.bias = carve([P, H, HANKEL])
            L.hankel = L.probs[:, 0:H * HANKEL // T, :].rearrange("p a (c i) -> p (a c) i", i=HANKEL)
            L.table = carve([H, 384])
            L.last = carve([H, 1])
            L.bp = carve([1, D])
            L.wr, L.br = carve([P, E3]), carve([P, E3])
            L.sc, L.top, L.idx = carve([P, E3]), carve([P, 8]), carve([P, 8], U32)
            L.w1, L.w2 = carve([P, TOP3, D]), carve([P, TOP3, D])
            L.b1 = [carve([P, 1]) for _ in range(TOP3)]
            L.b2 = [carve([1, D]) for _ in range(TOP3)]
            L.hT = carve([P, TOP3, T])
            L.tabled = nc.dram_tensor("bias_by_distance", [H, 384], F32, kind="Internal").ap()
            L.chain = s("dve_chain", 19)
            L.chosen = s("experts_chosen", 1)
            L.picked = s("experts_in", 16 * 4 * TOP3, 1)
            L.started += [L.picked]
            L.table_dve, L.table_dma = sem("table_dve"), sem("table_dma")
            L.bias_full, L.bias_free = sem("bias_full"), sem("bias_free")
            NW = 16 * 12

            project = [(t, 0, 0, True) for t in ("center", "norm", "k", "q", "v", "choice")]
            first_steps = [(what, 0, i, False) for what, _, i, _ in project] + group_steps(L, 0)
            more_steps = (beside(group_steps(L, 1), project, 8, 5) + group_steps(L, 2) + group_steps(L, 3) +
                          group_steps(L, 4, True))
            last_steps = [step for g in range(1, NG + 1) for step in group_steps(L, g)]

            def sp_prog(sp):
                L.loads = 0
                load(sp, L, L.table[:, 0:TABLE3], a["L3_attn_bias_table"])
                load(sp, L, L.scale, a["L3_attn_temperature"].partition_broadcast(P))
                for dst, name in ((L.w["k"], "L3_attn_Wk"), (L.w["q"], "L3_attn_Wq"), (L.w["v"], "L3_attn_Wv"),
                                  (L.w["o"], "L3_attn_Wp"), (L.bq, "L3_attn_bq"), (L.bk, "L3_attn_bk"),
                                  (L.bp, "L3_attn_bp"), (L.wr, "L3_ffn_Wr")):
                    load(sp, L, dst, a[name])
                load(sp, L, L.bv, a["L3_attn_bv"].partition_broadcast(P))
                load(sp, L, L.br, a["L3_ffn_br"].partition_broadcast(P))
                sp.wait_ge(L.table_dve, 3)
                sp.dma_start(L.tabled, L.table[:]).then_inc(L.table_dma, 16)
                sp.wait_ge(L.table_dma, 16)
                sp.dma_start(L.hankel[:], bass.AP(L.tabled.tensor, 0, [[1, P], [384, H], [1, HANKEL]])
                             ).then_inc(L.table_dma, 16)

                def pick(b):
                    sp.wait_ge(L.late.full.sem, L.late.full.at(b, 0))
                    sp.wait_ge(L.chosen.sem, L.chosen.at(b, 1))
                    settle(sp)
                    for k in range(TOP3):
                        e = sp.value_load(L.idx[0:1, k:k + 1], min_val=0, max_val=E3 - 1)
                        for dst, src in ((L.w1[:, k, :], a["L3_ffn_W1"][bass.ds(e, 1), :, :]),
                                         (L.w2[:, k, :], a["L3_ffn_W2"][bass.ds(e, 1), :, :]),
                                         (L.b1[k], a["L3_ffn_b1"][bass.ds(e, 1), :, :]),
                                         (L.b2[k], a["L3_ffn_b2"][bass.ds(e, 1), :, :])):
                            sp.dma_start(dst, src.rearrange("e p c -> (e p) c")).then_inc(L.picked.sem, 16)
                sp_expand_ahead(sp, L, pick)

            def pool_prog(pool):
                pool_attention_setup(pool, L)

                def body(b):
                    pool_norm(pool, L, b)
                    pool_split_q(pool, L, b)
                each_batch(pool, body)

            def act_prog(act):
                act.wait_ge(L.weights, NW)

                def trip(b, more):
                    take_steps(act_step, act, L, b, more_steps if more else last_steps)
                    for k in range(TOP3):
                        bk = there(act, L, b, f"h{k}")
                        emptied(L, f"h{k}", act.activation(L.hT[:, k, :], bk[:], ACT.Gelu,
                                                           bias=L.b1[k][:, 0:1]))
                    act_turn_attention(act, L, b)
                pipelined(act, L, lambda b: take_steps(act_step, act, L, b, first_steps), trip)

            def pe_prog(pe):
                pe.wait_ge(L.weights, NW)
                pe.wait_ge(L.setup, 3 * L.copies)
                pe.wait_ge(L.table_dma, 32)
                for n in range(H // 2):
                    if n >= 1:
                        pe.wait_ge(L.bias_free, n)
                    pe.matmul(bank[1][:], flip[:], L.hankel[:, 2 * n:2 * n + 2, :].rearrange("p h i -> p (h i)"),
                              start=True, stop=True).then_inc(L.bias_full, 1)
                pe.wait_ge(L.bias_free, H // 2)

                def choice(pe, L, b, _):
                    bk = take(pe, L, b, "score")
                    fill(L, "score", pe.matmul(bk[:, 0:E3], xnT[b.parity][:, 0:1].to_broadcast([P, P]), L.wr[:],
                                               start=True, stop=True))
                L.own_pe = {"choice": choice}

                def trip(b, more):
                    xt = xnT[b.parity]
                    take_steps(pe_step, pe, L, b, more_steps if more else last_steps)
                    pe.wait_ge(L.picked.sem, L.picked.at(b, 16 * 4 * TOP3))
                    for k in range(TOP3):
                        bk = take(pe, L, b, f"h{k}")
                        fill(L, f"h{k}", pe.matmul(bk[:], L.w1[:, k, :], xt[:], start=True, stop=True))
                    pe_attended(pe, L, b, NG - 1)
                    take(pe, L, b, "mix")
                    ready(pe, L, b, f"h{TOP3 - 1}")
                    pe_bias(pe, L.b2[0])
                    for t in range(NT):
                        cols = slice(t * P, (t + 1) * P)
                        pe.matmul(bank[1][:, cols], ones[0:1, :], L.b2[1][:], start=False, stop=False,
                                  skip_group_check=True)
                        for k in range(TOP3):
                            ins = pe.matmul(bank[1][:, cols], L.hT[:, k, cols], L.w2[:, k, :], start=False,
                                            stop=(k == TOP3 - 1), skip_group_check=True)
                    fill(L, "mix", ins)
                    pe_turn_attention(pe, L, b)
                    take(pe, L, b, "out")
                    pe_bias(pe, L.bp)
                    fill(L, "out", pe_out(pe, L, b))
                pipelined(pe, L, lambda b: take_steps(pe_step, pe, L, b, first_steps), trip)

            def dve_prog(dve):
                dve.wait_ge(L.weights, NW)
                dve.tensor_copy(L.last[:], L.table[:, TABLE3 - 1:TABLE3]).then_inc(L.table_dve, 1)
                dve.memset(L.table[:, TABLE3:384], 0.0).then_inc(L.table_dve, 1)
                dve.wait_ge(L.table_dve, 2)
                dve.tensor_scalar(L.table[:, 0:TABLE3], L.table[:, 0:TABLE3], L.last[:, 0:1], None,
                                  ALU.subtract).then_inc(L.table_dve, 1)
                dve.tensor_scalar(L.scale[:], L.scale[:], 0.1, 10.0, ALU.max, ALU.min).then_inc(L.table_dve, 1)
                dve.wait_ge(L.table_dve, 4)
                dve.tensor_scalar(L.scale[:], L.scale[:], float(np.sqrt(np.float32(D))), None,
                                  ALU.mult).then_inc(L.table_dve, 1)
                dve.wait_ge(L.table_dve, 5)
                dve.reciprocal(L.scale[:], L.scale[:]).then_inc(L.table_dve, 1)
                dve.wait_ge(L.table_dve, 6)
                for n in range(H // 2):
                    dve.wait_ge(L.bias_full, n + 1)
                    dve.tensor_copy(L.bias[:, 2 * n:2 * n + 2, :].rearrange("p h i -> p (h i)"),
                                    bank[1][:]).then_inc(L.bias_free, 1)

                def choice(dve, L, b, _):
                    bk = there(dve, L, b, "score")
                    emptied(L, "score", dve.tensor_tensor(L.sc[:], bk[:, 0:E3], L.br[:], ALU.add))
                    ready(dve, L, b, "score")
                    settle(dve)
                    link(dve, L, dve.max(L.top[:], L.sc[:]))
                    dve.wait_ge(L.picked.sem, L.picked.at(b, 0))
                    settle(dve)
                    dve.max_index(L.idx[:], L.top[:], L.sc[:]).then_inc(L.chosen.sem, 1)
                L.own_dve = {"choice": choice}

                def trip(b, more):
                    take_steps(dve_step, dve, L, b, more_steps if more else last_steps)
                    dve_divide(dve, L, b, NG - 1)
                    rows = x[:, bass.ds(b.index * NT, NT), :]
                    bk = there(dve, L, b, "mix")
                    emptied(L, "mix", dve.scalar_tensor_tensor(
                        out=acc[:], in0=bk[:].rearrange("p (t n) -> p t n", t=NT), scalar=1.0 / TOP3,
                        in1=rows, op0=ALU.mult, op1=ALU.add))
                    ready(dve, L, b, "mix")
                    there(dve, L, b, "out")
                    emptied(L, "out", dve.tensor_tensor(rows, bk[:].rearrange("p (t n) -> p t n", t=NT), acc[:],
                                                        ALU.add))
                    assert not more or L.count == L.chain.per_batch, L.count
                pipelined(dve, L, lambda b: take_steps(dve_step, dve, L, b, first_steps), trip)

            return L, sp_prog, pool_prog, act_prog, pe_prog, dve_prog

        made = {0: layer0, 1: layer1, 2: layer2, 3: layer3}
        programs = [made[i]() for i in layers]

        def finish_layer(eng, n):
            eng.drain().then_inc(layer_done, 1)
            eng.wait_ge(layer_done, 5 * (n + 1))

        block = stack.enter_context(nc.Block())

        @block.sync
        def _(sp):
            for dst, name in ((ident, "const_ident"), (flip, "const_flip"), (mask_f, "const_keep"),
                              (iota16, "const_iota"), (mask_qf, "const_mask")):
                sp.dma_start(dst[:], a[name]).then_inc(consts_loaded, 16)
            sp.dma_start(x[:], a["L0_attn_x"].rearrange("b (t p) d -> p (b t) d", p=P)).then_inc(x_loaded, 16)
            for n, (_, sp_prog, *_rest) in enumerate(programs):
                sp_prog(sp)
                finish_layer(sp, n)
            sp.dma_start(out.rearrange("b (t p) d -> p (b t) d", p=P), x[:]).then_inc(out_stored, 16)
            sp.wait_ge(out_stored, 16)

        @block.gpsimd
        def _(pool):
            for L, *_rest in programs:
                for signal in L.init + L.started:
                    pool.sem_inc(signal.sem, signal.before)
            pool.memset(ones[:], 1.0).then_inc(ones_set, 1)
            pool.memset(mhalf[:], -0.5).then_inc(ones_set, 1)
            pool.wait_ge(ones_set, 2)
            for n, (_, _, pool_prog, *_rest) in enumerate(programs):
                pool_prog(pool)
                finish_layer(pool, n)

        @block.scalar
        def _(act):
            for n, (_, _, _, act_prog, *_rest) in enumerate(programs):
                act_prog(act)
                finish_layer(act, n)

        @block.tensor
        def _(pe):
            pe.wait_ge(consts_loaded, 16 * 5)
            pe.wait_ge(consts_cast, 3)
            pe.wait_ge(ones_set, 1)
            for n, (_, _, _, _, pe_prog, _dve) in enumerate(programs):
                pe_prog(pe)
                finish_layer(pe, n)

        @block.vector
        def _(dve):
            dve.wait_ge(consts_loaded, 16 * 5)
            dve.tensor_copy(identb[:], ident[:]).then_inc(consts_cast, 1)
            dve.tensor_copy(mask_q[:], mask_qf[:, 0, :]).then_inc(consts_cast, 1)
            dve.tensor_copy(mask_k[:], mask_qf[:, 1, :]).then_inc(consts_cast, 1)
            dve.wait_ge(x_loaded, 16)
            for n, (*_rest, dve_prog) in enumerate(programs):
                dve_prog(dve)
                finish_layer(dve, n)


def _layouts(v):
    c = np.ascontiguousarray
    out = {"L0_attn_x": v["L0_attn_x"]}
    for k in ("q", "k", "v", "o"):
        out[f"L0_attn_W{k}"] = c(v[f"L0_attn_W{k}"].T)
    for k in ("q", "k"):
        out[f"L0_attn_b{k}"] = v[f"L0_attn_b{k}"].reshape(D, 1)
        out[f"L3_attn_b{k}"] = v[f"L3_attn_b{k}"].reshape(D, 1)
    out["L0_attn_bo"] = v["L0_attn_bo"].reshape(1, D)
    for name in ("L0_attn_bv", "L0_ffn_rb", "L1_attn_decay_log", "L1_ffn_router_b", "L3_attn_bv", "L3_ffn_br",
                 "L3_attn_temperature"):
        out[name] = v[name]
    out["L0_ffn_keys"] = c(v["L0_ffn_keys"].T)
    out["L0_ffn_rw"] = c(v["L0_ffn_rw"].T)
    out["L0_ffn_w1"] = c(v["L0_ffn_w1"].transpose(2, 0, 1))
    out["L0_ffn_w2"] = c(v["L0_ffn_w2"].transpose(2, 0, 1).reshape(4, P, E0, D).transpose(1, 2, 0, 3))
    out["L0_ffn_b1"] = c(v["L0_ffn_b1"].reshape(E0, 4, P).transpose(2, 0, 1).reshape(P, E0 * 4))
    out["L0_ffn_b2"] = v["L0_ffn_b2"]
    for name in ("W_Q", "W_K", "W_V", "W_g_w"):
        out[f"L1_attn_{name}"] = c(v[f"L1_attn_{name}"].T)
    out["L1_attn_W_g_b"] = v["L1_attn_W_g_b"].reshape(1, H1 * DK1)
    out["L1_attn_W_O"] = c(v["L1_attn_W_O"].T.reshape(4, P, D).transpose(1, 0, 2))
    out["L1_ffn_router_w"] = v["L1_ffn_router_w"]
    out["L1_ffn_w1"] = c(v["L1_ffn_w1"].transpose(1, 0, 2))
    out["L1_ffn_w2"] = c(v["L1_ffn_w2"].reshape(E1, 4, P, D).transpose(2, 0, 1, 3))
    w = v["L2_attn_W1"].reshape(D, H, 3, HD)
    bb = v["L2_attn_b1"].reshape(H, 3, HD)
    for i, k in enumerate("qkv"):
        out[f"L2_attn_W{k}"] = c(w[:, :, i, :].reshape(D, D))
        out[f"L2_attn_b{k}"] = c(bb[:, i, :].reshape(D, 1))
    out["L2_attn_bv"] = out["L2_attn_bv"].reshape(D)
    out["L2_attn_Wp"] = v["L2_attn_Wp"]
    out["L2_attn_bp"] = v["L2_attn_bp"].reshape(1, D)
    out["L2_ffn_W_base"] = v["L2_ffn_W_base"]
    out["L2_ffn_b_base"] = v["L2_ffn_b_base"].reshape(1, D)
    out["L2_ffn_Wd1"] = c(v["L2_ffn_Wd1"].transpose(1, 0, 2).reshape(D, 2, P))
    out["L2_ffn_bd1"] = c(v["L2_ffn_bd1"].reshape(2, P).T)
    out["L2_ffn_Wd2"] = c(v["L2_ffn_Wd2"].reshape(2, P, D).transpose(1, 0, 2))
    out["L2_ffn_bd2"] = c(v["L2_ffn_bd2"].T)
    out["L2_ffn_Wa_down"], out["L2_ffn_Wa_up"] = v["L2_ffn_Wa_down"], v["L2_ffn_Wa_up"]
    out["L2_ffn_ba_down"] = v["L2_ffn_ba_down"].reshape(E2, R2, 1)
    out["L2_ffn_ba_up"] = v["L2_ffn_ba_up"].reshape(E2, 1, D)
    for name in ("L3_attn_Wq", "L3_attn_Wk", "L3_attn_Wv", "L3_attn_Wp", "L3_ffn_Wr", "L3_ffn_W1", "L3_ffn_W2"):
        out[name] = v[name]
    out["L3_attn_bp"] = v["L3_attn_bp"].reshape(1, D)
    out["L3_attn_bias_table"] = c(v["L3_attn_bias_table"].T)
    out["L3_ffn_b1"] = v["L3_ffn_b1"].reshape(E3, D, 1)
    out["L3_ffn_b2"] = v["L3_ffn_b2"].reshape(E3, 1, D)
    p, f = np.arange(P)[:, None], np.arange(P)[None, :]
    out["const_ident"] = np.eye(P, dtype=np.float32)
    out["const_flip"] = c(np.eye(P, dtype=np.float32)[::-1])
    out["const_keep"] = (f >= p).astype(np.float32)
    out["const_iota"] = np.tile(np.arange(16, dtype=np.float32), (P, 1))
    out["const_mask"] = c(np.stack([(f > p), (p > f)], 1).astype(np.float32) * np.float32(-3e38))
    out["const_dist"] = np.maximum(np.arange(T)[None, :] - p, 0).astype(np.float32)
    return {k: c(z) for k, z in out.items()}


def kernel(**inputs):
    import concourse.bacc as bacc
    from concourse.bass_utils import run_bass_kernel_spmd

    arrays = _layouts({k: np.asarray(z) for k, z in inputs.items()})
    nc = bacc.Bacc("TRN2", target_bir_lowering=False, num_devices=1)
    a = {k: nc.dram_tensor(f"in_{k}", list(z.shape), F32, kind="ExternalInput").ap() for k, z in arrays.items()}
    out = nc.dram_tensor("out", [NBATCH, T, D], F32, kind="ExternalOutput").ap()
    build(nc, a, out)
    r = run_bass_kernel_spmd(nc, [{f"in_{k}": z for k, z in arrays.items()}], core_ids=[0])
    return r.results[0]["out"]
```
